# Optimizing a Trainium2 kernel written in Bass

```python
import numpy as np
import jax
import jax.numpy as jnp

def _softmax(x, axis=-1):
    return jax.nn.softmax(x, axis=axis)

def _gelu(x):
    return jax.nn.gelu(x, approximate=True)

def _silu(x):
    return jax.nn.silu(x)

def _sigmoid(x):
    return jax.nn.sigmoid(x)

def _layernorm(x, axis=-1, eps=1e-05):
    m = jnp.mean(x, axis=axis, keepdims=True)
    v = jnp.var(x, axis=axis, keepdims=True)
    return (x - m) / jnp.sqrt(v + eps)

def _scatter_add(tgt, idx, src, axis=0):
    return tgt.at[idx].add(src)

def _segment_sum(src, seg, n):
    return jax.ops.segment_sum(src, seg, n)
kernel_name = 'mk_adaln_d2_jaxref_r4_88abc0'

def setup_inputs(seed: int=0):
    np.random.seed(seed)
    _w = jnp.asarray

    def _L0_attn_setup():
        import jax, jax.numpy as jnp
        import numpy as np
        from jax import lax
        DIM = 256
        H = 16
        HD = DIM // H
        D_INNER = 4
        CHUNK = 16
        BASE_LR = 0.001
        KSZ = 4

        def short_conv(x, w):
            xT = jnp.transpose(x, (0, 2, 1))
            y = lax.conv_general_dilated(xT, w[:, None, :], window_strides=(1,), padding=[(KSZ - 1, 0)], feature_group_count=x.shape[-1], dimension_numbers=('NCH', 'OIH', 'NCH'))
            return jnp.transpose(y + xT, (0, 2, 1))

        def l2norm(x):
            return x / jnp.linalg.norm(x, axis=-1, keepdims=True)

        def attn(q, k, v):
            s = jnp.einsum('bqhd,bkhd->bhqk', q, k) / jnp.sqrt(jnp.asarray(q.shape[-1], q.dtype))
            p = jax.nn.softmax(s, axis=-1)
            return jnp.einsum('bhqk,bkhd->bqhd', p, v)

        def _forward(hidden_states, Wq, Wk, Wv, Wlr, Wg, Wo, cq, ck, cv, W_in_init, W_out_init, ln_g, ln_b):
            b, l, _ = hidden_states.shape
            q = l2norm(jax.nn.silu(short_conv(hidden_states @ Wq.T, cq)).reshape(b, l, H, HD))
            k = l2norm(jax.nn.silu(short_conv(hidden_states @ Wk.T, ck)).reshape(b, l, H, HD))
            v = jax.nn.silu(short_conv(hidden_states @ Wv.T, cv)).reshape(b, l, H, HD)
            lr = jax.nn.softplus(hidden_states @ Wlr.T + BASE_LR).reshape(b, l, H, 2)
            nc = l // CHUNK
            to_chunks = lambda x: x.reshape(b, nc, CHUNK, H, -1).transpose(1, 0, 2, 3, 4)
            qc, kc, vc, lrc = map(to_chunks, (q, k, v, lr))
            W_in0 = jnp.broadcast_to(W_in_init, (b, D_INNER, H, HD))
            W_out0 = jnp.broadcast_to(W_out_init, (b, D_INNER, H, HD))
            mask = jnp.tril(jnp.ones((CHUNK, CHUNK), jnp.float32))

            def step(carry, xs):
                W_in, W_out = carry
                q_t, k_t, v_t, lr_t = xs
                k_h = jax.nn.softmax(jnp.einsum('blhd,bDhd->blhD', k_t, W_in), axis=-1) * lr_t[..., 1:]
                q_h = jax.nn.softmax(jnp.einsum('blhd,bDhd->blhD', q_t, W_in), axis=-1)
                qk = jnp.einsum('bqhD,bkhD->bhqk', q_h, k_h) * mask
                o_t = jnp.einsum('bqhD,bDhd->bqhd', q_h, W_out) + jnp.einsum('bhqk,bkhd->bqhd', qk, v_t)
                W_out = W_out + jnp.einsum('bnhD,bnhd->bDhd', k_h, v_t)
                lr_in = lr_t[:, :1, :, 0:1]
                lr_out = lr_t[:, :1, :, 1:2]
                for _ in range(2):
                    g_out = -attn(W_in, k_t, v_t)
                    g_in = -attn(W_out, v_t, k_t)
                    W_in = W_in - lr_in * g_in
                    W_out = W_out - lr_out * g_out
                return ((W_in, W_out), o_t)
            _, o = lax.scan(step, (W_in0, W_out0), (qc, kc, vc, lrc))
            o = o.transpose(1, 0, 2, 3, 4).reshape(b, l, H, HD)
            mu = o.mean(-1, keepdims=True)
            var = ((o - mu) ** 2).mean(-1, keepdims=True)
            o = (o - mu) / jnp.sqrt(var + 1e-05) * ln_g + ln_b
            o = o.reshape(b, l, DIM)
            gate = hidden_states @ Wg.T
            return o * gate @ Wo.T
        key = jax.random.key(seed)
        ks = jax.random.split(key, 12)
        b, l = (4, 1024)
        s = 1.0 / np.sqrt(DIM)
        return {'hidden_states': jax.random.normal(ks[0], (b, l, DIM), jnp.float32), 'Wq': jax.random.normal(ks[1], (DIM, DIM), jnp.float32) * s, 'Wk': jax.random.normal(ks[2], (DIM, DIM), jnp.float32) * s, 'Wv': jax.random.normal(ks[3], (DIM, DIM), jnp.float32) * s, 'Wlr': jax.random.normal(ks[4], (H * 2, DIM), jnp.float32) * s, 'Wg': jax.random.normal(ks[5], (DIM, DIM), jnp.float32) * s, 'Wo': jax.random.normal(ks[6], (DIM, DIM), jnp.float32) * s, 'cq': jax.random.normal(ks[7], (DIM, KSZ), jnp.float32) * 0.1, 'ck': jax.random.normal(ks[8], (DIM, KSZ), jnp.float32) * 0.1, 'cv': jax.random.normal(ks[9], (DIM, KSZ), jnp.float32) * 0.1, 'W_in_init': jax.random.normal(ks[10], (1, D_INNER, H, HD), jnp.float32) / np.sqrt(HD), 'W_out_init': jax.random.normal(ks[11], (1, D_INNER, H, HD), jnp.float32) / np.sqrt(D_INNER), 'ln_g': jnp.ones((HD,), jnp.float32), 'ln_b': jnp.zeros((HD,), jnp.float32)}
    _L0_attn_in = _L0_attn_setup()

    def _L0_ffn_setup():
        import jax, jax.numpy as jnp
        import numpy as np
        D_MODEL, D_FF, RANK = (256, 1024, 64)
        B, S = (4, 1024)
        key = jax.random.key(seed)
        ks = jax.random.split(key, 7)
        return {'x': jax.random.normal(ks[0], (B, S, D_MODEL), dtype=jnp.float32), 'U1': jax.random.normal(ks[1], (D_MODEL, RANK), dtype=jnp.float32) * 0.02, 'V1': jax.random.normal(ks[2], (RANK, D_FF), dtype=jnp.float32) * 0.02, 'b1': jnp.zeros((D_FF,), dtype=jnp.float32), 'U2': jax.random.normal(ks[3], (D_FF, RANK), dtype=jnp.float32) * 0.02, 'V2': jax.random.normal(ks[4], (RANK, D_MODEL), dtype=jnp.float32) * 0.02, 'b2': jnp.zeros((D_MODEL,), dtype=jnp.float32)}
    _L0_ffn_in = _L0_ffn_setup()
    _L0_c = _w((lambda *s: np.random.randn(*s).astype(np.float32) * 0.05)(16, 256))
    _L0_wmod = _w((lambda *s: np.random.randn(*s).astype(np.float32) * 0.05)(256, 6 * 256) * 256 ** (-0.5))

    def _L1_attn_setup():
        import jax, jax.numpy as jnp
        import numpy as np
        N_HEAD = 16
        N_EMBD = 256
        LOCAL_WINDOW = 64
        GLOBAL_IDX = np.array([0, 1, 2, 3], dtype=np.int64)

        def build_mask(T):
            i = np.arange(T)[:, None]
            j = np.arange(T)[None, :]
            causal = j <= i
            local = causal & (j >= i - LOCAL_WINDOW + 1)
            g_row = np.isin(np.arange(T), GLOBAL_IDX)[:, None]
            g_col = np.isin(np.arange(T), GLOBAL_IDX)[None, :]
            mask = local | g_row & causal | g_col & causal
            return jnp.asarray(mask)
        key = jax.random.key(seed)
        k1, k2, k3 = jax.random.split(key, 3)
        B, T, C = (2, 512, N_EMBD)
        x = jax.random.normal(k1, (B, T, C), dtype=jnp.float32)
        w_attn = jax.random.normal(k2, (3 * C, C), dtype=jnp.float32) * (1.0 / np.sqrt(C))
        w_proj = jax.random.normal(k3, (C, C), dtype=jnp.float32) * (1.0 / np.sqrt(C))
        return {'x': x, 'w_attn': w_attn, 'w_proj': w_proj}
    _L1_attn_in = _L1_attn_setup()

    def _L1_ffn_setup():
        import jax, jax.numpy as jnp
        import numpy as np
        DIM = 256

        def _reference_tuple_inner(x, W_r, W_k, W_v, mu_r, mu_k):
            B, T, C = x.shape
            x_prev = jnp.concatenate([jnp.zeros((B, 1, C), x.dtype), x[:, :-1, :]], axis=1)
            xr = mu_r * x + (1.0 - mu_r) * x_prev
            xk = mu_k * x + (1.0 - mu_k) * x_prev
            r = jax.nn.sigmoid(jnp.einsum('btc,dc->btd', xr, W_r))
            k = jnp.einsum('btc,dc->btd', xk, W_k)
            k_act = jnp.square(jax.nn.relu(k))
            out = r * jnp.einsum('btc,dc->btd', k_act, W_v)
            new_state = x[:, -1, :]
            return (out, new_state)
        key = jax.random.key(seed)
        ks = jax.random.split(key, 6)
        B, T, C = (8, 512, DIM)
        x = jax.random.normal(ks[0], (B, T, C), dtype=jnp.float32)
        s = 1.0 / np.sqrt(C)
        W_r = jax.random.uniform(ks[1], (C, C), jnp.float32, -s, s)
        W_k = jax.random.uniform(ks[2], (C, C), jnp.float32, -s, s)
        W_v = jax.random.uniform(ks[3], (C, C), jnp.float32, -s, s)
        mu_r = jax.random.uniform(ks[4], (C,), jnp.float32)
        mu_k = jax.random.uniform(ks[5], (C,), jnp.float32)
        return {'x': x, 'W_r': W_r, 'W_k': W_k, 'W_v': W_v, 'mu_r': mu_r, 'mu_k': mu_k}
    _L1_ffn_in = _L1_ffn_setup()
    _L1_c = _w((lambda *s: np.random.randn(*s).astype(np.float32) * 0.05)(16, 256))
    _L1_wmod = _w((lambda *s: np.random.randn(*s).astype(np.float32) * 0.05)(256, 6 * 256) * 256 ** (-0.5))
    _d = {'L0_attn_hidden_states': _L0_attn_in['hidden_states'], 'L0_attn_Wq': _L0_attn_in['Wq'], 'L0_attn_Wk': _L0_attn_in['Wk'], 'L0_attn_Wv': _L0_attn_in['Wv'], 'L0_attn_Wlr': _L0_attn_in['Wlr'], 'L0_attn_Wg': _L0_attn_in['Wg'], 'L0_attn_Wo': _L0_attn_in['Wo'], 'L0_attn_cq': _L0_attn_in['cq'], 'L0_attn_ck': _L0_attn_in['ck'], 'L0_attn_cv': _L0_attn_in['cv'], 'L0_attn_W_in_init': _L0_attn_in['W_in_init'], 'L0_attn_W_out_init': _L0_attn_in['W_out_init'], 'L0_attn_ln_g': _L0_attn_in['ln_g'], 'L0_attn_ln_b': _L0_attn_in['ln_b'], 'L0_ffn_U1': _L0_ffn_in['U1'], 'L0_ffn_V1': _L0_ffn_in['V1'], 'L0_ffn_b1': _L0_ffn_in['b1'], 'L0_ffn_U2': _L0_ffn_in['U2'], 'L0_ffn_V2': _L0_ffn_in['V2'], 'L0_ffn_b2': _L0_ffn_in['b2'], 'L0_c': _L0_c, 'L0_wmod': _L0_wmod, 'L1_attn_w_attn': _L1_attn_in['w_attn'], 'L1_attn_w_proj': _L1_attn_in['w_proj'], 'L1_ffn_W_r': _L1_ffn_in['W_r'], 'L1_ffn_W_k': _L1_ffn_in['W_k'], 'L1_ffn_W_v': _L1_ffn_in['W_v'], 'L1_ffn_mu_r': _L1_ffn_in['mu_r'], 'L1_ffn_mu_k': _L1_ffn_in['mu_k'], 'L1_c': _L1_c, 'L1_wmod': _L1_wmod}
    _x0 = _d['L0_attn_hidden_states']
    _d['L0_attn_hidden_states'] = jax.random.normal(jax.random.fold_in(jax.random.key(seed), 1), (16, 512, 256), dtype=_x0.dtype)
    del _x0
    return _d

def reference(L0_attn_hidden_states, L0_attn_Wq, L0_attn_Wk, L0_attn_Wv, L0_attn_Wlr, L0_attn_Wg, L0_attn_Wo, L0_attn_cq, L0_attn_ck, L0_attn_cv, L0_attn_W_in_init, L0_attn_W_out_init, L0_attn_ln_g, L0_attn_ln_b, L0_ffn_U1, L0_ffn_V1, L0_ffn_b1, L0_ffn_U2, L0_ffn_V2, L0_ffn_b2, L0_c, L0_wmod, L1_attn_w_attn, L1_attn_w_proj, L1_ffn_W_r, L1_ffn_W_k, L1_ffn_W_v, L1_ffn_mu_r, L1_ffn_mu_k, L1_c, L1_wmod):

    def _L0_attn_ref(hidden_states, Wq, Wk, Wv, Wlr, Wg, Wo, cq, ck, cv, W_in_init, W_out_init, ln_g, ln_b):
        import jax, jax.numpy as jnp
        import numpy as np
        from jax import lax
        DIM = 256
        H = 16
        HD = DIM // H
        D_INNER = 4
        CHUNK = 16
        BASE_LR = 0.001
        KSZ = 4

        def short_conv(x, w):
            xT = jnp.transpose(x, (0, 2, 1))
            y = lax.conv_general_dilated(xT, w[:, None, :], window_strides=(1,), padding=[(KSZ - 1, 0)], feature_group_count=x.shape[-1], dimension_numbers=('NCH', 'OIH', 'NCH'))
            return jnp.transpose(y + xT, (0, 2, 1))

        def l2norm(x):
            return x / jnp.linalg.norm(x, axis=-1, keepdims=True)

        def attn(q, k, v):
            s = jnp.einsum('bqhd,bkhd->bhqk', q, k) / jnp.sqrt(jnp.asarray(q.shape[-1], q.dtype))
            p = jax.nn.softmax(s, axis=-1)
            return jnp.einsum('bhqk,bkhd->bqhd', p, v)

        def _forward(hidden_states, Wq, Wk, Wv, Wlr, Wg, Wo, cq, ck, cv, W_in_init, W_out_init, ln_g, ln_b):
            b, l, _ = hidden_states.shape
            q = l2norm(jax.nn.silu(short_conv(hidden_states @ Wq.T, cq)).reshape(b, l, H, HD))
            k = l2norm(jax.nn.silu(short_conv(hidden_states @ Wk.T, ck)).reshape(b, l, H, HD))
            v = jax.nn.silu(short_conv(hidden_states @ Wv.T, cv)).reshape(b, l, H, HD)
            lr = jax.nn.softplus(hidden_states @ Wlr.T + BASE_LR).reshape(b, l, H, 2)
            nc = l // CHUNK
            to_chunks = lambda x: x.reshape(b, nc, CHUNK, H, -1).transpose(1, 0, 2, 3, 4)
            qc, kc, vc, lrc = map(to_chunks, (q, k, v, lr))
            W_in0 = jnp.broadcast_to(W_in_init, (b, D_INNER, H, HD))
            W_out0 = jnp.broadcast_to(W_out_init, (b, D_INNER, H, HD))
            mask = jnp.tril(jnp.ones((CHUNK, CHUNK), jnp.float32))

            def step(carry, xs):
                W_in, W_out = carry
                q_t, k_t, v_t, lr_t = xs
                k_h = jax.nn.softmax(jnp.einsum('blhd,bDhd->blhD', k_t, W_in), axis=-1) * lr_t[..., 1:]
                q_h = jax.nn.softmax(jnp.einsum('blhd,bDhd->blhD', q_t, W_in), axis=-1)
                qk = jnp.einsum('bqhD,bkhD->bhqk', q_h, k_h) * mask
                o_t = jnp.einsum('bqhD,bDhd->bqhd', q_h, W_out) + jnp.einsum('bhqk,bkhd->bqhd', qk, v_t)
                W_out = W_out + jnp.einsum('bnhD,bnhd->bDhd', k_h, v_t)
                lr_in = lr_t[:, :1, :, 0:1]
                lr_out = lr_t[:, :1, :, 1:2]
                for _ in range(2):
                    g_out = -attn(W_in, k_t, v_t)
                    g_in = -attn(W_out, v_t, k_t)
                    W_in = W_in - lr_in * g_in
                    W_out = W_out - lr_out * g_out
                return ((W_in, W_out), o_t)
            _, o = lax.scan(step, (W_in0, W_out0), (qc, kc, vc, lrc))
            o = o.transpose(1, 0, 2, 3, 4).reshape(b, l, H, HD)
            mu = o.mean(-1, keepdims=True)
            var = ((o - mu) ** 2).mean(-1, keepdims=True)
            o = (o - mu) / jnp.sqrt(var + 1e-05) * ln_g + ln_b
            o = o.reshape(b, l, DIM)
            gate = hidden_states @ Wg.T
            return o * gate @ Wo.T
        return _forward(hidden_states, Wq, Wk, Wv, Wlr, Wg, Wo, cq, ck, cv, W_in_init, W_out_init, ln_g, ln_b)

    def _L0_ffn_ref(x, U1, V1, b1, U2, V2, b2):
        import jax, jax.numpy as jnp
        import numpy as np
        D_MODEL, D_FF, RANK = (256, 1024, 64)
        B, S = (4, 1024)
        P = jnp.einsum('bsd,dr->bsr', x, U1)
        H = jax.nn.gelu(jnp.einsum('bsr,rf->bsf', P, V1) + b1)
        Q = jnp.einsum('bsf,fr->bsr', H, U2)
        return jnp.einsum('bsr,rd->bsd', Q, V2) + b2

    def _L1_attn_ref(x, w_attn, w_proj):
        import jax, jax.numpy as jnp
        import numpy as np
        N_HEAD = 16
        N_EMBD = 256
        LOCAL_WINDOW = 64
        GLOBAL_IDX = np.array([0, 1, 2, 3], dtype=np.int64)

        def build_mask(T):
            i = np.arange(T)[:, None]
            j = np.arange(T)[None, :]
            causal = j <= i
            local = causal & (j >= i - LOCAL_WINDOW + 1)
            g_row = np.isin(np.arange(T), GLOBAL_IDX)[:, None]
            g_col = np.isin(np.arange(T), GLOBAL_IDX)[None, :]
            mask = local | g_row & causal | g_col & causal
            return jnp.asarray(mask)
        B, T, C = x.shape
        H, D = (N_HEAD, C // N_HEAD)
        qkv = jnp.einsum('btc,fc->btf', x, w_attn)
        q, k, v = jnp.split(qkv, 3, axis=-1)
        q = q.reshape(B, T, H, D).transpose(0, 2, 1, 3)
        k = k.reshape(B, T, H, D).transpose(0, 2, 1, 3)
        v = v.reshape(B, T, H, D).transpose(0, 2, 1, 3)
        mask = build_mask(T)
        scale = 1.0 / np.sqrt(D)
        att = jnp.einsum('bhqd,bhkd->bhqk', q, k) * scale
        att = jnp.where(mask, att, jnp.finfo(att.dtype).min)
        att = jax.nn.softmax(att, axis=-1)
        y = jnp.einsum('bhqk,bhkd->bhqd', att, v)
        y = y.transpose(0, 2, 1, 3).reshape(B, T, C)
        return jnp.einsum('btc,oc->bto', y, w_proj)

    def _L1_ffn_ref(x, W_r, W_k, W_v, mu_r, mu_k):
        import jax, jax.numpy as jnp
        import numpy as np
        DIM = 256

        def _reference_tuple_inner(x, W_r, W_k, W_v, mu_r, mu_k):
            B, T, C = x.shape
            x_prev = jnp.concatenate([jnp.zeros((B, 1, C), x.dtype), x[:, :-1, :]], axis=1)
            xr = mu_r * x + (1.0 - mu_r) * x_prev
            xk = mu_k * x + (1.0 - mu_k) * x_prev
            r = jax.nn.sigmoid(jnp.einsum('btc,dc->btd', xr, W_r))
            k = jnp.einsum('btc,dc->btd', xk, W_k)
            k_act = jnp.square(jax.nn.relu(k))
            out = r * jnp.einsum('btc,dc->btd', k_act, W_v)
            new_state = x[:, -1, :]
            return (out, new_state)
        return _reference_tuple_inner(x, W_r, W_k, W_v, mu_r, mu_k)[0]
    x = L0_attn_hidden_states
    mod = (_silu(L0_c) @ L0_wmod).reshape(L0_c.shape[0], 6, 1, -1)
    sa, ca, ga, sb, cb, gb = (mod[:, 0], mod[:, 1], mod[:, 2], mod[:, 3], mod[:, 4], mod[:, 5])
    ga = (2 * (ga >= 0) - 1) * jnp.maximum(jnp.abs(ga), 0.25)
    gb = (2 * (gb >= 0) - 1) * jnp.maximum(jnp.abs(gb), 0.25)
    h = _layernorm(x, axis=-1) * (1 + ca) + sa
    x = x + ga * _L0_attn_ref(h, L0_attn_Wq, L0_attn_Wk, L0_attn_Wv, L0_attn_Wlr, L0_attn_Wg, L0_attn_Wo, L0_attn_cq, L0_attn_ck, L0_attn_cv, L0_attn_W_in_init, L0_attn_W_out_init, L0_attn_ln_g, L0_attn_ln_b)
    h = _layernorm(x, axis=-1) * (1 + cb) + sb
    x = x + gb * _L0_ffn_ref(h, L0_ffn_U1, L0_ffn_V1, L0_ffn_b1, L0_ffn_U2, L0_ffn_V2, L0_ffn_b2)
    mod = (_silu(L1_c) @ L1_wmod).reshape(L1_c.shape[0], 6, 1, -1)
    sa, ca, ga, sb, cb, gb = (mod[:, 0], mod[:, 1], mod[:, 2], mod[:, 3], mod[:, 4], mod[:, 5])
    ga = (2 * (ga >= 0) - 1) * jnp.maximum(jnp.abs(ga), 0.25)
    gb = (2 * (gb >= 0) - 1) * jnp.maximum(jnp.abs(gb), 0.25)
    h = _layernorm(x, axis=-1) * (1 + ca) + sa
    x = x + ga * _L1_attn_ref(h, L1_attn_w_attn, L1_attn_w_proj)
    h = _layernorm(x, axis=-1) * (1 + cb) + sb
    x = x + gb * _L1_ffn_ref(h, L1_ffn_W_r, L1_ffn_W_k, L1_ffn_W_v, L1_ffn_mu_r, L1_ffn_mu_k)
    return x

_drawn_inputs = setup_inputs


def setup_inputs(seed=0):
    import zlib

    import numpy as np

    out = dict(_drawn_inputs(seed))
    spreads = {'L0_attn_ln_g': (1.0, 0.2),
     'L0_attn_ln_b': (0.0, 0.329),
     'L0_ffn_b1': (0.0, 0.8),
     'L0_ffn_b2': (0.0, 2.0)}
    factors = {'L0_attn_Wq': 3.56,
     'L0_attn_cq': 8.0,
     'L0_attn_ck': 7.323,
     'L0_attn_W_in_init': 3.958,
     'L0_ffn_U1': 8.0,
     'L0_ffn_V1': 8.0,
     'L0_ffn_U2': 8.0,
     'L0_ffn_V2': 8.0,
     'L1_ffn_W_r': 8.0,
     'L1_ffn_W_k': 3.147,
     'L1_ffn_W_v': 2.884,
     'L1_ffn_mu_r': 8.0,
     'L1_ffn_mu_k': 5.218}
    for name, (base, spread) in spreads.items():
        noise = np.random.default_rng([zlib.crc32(name.encode()), seed]).standard_normal(out[name].shape)
        drawn = base * np.exp(spread * noise) if base else spread * noise
        out[name] = jnp.asarray(drawn.astype(out[name].dtype))
    for name, factor in factors.items():
        out[name] = (out[name] * factor).astype(out[name].dtype)
    return out
```

```python
from contextlib import ExitStack

import numpy as np
import concourse.bass as bass
from concourse import mybir

P = 128
BATCH, TOK, DIM = 16, 512, 256
HEADS, HD = 16, 16
KT = DIM // P
TT = TOK // P
INNER, CHUNK, TAPS = 4, 16, 4
D_FF, RANK = 1024, 64
FT = D_FF // P
WINDOW, NGLOB = 64, 4
GROUP_B = P // HEADS
GROUPS = BATCH // GROUP_B
BLOCK = 128
BLOCKS = TOK // BLOCK
CPB = BLOCK // CHUNK
QF = 32
FRAMES = TOK // QF
HF, QTR = FRAMES // 2, FRAMES // 4
KEYS = WINDOW + QF + NGLOB
QUADS = HEADS // 4
ROWS = INNER * CHUNK
PROD = ROWS * HD
BASE_LR = 0.001
EPS = 1e-5
MASKED = -3.0e38
N_MOD = 6
LAYERS = 2
ARENA = 36816

ALU = mybir.AluOpType
ACT = mybir.ActivationFunctionType
AX = mybir.AxisListType
F32 = mybir.dt.float32
BF16 = mybir.dt.bfloat16


class Steps:

    def __init__(self, sem, names):
        self.sem, self.names, self.marked = sem, list(names), 0
        self.index = {name: k for k, name in enumerate(self.names)}
        assert len(self.index) == len(self.names)

    def mark(self, name):
        assert self.names[self.marked % len(self.names)] == name, (self.names[self.marked % len(self.names)], name)
        self.marked += 1
        return self.sem

    def at(self, n, name):
        return (n + 1) * len(self.names) + self.index[name] + 1

    def before(self, n, name):
        return n * len(self.names) + self.index[name] + 1


QKV = ["q0", "q1", "k0", "k1", "v0", "v1"]


def adaln_two_layers(nc, x, w_in, taps, w_out, ln_g, ln_b, w_in_init, w_out_init, u1, v1, b1, u2, v2, b2,
                     cond, wmod, w_attn, w_proj, w_r, w_k, w_v, mu, ident_c, blocks_c, parity_c, mask_c, out):
    ctx = ExitStack()
    with ctx:
        def sb(name, shape, dt=F32):
            return ctx.enter_context(nc.sbuf_tensor(name, shape, dt))

        def sem(name):
            return ctx.enter_context(nc.semaphore(name))

        psum = ctx.enter_context(nc.psum_tensor("psum", [P, 8, 512], F32))
        bank = [psum[:, i] for i in range(8)]

        def dram(name, shape):
            return nc.dram_tensor(name, shape, F32, kind="Internal").ap()

        qkv_d = [dram(f"{c}_d", [BATCH, DIM, TOK]) for c in "qkv"]
        gate_d = dram("gate_d", [BATCH, DIM, TOK])
        lr_d = dram("lr_d", [BATCH, 2 * HEADS, TOK])
        o_d = dram("o_d", [BATCH, DIM, TOK])

        w_in_sb = sb("w_in_sb", [P, KT, 4 * DIM + 2 * HEADS])
        taps_sb = sb("taps_sb", [P, KT, 3 * TAPS])
        w_out_sb = sb("w_out_sb", [P, KT, DIM])
        lngb_sb = sb("lngb_sb", [P, 2])
        u1_sb = sb("u1_sb", [P, KT, RANK])
        v1_sb = sb("v1_sb", [RANK + 1, D_FF])
        u2_sb = sb("u2_sb", [P, FT, RANK])
        v2_sb = sb("v2_sb", [RANK + 1, DIM])
        w_attn_sb = sb("w_attn_sb", [P, KT, 3 * DIM])
        w_proj_sb = sb("w_proj_sb", [P, KT, DIM])
        w_rkv_sb = sb("w_rkv_sb", [P, 3, KT, DIM])
        mu_sb = sb("mu_sb", [P, 2, KT])
        ident = sb("ident", [P, P])
        identb = sb("identb", [P, P], BF16)
        mean16 = sb("mean16", [P, P])
        parity = sb("parity", [P, 7])
        mask_sb = sb("mask_sb", [P, 4, KT * KEYS], BF16)
        state0 = sb("state0", [P, 2, ROWS])
        modc = sb("modc", [P, LAYERS * N_MOD * KT, BATCH])
        gates_row = sb("gates_row", [BATCH, 2 * LAYERS * DIM])

        arena = sb("arena", [P, ARENA])
        top = [0]

        def carve(*shape):
            size = int(np.prod(shape))
            ap = arena[:, top[0]:top[0] + size]
            top[0] += size
            assert top[0] <= ARENA, top[0]
            if len(shape) == 2:
                ap = ap.rearrange("p (a b) -> p a b", a=shape[0])
            if len(shape) == 3:
                ap = ap.rearrange("p (a b c) -> p a b c", a=shape[0], b=shape[1])
            return ap


        wmod_sb = carve(LAYERS, KT, N_MOD * DIM)
        cond_sb = carve(LAYERS, KT, BATCH)
        cond_silu = carve(LAYERS, KT, BATCH)
        g_raw = carve(2 * LAYERS * DIM)
        g_sign = carve(2 * LAYERS * DIM)
        g_size = carve(2 * LAYERS * DIM)

        top[0] = 0
        a_x = carve(TT, DIM)
        a_xhat = carve(TT, DIM)
        a_stat = carve(TT, 6)
        a_mv = carve(TT, 2)
        a_std = carve(TT)
        a_rstd = carve(TT)
        a_modb = carve(2 * KT)
        a_h = carve(KT, TOK)
        a_acc = carve(6, TOK)
        a_gate = carve(KT, TOK)
        a_lr = carve(TOK)

        top[0] = 0
        scan_keep = carve(PROD)
        k_blk, q_blk, v_blk = (carve(HD, BLOCK) for _ in range(3))
        lr_blk = carve(2, BLOCK)
        o_blk = carve(HD, BLOCK)
        sq_blk = carve(2, HD, BLOCK)
        norm, rnorm, nsq = carve(2, BLOCK), carve(2, BLOCK), carve(2, BLOCK)
        lr_abs, lr_exp, lr_ln, lr_fin = (carve(2, BLOCK) for _ in range(4))
        t_dve, t_kv, t_g, t_b2, t_q, t_o, run = (carve(PROD) for _ in range(7))
        t_q8, t_q4, t_q2, t_o2 = carve(PROD // 2), carve(PROD // 4), carve(PROD // 8), carve(PROD // 2)
        win, win1, wout2, wout, d_in, d_out = (carve(ROWS) for _ in range(6))
        s_a, e_k, e_p, p_out1, k_hat, s_b, e_b, p_in1, s_q, e_q, q_hat = (carve(ROWS) for _ in range(11))
        s_2, e_2, p_2 = (carve(2 * INNER, CHUNK) for _ in range(3))
        m_k, z_k, r_k, rl_k, m_q, z_q, r_q = (carve(CHUNK) for _ in range(7))
        m_p, z_p, r_p, rl_p, m_b, z_b, r_b, rl_b = (carve(INNER) for _ in range(8))
        m_2, z_2, r_2, rl_2 = (carve(2 * INNER) for _ in range(4))

        top[0] = 0
        SLOTS = range(2)
        c_x = [carve(TT, DIM) for _ in SLOTS]
        c_xy = [carve(TT * DIM) for _ in SLOTS]
        c_xhat = [t.rearrange("p (a b) -> p a b", a=TT) for t in c_xy]
        c_y = [t.rearrange("p (t k q) -> p t k q", t=TT, k=KT) for t in c_xy]
        c_stat = [carve(TT, 6) for _ in SLOTS]
        c_mv = [carve(TT, 2) for _ in SLOTS]
        c_std = [carve(TT) for _ in SLOTS]
        c_rstd = [carve(TT) for _ in SLOTS]
        c_modb = [carve(3, 2 * KT) for _ in SLOTS]
        c_pick = [carve(P) for _ in SLOTS]
        c_h = [carve(KT, TOK + 1) for _ in SLOTS]
        c_h3 = [carve(KT, FRAMES, KEYS) for _ in SLOTS]
        c_wo = [carve(KT, DIM) for _ in SLOTS]
        c_wp = [carve(KT, DIM) for _ in SLOTS]
        c_wv = [carve(KT, DIM) for _ in SLOTS]
        c_v2 = [carve(DIM) for _ in SLOTS]
        c_soft = [carve(2, 4, KEYS) for _ in SLOTS]
        c_max, c_sum, c_rec = ([carve(4) for _ in SLOTS] for _ in range(3))
        c_pt = [carve(4 * P) for _ in SLOTS]
        c_yeven = [carve(KT * QTR, QF) for _ in SLOTS]
        base = top[0]
        c_o, c_gate, c_osq, c_ostd = ([carve(KT, TOK) for _ in SLOTS] for _ in range(4))
        top[0] = base
        c_pq = [carve(2, TOK) for _ in SLOTS]
        c_p, c_qr = [t[:, 0] for t in c_pq], [t[:, 1] for t in c_pq]
        c_one = [t[RANK:RANK + 1] for t in c_pq]
        c_f = [carve(3, TOK) for _ in SLOTS]
        top[0] = base
        c_qq = [carve(KT, TOK) for _ in SLOTS]
        c_qb = [carve(KT, FRAMES // 2, 4 * QF) for _ in SLOTS]
        c_k = [carve(KT, FRAMES, KEYS) for _ in SLOTS]
        c_v = [carve(FRAMES // 2, DIM) for _ in SLOTS]
        top[0] = base
        c_d = [carve(KT, TOK) for _ in SLOTS]
        c_xr = [carve(KT, TOK) for _ in SLOTS]
        c_xk = [carve(KT, TOK) for _ in SLOTS]
        c_r = [carve(TT, DIM) for _ in SLOTS]
        c_kk = [carve(KT, TOK) for _ in SLOTS]
        c_rv = [carve(TT, DIM) for _ in SLOTS]

        held = sem("held")

        def hold(eng):
            eng.sem_inc(held, 1)

        cond_loaded, wmod_loaded = sem("cond_loaded"), sem("wmod_loaded")
        consts_loaded = sem("consts_loaded")
        weights_loaded = sem("weights_loaded")
        su_act = Steps(sem("su_act"), ["silu", "modc", "raw0", "raw1"])
        su_pe = Steps(sem("su_pe"), ["mod", "gate0", "gate1"])
        su_dve = Steps(sem("su_dve"), ["identb", "plus1", "plus2", "plus3", "plus4", "tap", "side", "sign", "size", "gates"])

        x_loaded = sem("x_loaded")
        a_stored = {t: sem(f"stored_{t}") for t in QKV + ["g0", "g1", "lr"]}
        ln_dve = Steps(sem("ln_dve"), [f"st{t}" for t in range(TT)] + [f"ag{t}" for t in range(TT)] + ["rec"]
                       + [f"xh{t}" for t in range(TT)])
        ln_act = Steps(sem("ln_act"), ["modb", "std", "h0", "h1"])
        ln_pe = Steps(sem("ln_pe"), ["t0", "t1"])
        pr_pe = Steps(sem("pr_pe"), QKV + ["g0", "g1", "lr"])
        pr_act = Steps(sem("pr_act"), ["tap0", "tap1", "tap2", "silu0", "tap3", "silu1", "tap4", "silu2", "tap5",
                                       "silu3", "g0", "silu4", "g1", "silu5", "lr"])
        pr_dve = Steps(sem("pr_dve"), [f"c{t}{j}" for t in range(6) for j in (1, 2, 3)])

        blk_loaded = sem("blk_loaded")
        o_stored = sem("o_stored")
        scan_ready = Steps(sem("scan_ready"), ["ones", "zeros"])
        st_dve = Steps(sem("st_dve"), ["in", "out"])
        bl_act = Steps(sem("bl_act"), ["sq_q", "sq_k", "abs", "sqrt", "exp", "ln"])
        bl_dve = Steps(sem("bl_dve"), ["n_q", "n_k", "rec", "k", "lr"])
        bl_pool = Steps(sem("bl_pool"), ["q"])
        re_act = Steps(sem("re_act"), ["ek", "ep", "eb", "eq", "e2"])
        re_pool = Steps(sem("re_pool"), ["sq_mul", "sq8", "sq4", "sq2", "sq1", "g1", "b2", "g2", "o_mul", "o2", "o1"])
        re_dve = Steps(sem("re_dve"), [
            "a0_mul", "a0", "kmax", "ksub", "pmax", "psub", "ksum", "krec", "klr", "kh", "kv", "psum", "prec", "plr",
            "p1", "carry", "run", "b1_mul", "b1", "bmax", "bsub", "qmax", "qsub", "d_out1", "wout2", "bsum", "brec",
            "blr", "pin", "d1_mul", "d1", "win1", "a1_mul", "a1", "b2", "max2", "sub2", "qsum", "qrec", "qh",
            "sum2", "rec2", "lr2", "p2", "d2_mul", "d2", "win", "d_out2", "wout"])

        c_ready = sem("c_ready")
        c_loaded = [sem(f"c_loaded{s}") for s in SLOTS]
        out_stored = [sem(f"out_stored{s}") for s in SLOTS]
        HALVES = range(2)
        ln_names = lambda i, s: [f"st{i}{s}{t}" for t in range(TT)] + [f"ag{i}{s}{t}" for t in range(TT)]
        xh_names = lambda i, s: [f"rec{i}{s}"] + [f"xh{i}{s}{t}" for t in range(TT)]

        def each(*fs):
            return [n for s in SLOTS for f in fs for n in f(s)]

        def att_dve(half):
            names = [n for s in SLOTS for n in (f"max{s}{half * HF}", f"sub{s}{half * HF}")]
            for f in range(half * HF, half * HF + HF):
                for s in SLOTS:
                    if f + 1 < half * HF + HF:
                        names += [f"max{s}{f + 1}", f"sub{s}{f + 1}"]
                    names += [f"sum{s}{f}", f"arec{s}{f}"]
                if f % QTR == 0 and f % HF:
                    names += [f"y{s}{f // QTR - 1}" for s in SLOTS]
            return names + [f"y{s}{2 * half + 1}" for s in SLOTS]

        def att_act(half):
            names = []
            for f in range(half * HF, half * HF + HF):
                names += [f"exp{s}{f}" for s in SLOTS]
                if f % QTR == 0 and f % HF:
                    names += [f"ye{s}{f // QTR - 1}" for s in SLOTS]
                names += [f"pt{s}{f}" for s in SLOTS]
            return names + [f"ye{s}{2 * half + 1}" for s in SLOTS]

        c_dve = Steps(sem("c_dve"),
            each(lambda s: [f"pick{s}", f"modb{s}"])
            + each(lambda s: [f"wo{s}", f"v2{s}", f"wp{s}", f"wv{s}"])
            + each(lambda s: [f"oc{s}{k}" for k in range(KT)])
            + each(lambda s: [f"orec{s}", f"on{s}", f"og{s}", f"oz{s}"])
            + each(lambda s: [f"x1{s}0", f"x1{s}1"] + ln_names(1, s)) + each(lambda s: xh_names(1, s))
            + each(lambda s: [f"x2{s}0", f"x2{s}1"] + ln_names(2, s)) + each(lambda s: xh_names(2, s))
            + each(lambda s: [f"ks{s}{g}" for g in range(4)])
            + [n for h in HALVES for n in
               each(lambda s: [f"qb{s}{h}{k}{j}" for k in range(KT) for j in range(4)])
               + each(lambda s: [f"vf{s}{h}{i}" for i in (1, 3)])
               + att_dve(h)]
            + each(lambda s: [f"x3{s}0", f"x3{s}1"] + ln_names(3, s)) + each(lambda s: xh_names(3, s))
            + each(lambda s: [f"{m}{s}{k}" for k in range(KT) for m in ("xr", "xk")])
            + each(lambda s: [f"rv{s}0", f"rv{s}1"]))
        c_act = Steps(sem("c_act"),
            each(lambda s: [f"osq{s}{k}" for k in range(KT)]) + each(lambda s: [f"ostd{s}{k}" for k in range(KT)])
            + each(lambda s: [f"std1{s}"]) + each(lambda s: [f"h1{s}{k}" for k in range(KT)])
            + each(lambda s: [f"p{s}"]) + [f"gelu{s}{f}" for f in range(FT) for s in SLOTS] + each(lambda s: [f"qr{s}"])
            + each(lambda s: [f"std2{s}"]) + each(lambda s: [f"h3{s}{k}{g}" for k in range(KT) for g in range(4)])
            + each(lambda s: [f"q{s}0", f"q{s}1"] + [f"ks{s}{g}" for g in range(4)])
            + [n for h in HALVES for n in
               each(lambda s: [f"vf{s}{h}{i}" for i in (0, 2)])
               + att_act(h)]
            + each(lambda s: [f"std3{s}"]) + each(lambda s: [f"h4{s}{k}" for k in range(KT)])
            + each(lambda s: [f"r{s}0", f"r{s}1", f"kk{s}0", f"kk{s}1"]))

        def ffn_pe():
            names = [f"v1{s}{f}" for s in SLOTS for f in range(3)]
            for f in range(FT):
                for s in SLOTS:
                    names.append(f"u2{s}{f}")
                    if f + 3 < FT:
                        names.append(f"v1{s}{f + 3}")
            return names

        def att_pe(half):
            names = [f"s{s}{half * HF}" for s in SLOTS]
            for f in range(half * HF, half * HF + HF):
                if f + 1 < half * HF + HF:
                    names += [f"s{s}{f + 1}" for s in SLOTS]
                names += [f"t{s}{f}" for s in SLOTS] + [f"pv{s}{f}" for s in SLOTS]
            return names

        c_pe = Steps(sem("c_pe"),
            each(lambda s: [f"gb{s}0", f"gb{s}1", f"mean{s}0", f"mean{s}1"])
            + each(lambda s: [f"var{s}0", f"var{s}1"]) + each(lambda s: [f"wo{s}0", f"wo{s}1"])
            + each(lambda s: [f"turn1{s}0", f"turn1{s}1"]) + each(lambda s: [f"u1{s}"]) + ffn_pe()
            + each(lambda s: [f"v2{s}0", f"v2{s}1"]) + each(lambda s: [f"turn2{s}0", f"turn2{s}1"])
            + each(lambda s: [f"q{s}0", f"q{s}1", f"k{s}0", f"k{s}1"])
            + [n for h in HALVES for n in each(lambda s: [f"vf{s}{h}{i}" for i in range(4)]) + att_pe(h)]
            + each(lambda s: [f"wp{s}0", f"wp{s}1"]) + each(lambda s: [f"turn3{s}0", f"turn3{s}1"])
            + each(lambda s: [f"r{s}0", f"r{s}1", f"kk{s}0", f"kk{s}1"]) + each(lambda s: [f"vv{s}0", f"vv{s}1"]))
        c_pool = Steps(sem("c_pool"),
            each(lambda s: [f"one{s}"])
            + [f"prob{s}{f}" for f in range(FRAMES) for s in SLOTS]
            + each(lambda s: [f"d{s}"]) + each(lambda s: [f"kk{s}0", f"kk{s}1"]) + each(lambda s: [f"x4{s}0", f"x4{s}1"]))

        block = ctx.enter_context(nc.Block())

        def phase_a_done(eng):
            eng.wait_ge(pr_act.sem, pr_act.before(BATCH, "lr"))
            eng.wait_ge(pr_dve.sem, pr_dve.before(BATCH, "c53"))
            eng.wait_ge(pr_pe.sem, pr_pe.before(BATCH, "lr"))
            for s in a_stored.values():
                eng.wait_ge(s, 16 * BATCH)

        NBLK = GROUPS * BLOCKS

        @block.sync
        def _(sp):
            sp.dma_start(cond_sb, cond.rearrange("l (k p) b -> p l k b", p=P)).then_inc(cond_loaded, 16)
            for layer in range(LAYERS):
                sp.dma_start(wmod_sb[:, layer], wmod[layer].rearrange("(k p) n -> p k n", p=P)).then_inc(wmod_loaded, 16)
            for dst, src in ((ident[:], ident_c), (mean16[:], blocks_c), (parity[:], parity_c)):
                sp.dma_start(dst, src).then_inc(consts_loaded, 16)
            for dst, src in (
                (w_in_sb[:], w_in.rearrange("(k p) n -> p k n", p=P)),
                (taps_sb[:], taps.rearrange("(k p) n -> p k n", p=P)),
                (w_out_sb[:], w_out.rearrange("(k p) n -> p k n", p=P)),
                (lngb_sb[:, 0:1], ln_g),
                (lngb_sb[:, 1:2], ln_b),
                (u1_sb[:], u1.rearrange("(k p) n -> p k n", p=P)),
                (v1_sb[0:RANK], v1),
                (v1_sb[RANK:RANK + 1], b1),
                (u2_sb[:], u2.rearrange("(k p) n -> p k n", p=P)),
                (v2_sb[0:RANK], v2),
                (v2_sb[RANK:RANK + 1], b2),
                (w_attn_sb[:], w_attn.rearrange("(k p) n -> p k n", p=P)),
                (w_proj_sb[:], w_proj.rearrange("(k p) n -> p k n", p=P)),
                (w_rkv_sb[:, 0], w_r.rearrange("(k p) n -> p k n", p=P)),
                (w_rkv_sb[:, 1], w_k.rearrange("(k p) n -> p k n", p=P)),
                (w_rkv_sb[:, 2], w_v.rearrange("(k p) n -> p k n", p=P)),
                (mu_sb[:], mu),
                (mask_sb[:], mask_c),
            ):
                sp.dma_start(dst, src).then_inc(weights_loaded, 16)
            for g in range(GROUP_B):
                rows = slice(g * HEADS, (g + 1) * HEADS)
                for i, init in enumerate((w_in_init, w_out_init)):
                    sp.dma_start(state0[rows, i].rearrange("p (a d) -> p a d", a=INNER),
                                 init.rearrange("a h d -> h a d")).then_inc(weights_loaded, 16)

            sp.wait_ge(su_pe.sem, su_pe.before(1, "gate1"))
            sp.wait_ge(su_dve.sem, su_dve.before(1, "gates"))

            def load_x(n):
                sp.dma_start(a_x, x[bass.ds(n, 1)].rearrange("o (t p) d -> p (o t) d", p=P)).then_inc(x_loaded, 16)

            def stores(n):
                for t, name in enumerate(QKV):
                    sp.wait_ge(pr_act.sem, pr_act.at(n, f"silu{t}"))
                    dst = qkv_d[t // KT][bass.ds(n, 1)].rearrange("o c t -> (o c) t")[(t % KT) * P:(t % KT + 1) * P]
                    sp.dma_start(dst, a_acc[:, t]).then_inc(a_stored[name], 16)
                for k in range(KT):
                    sp.wait_ge(pr_act.sem, pr_act.at(n, f"g{k}"))
                    dst = gate_d[bass.ds(n, 1)].rearrange("o c t -> (o c) t")[k * P:(k + 1) * P]
                    sp.dma_start(dst, a_gate[:, k]).then_inc(a_stored[f"g{k}"], 16)
                sp.wait_ge(pr_act.sem, pr_act.at(n, "lr"))
                sp.dma_start(lr_d[bass.ds(n, 1)].rearrange("o c t -> (o c) t"), a_lr[0:2 * HEADS]).then_inc(a_stored["lr"], 16)

            load_x(0)
            with sp.Fori(0, BATCH - 1) as n:
                sp.wait_ge(ln_dve.sem, ln_dve.at(n, "xh3"))
                load_x(n + 1)
                stores(n)
            stores(BATCH - 1)

            phase_a_done(sp)
            pair = lambda d: d.rearrange("b (h d) t -> (b h) d t", h=HEADS)
            with sp.Fori(0, GROUPS) as g:
                with sp.Fori(0, BLOCKS) as t:
                    n = g * BLOCKS + t
                    sp.wait_ge(re_dve.sem, re_dve.before(n * CPB, "wout"))
                    sp.wait_ge(re_pool.sem, re_pool.before(n * CPB, "o_mul"))
                    for dst, src in ((q_blk, qkv_d[0]), (k_blk, qkv_d[1]), (v_blk, qkv_d[2])):
                        sp.dma_start(dst, pair(src)[bass.ds(g * P, P), :, bass.ds(t * BLOCK, BLOCK)]).then_inc(blk_loaded, 16)
                    sp.dma_start(lr_blk, lr_d.rearrange("b (h i) t -> (b h) i t", i=2)[
                        bass.ds(g * P, P), :, bass.ds(t * BLOCK, BLOCK)]).then_inc(blk_loaded, 16)
                    sp.wait_ge(re_pool.sem, re_pool.before((n + 1) * CPB, "o1"))
                    sp.dma_start(pair(o_d)[bass.ds(g * P, P), :, bass.ds(t * BLOCK, BLOCK)], o_blk).then_inc(o_stored, 16)

            sp.wait_ge(c_ready, 5 * len(SLOTS))
            with sp.Fori(0, BATCH // 2) as i:
                for s in SLOTS:
                    b = i * 2 + s
                    sp.wait_ge(out_stored[s], 32 * i)
                    sp.dma_start(c_x[s], x[bass.ds(b, 1)].rearrange("o (t p) d -> p (o t) d", p=P)).then_inc(c_loaded[s], 16)
                    sp.wait_ge(c_pool.sem, c_pool.before(i, "x411"))
                    hold(sp)
                    for dst, src in ((c_o[s], o_d), (c_gate[s], gate_d)):
                        sp.dma_start(dst, src[bass.ds(b, 1)].rearrange("o (k p) t -> p (o k) t", p=P)).then_inc(c_loaded[s], 16)
                for s in SLOTS:
                    b = i * 2 + s
                    for a in range(2):
                        sp.wait_ge(c_pool.sem, c_pool.at(i, f"x4{s}{a}"))
                        hold(sp)
                        sp.dma_start(out[bass.ds(b, 1)].rearrange("o (t p) d -> p (o t) d", p=P)[:, 2 * a:2 * a + 2],
                                     c_x[s][:, 2 * a:2 * a + 2]).then_inc(out_stored[s], 16)
            for s in SLOTS:
                sp.wait_ge(out_stored[s], 32 * (BATCH // 2))

        @block.tensor
        def _(pe):
            for st in (su_pe, ln_pe, pr_pe, c_pe):
                pe.sem_inc(st.sem, len(st.names))
            pe.wait_ge(wmod_loaded, 16 * LAYERS)
            pe.wait_ge(su_act.sem, su_act.at(0, "silu"))
            for layer in range(LAYERS):
                for m in range(N_MOD * KT):
                    col = (layer * N_MOD * KT + m) * BATCH
                    for k in range(KT):
                        mm = pe.matmul(bank[0][:, col:col + BATCH], wmod_sb[:, layer, k, m * P:(m + 1) * P],
                                       cond_silu[:, layer, k], start=(k == 0), stop=(k == KT - 1))
            mm.then_inc(su_pe.mark("mod"), 1)
            for layer in range(LAYERS):
                for j, which in enumerate((2, 5)):
                    for k in range(KT):
                        mm = pe.matmul(bank[1 + layer][0:BATCH, j * DIM:(j + 1) * DIM], cond_silu[:, layer, k],
                                       wmod_sb[:, layer, k, which * DIM:(which + 1) * DIM],
                                       start=(k == 0), stop=(k == KT - 1))
                mm.then_inc(su_pe.mark(f"gate{layer}"), 1)

            def turn(m):
                pe.wait_ge(ln_dve.sem, ln_dve.at(m, "xh3"))
                pe.wait_ge(ln_act.sem, ln_act.before(m, "h1"))
                for k in range(KT):
                    for t in range(TT):
                        mm = pe.transpose(bank[k][:, t * P:(t + 1) * P], a_xhat[:, t, k * P:(k + 1) * P], ident[:])
                    mm.then_inc(ln_pe.mark(f"t{k}"), 1)

            def project(n):
                pe.wait_ge(ln_act.sem, ln_act.at(n, "h1"))
                for j, name in enumerate(QKV + ["g0", "g1", "lr"]):
                    if name == "g0":
                        pe.wait_ge(pr_dve.sem, pr_dve.at(n, "c03"))
                    elif name == "g1":
                        pe.wait_ge(pr_dve.sem, pr_dve.at(n, "c13"))
                    elif name == "lr":
                        pe.wait_ge(pr_dve.sem, pr_dve.at(n, "c23"))
                    elif name == "q0":
                        pe.wait_ge(pr_act.sem, pr_act.before(n, "g0"))
                    elif name == "q1":
                        pe.wait_ge(pr_act.sem, pr_act.before(n, "g1"))
                    elif name == "k0":
                        pe.wait_ge(pr_act.sem, pr_act.before(n, "lr"))
                    else:
                        pe.wait_ge(pr_dve.sem, pr_dve.before(n, f"c{j}3"))
                    rows = 2 * HEADS if name == "lr" else P
                    for k in range(KT):
                        mm = pe.matmul(bank[2 + j % 6][0:rows], w_in_sb[:, k, j * P:j * P + rows], a_h[:, k],
                                       start=(k == 0), stop=(k == KT - 1))
                    mm.then_inc(pr_pe.mark(name), 1)

            pe.wait_ge(consts_loaded, 48)
            pe.wait_ge(weights_loaded, 16 * (18 + 2 * GROUP_B))
            pe.wait_ge(su_act.sem, su_act.at(0, "modc"))
            turn(0)
            pe.wait_ge(su_act.sem, su_act.at(0, "raw1"))
            with pe.Fori(0, BATCH - 1) as n:
                project(n)
                turn(n + 1)
            project(BATCH - 1)

            phase_a_done(pe)
            with pe.Fori(0, BATCH // 2) as i:
                B = lambda s, j: bank[4 * s + j]
                for s in SLOTS:
                    pe.wait_ge(c_dve.sem, c_dve.at(i, f"pick{s}"))
                    pe.wait_ge(c_dve.sem, c_dve.before(i, f"rv{s}1"))
                    for layer in range(LAYERS):
                        mm = pe.matmul(B(s, layer)[:], c_pick[s][0:BATCH], gates_row[:, layer * 2 * DIM:(layer + 1) * 2 * DIM],
                                       start=True, stop=True)
                        mm.then_inc(c_pe.mark(f"gb{s}{layer}"), 1)
                    pe.wait_ge(c_loaded[s], 48 * (i + 1))
                    pe.wait_ge(c_act.sem, c_act.before(i, f"kk{s}1"))
                    for k in range(KT):
                        mm = pe.matmul(B(s, 2 + k)[:], mean16[:], c_o[s][:, k], start=True, stop=True)
                        mm.then_inc(c_pe.mark(f"mean{s}{k}"), 1)
                for s in SLOTS:
                    for k in range(KT):
                        pe.wait_ge(c_act.sem, c_act.at(i, f"osq{s}{k}"))
                        pe.wait_ge(c_dve.sem, c_dve.at(i, f"oc{s}{k}"))
                        mm = pe.matmul(B(s, 2 + k)[:], mean16[:], c_osq[s][:, k], start=True, stop=True)
                        mm.then_inc(c_pe.mark(f"var{s}{k}"), 1)

                def rows_out(s, name, lhs, rhs, banks):
                    for a in range(2):
                        for j in range(2):
                            for k in range(KT):
                                mm = pe.matmul(B(s, banks[a])[:, j * DIM:(j + 1) * DIM], lhs(k, 2 * a + j), rhs(k),
                                               start=(k == 0), stop=(k == KT - 1))
                        mm.then_inc(c_pe.mark(f"{name}{s}{a}"), 1)

                def tok(t):
                    return slice(t * P, (t + 1) * P)

                def turn_c(s, stage, banks):
                    pe.wait_ge(c_dve.sem, c_dve.at(i, f"xh{stage}{s}3"))
                    for k in range(KT):
                        for t in range(TT):
                            mm = pe.transpose(B(s, banks[k])[:, tok(t)], c_xhat[s][:, t, k * P:(k + 1) * P], ident[:])
                        mm.then_inc(c_pe.mark(f"turn{stage}{s}{k}"), 1)

                for s in SLOTS:
                    pe.wait_ge(c_dve.sem, c_dve.at(i, f"oz{s}"))
                    rows_out(s, "wo", lambda k, t: c_o[s][:, k, tok(t)], lambda k: c_wo[s][:, k], (0, 1))
                for s in SLOTS:
                    pe.wait_ge(c_act.sem, c_act.at(i, f"ostd{s}1"))
                    turn_c(s, 1, (2, 3))
                for s in SLOTS:
                    pe.wait_ge(c_act.sem, c_act.at(i, f"h1{s}1"))
                    for k in range(KT):
                        mm = pe.matmul(B(s, 0)[0:RANK], u1_sb[:, k], c_h[s][:, k, 1:TOK + 1], start=(k == 0), stop=(k == KT - 1))
                    mm.then_inc(c_pe.mark(f"u1{s}"), 1)

                def up(s, f):
                    if f == 0:
                        pe.wait_ge(c_act.sem, c_act.at(i, f"p{s}"))
                        pe.wait_ge(c_pool.sem, c_pool.at(i, f"one{s}"))
                    if f >= 3:
                        pe.wait_ge(c_act.sem, c_act.at(i, f"gelu{s}{f - 3}"))
                    mm = pe.matmul(B(s, 1 + f % 3)[:], v1_sb[:, f * P:(f + 1) * P], c_p[s][0:RANK + 1], start=True, stop=True)
                    mm.then_inc(c_pe.mark(f"v1{s}{f}"), 1)

                for s in SLOTS:
                    for f in range(3):
                        up(s, f)
                for f in range(FT):
                    for s in SLOTS:
                        pe.wait_ge(c_act.sem, c_act.at(i, f"gelu{s}{f}"))
                        mm = pe.matmul(B(s, 0)[0:RANK], u2_sb[:, f], c_f[s][:, f % 3], start=(f == 0), stop=(f == FT - 1))
                        mm.then_inc(c_pe.mark(f"u2{s}{f}"), 1)
                        if f + 3 < FT:
                            up(s, f + 3)
                for s in SLOTS:
                    pe.wait_ge(c_act.sem, c_act.at(i, f"qr{s}"))
                    for a in range(2):
                        for j in range(2):
                            mm = pe.matmul(B(s, 1 + a)[:, j * DIM:(j + 1) * DIM], c_qr[s][0:RANK + 1, tok(2 * a + j)],
                                           c_v2[s][0:RANK + 1], start=True, stop=True)
                        mm.then_inc(c_pe.mark(f"v2{s}{a}"), 1)
                for s in SLOTS:
                    turn_c(s, 2, (3, 0))
                own = lambda s, k: c_h3[s][:, k, :, WINDOW:WINDOW + QF]
                for s in SLOTS:
                    pe.wait_ge(c_act.sem, c_act.at(i, f"h3{s}{KT - 1}3"))
                    pe.wait_ge(c_dve.sem, c_dve.at(i, f"x2{s}1"))
                    for j, (name, bk) in enumerate((("q0", 1), ("q1", 2), ("k0", 3), ("k1", 0))):
                        for k in range(KT):
                            mm = pe.matmul(B(s, bk)[:], w_attn_sb[:, k, j * P:(j + 1) * P], own(s, k),
                                           start=(k == 0), stop=(k == KT - 1))
                        mm.then_inc(c_pe.mark(f"{name[0]}{s}{name[1]}"), 1)

                for half in HALVES:
                    for s in SLOTS:
                        if half == 0:
                            pe.wait_ge(c_act.sem, c_act.at(i, f"ks{s}3"))
                            pe.wait_ge(c_dve.sem, c_dve.at(i, f"ks{s}3"))
                        else:
                            pe.wait_ge(c_dve.sem, c_dve.at(i, f"y{s}1"))
                        for j in range(4):
                            for e in range(2):
                                f = half * HF + 2 * j + e
                                for k in range(KT):
                                    mm = pe.matmul(B(s, (j + 1) % 4)[0:KEYS, e * DIM:(e + 1) * DIM], c_h3[s][:, k, f],
                                                   w_attn_sb[:, k, 2 * DIM:3 * DIM], start=(k == 0), stop=(k == KT - 1))
                            mm.then_inc(c_pe.mark(f"vf{s}{half}{j}"), 1)

                    def scores(s, f):
                        if f % HF == 0:
                            pe.wait_ge(c_act.sem, c_act.at(i, f"vf{s}{half}0"))
                            pe.wait_ge(c_dve.sem, c_dve.at(i, f"vf{s}{half}3"))
                        else:
                            pe.wait_ge(c_dve.sem, c_dve.at(i, f"sub{s}{f - 1}"))
                        for top in range(2):
                            pe.matmul(B(s, top)[:, 0:KT * KEYS], identb[:], mask_sb[:, min(f, 3)], start=True, stop=False,
                                      skip_group_check=True)
                        for k in range(KT):
                            for top in range(2):
                                rows = slice(64 * top, 64 * top + 64)
                                mm = pe.matmul(B(s, top)[:, k * KEYS:(k + 1) * KEYS], c_qb[s][rows, k, f % HF],
                                               c_k[s][rows, k, f], start=False, stop=True, skip_group_check=True)
                        mm.then_inc(c_pe.mark(f"s{s}{f}"), 1)

                    for s in SLOTS:
                        scores(s, half * HF)
                    for f in range(half * HF, half * HF + HF):
                        if f + 1 < half * HF + HF:
                            for s in SLOTS:
                                scores(s, f + 1)
                        for s in SLOTS:
                            pe.wait_ge(c_pool.sem, c_pool.at(i, f"prob{s}{f}"))
                            if f % HF == 0:
                                pe.wait_ge(c_dve.sem, c_dve.at(i, f"vf{s}{half}1"))
                            else:
                                pe.wait_ge(c_act.sem, c_act.at(i, f"pt{s}{f - 1}"))
                            for u in range(QUADS):
                                mm = pe.transpose(B(s, 2)[0:KEYS, tok(u)], c_soft[s][:, f % 2, u], ident[:])
                            mm.then_inc(c_pe.mark(f"t{s}{f}"), 1)
                        for s in SLOTS:
                            pe.wait_ge(c_act.sem, c_act.at(i, f"pt{s}{f}"))
                            if f % HF == 0:
                                pe.wait_ge(c_act.sem, c_act.at(i, f"vf{s}{half}2"))
                                pe.wait_ge(c_dve.sem, c_dve.at(i, f"vf{s}{half}3"))
                            elif f % QTR == 0:
                                pe.wait_ge(c_dve.sem, c_dve.at(i, f"y{s}{f // QTR - 1}"))
                            for u in range(QUADS):
                                top, k = u // 2, u % 2
                                for pr in range(2):
                                    head = (k * P + 64 * top) // HD + 2 * pr
                                    row = 64 * top + 32 * pr
                                    col = (k * QTR + f % QTR) * 2 * QF
                                    mm = pe.matmul(B(s, 3)[row:row + 32, col:col + 2 * QF],
                                                   c_v[s][0:KEYS, f % HF, head * HD:(head + 2) * HD],
                                                   c_pt[s][0:KEYS, u * P + 64 * pr:u * P + 64 * pr + 64],
                                                   start=True, stop=True)
                            mm.then_inc(c_pe.mark(f"pv{s}{f}"), 1)
                for s in SLOTS:
                    pe.wait_ge(c_dve.sem, c_dve.at(i, f"y{s}3"))
                    rows_out(s, "wp", lambda k, t: c_y[s][:, t, k], lambda k: c_wp[s][:, k], (0, 1))
                for s in SLOTS:
                    turn_c(s, 3, (2, 3))
                for s in SLOTS:
                    pe.wait_ge(c_dve.sem, c_dve.at(i, f"xk{s}{KT - 1}"))
                    rows_out(s, "r", lambda k, t: c_xr[s][:, k, tok(t)], lambda k: w_rkv_sb[:, 0, k], (0, 1))
                    for m in range(KT):
                        for k in range(KT):
                            mm = pe.matmul(B(s, 2 + m)[:], w_rkv_sb[:, 1, k, m * P:(m + 1) * P], c_xk[s][:, k],
                                           start=(k == 0), stop=(k == KT - 1))
                        mm.then_inc(c_pe.mark(f"kk{s}{m}"), 1)
                for s in SLOTS:
                    pe.wait_ge(c_pool.sem, c_pool.at(i, f"kk{s}1"))
                    pe.wait_ge(c_act.sem, c_act.at(i, f"r{s}1"))
                    rows_out(s, "vv", lambda k, t: c_kk[s][:, k, tok(t)], lambda k: c_wv[s][:, k], (0, 1))

        @block.scalar
        def _(act):
            for st in (su_act, ln_act, pr_act, bl_act, re_act, c_act):
                act.sem_inc(st.sem, len(st.names))
            act.wait_ge(cond_loaded, 16)
            act.activation(cond_silu, cond_sb, ACT.Silu).then_inc(su_act.mark("silu"), 1)
            act.wait_ge(su_pe.sem, su_pe.at(0, "mod"))
            act.activation(modc[:].rearrange("p a b -> p (a b)"), bank[0][:, 0:LAYERS * N_MOD * KT * BATCH], ACT.Copy).then_inc(su_act.mark("modc"), 1)
            for layer in range(LAYERS):
                act.wait_ge(su_pe.sem, su_pe.at(0, f"gate{layer}"))
                act.activation(g_raw[0:BATCH, layer * 2 * DIM:(layer + 1) * 2 * DIM], bank[1 + layer][0:BATCH], ACT.Copy).then_inc(su_act.mark(f"raw{layer}"), 1)

            def norm_a(m):
                act.wait_ge(su_dve.sem, su_dve.at(0, "gates"))
                act.wait_ge(ln_act.sem, ln_act.before(m, "h1"))
                ins = act.activation(a_modb, modc[:, 0:2 * KT, bass.ds(m, 1)].rearrange("p a o -> p (a o)"), ACT.Copy)
                ins.then_inc(ln_act.mark("modb"), 1)
                act.wait_ge(ln_dve.sem, ln_dve.at(m, "ag3"))
                act.activation(a_std, a_mv[:, :, 1], ACT.Sqrt, bias=parity[:, 6:7]).then_inc(ln_act.mark("std"), 1)

            def modulate_a(m):
                act.wait_ge(ln_act.sem, ln_act.at(m, "modb"))
                act.wait_ge(pr_pe.sem, pr_pe.before(m, "lr"))
                for k in range(KT):
                    act.wait_ge(ln_pe.sem, ln_pe.at(m, f"t{k}"))
                    ins = act.activation(a_h[:, k], bank[k][:], ACT.Identity, bias=a_modb[:, k:k + 1], scale=a_modb[:, KT + k:KT + k + 1])
                    ins.then_inc(ln_act.mark(f"h{k}"), 1)

            def evacuate(n):
                def tap(t):
                    act.wait_ge(pr_pe.sem, pr_pe.at(n, QKV[t]))
                    act.wait_ge(a_stored[QKV[t]], 16 * n)
                    col = (t // KT) * TAPS + TAPS - 1
                    ins = act.activation(a_acc[:, t], bank[2 + t][:], ACT.Copy, scale=taps_sb[:, t % KT, col:col + 1])
                    ins.then_inc(pr_act.mark(f"tap{t}"), 1)

                def silu(t):
                    act.wait_ge(pr_dve.sem, pr_dve.at(n, f"c{t}3"))
                    act.activation(a_acc[:, t], a_acc[:, t], ACT.Silu).then_inc(pr_act.mark(f"silu{t}"), 1)

                def gate(k):
                    act.wait_ge(pr_pe.sem, pr_pe.at(n, f"g{k}"))
                    act.wait_ge(a_stored[f"g{k}"], 16 * n)
                    act.activation(a_gate[:, k], bank[2 + k][:], ACT.Copy).then_inc(pr_act.mark(f"g{k}"), 1)

                tap(0), tap(1), tap(2), silu(0), tap(3), silu(1), tap(4), silu(2), tap(5), silu(3)
                gate(0), silu(4), gate(1), silu(5)
                act.wait_ge(pr_pe.sem, pr_pe.at(n, "lr"))
                act.wait_ge(a_stored["lr"], 16 * n)
                ins = act.activation(a_lr[0:2 * HEADS], bank[4][0:2 * HEADS], ACT.Copy, bias=BASE_LR)
                ins.then_inc(pr_act.mark("lr"), 1)

            norm_a(0)
            modulate_a(0)
            with act.Fori(0, BATCH - 1) as n:
                norm_a(n + 1)
                evacuate(n)
                modulate_a(n + 1)
            evacuate(BATCH - 1)

            phase_a_done(act)
            with act.Fori(0, NBLK) as n:
                act.wait_ge(blk_loaded, 64 * (n + 1))
                act.wait_ge(bl_dve.sem, bl_dve.before(n, "n_k"))
                act.activation(sq_blk[:, 0], q_blk, ACT.Square).then_inc(bl_act.mark("sq_q"), 1)
                act.activation(sq_blk[:, 1], k_blk, ACT.Square).then_inc(bl_act.mark("sq_k"), 1)
                act.activation(lr_abs, lr_blk, ACT.Abs).then_inc(bl_act.mark("abs"), 1)
                act.wait_ge(bl_dve.sem, bl_dve.at(n, "n_k"))
                act.activation(norm, nsq, ACT.Sqrt).then_inc(bl_act.mark("sqrt"), 1)
                act.wait_ge(bl_act.sem, bl_act.at(n, "abs"))
                act.activation(lr_exp, lr_abs, ACT.Exp, scale=-1.0).then_inc(bl_act.mark("exp"), 1)
                act.wait_ge(bl_act.sem, bl_act.at(n, "exp"))
                act.activation(lr_ln, lr_exp, ACT.Ln, bias=1.0).then_inc(bl_act.mark("ln"), 1)
                with act.Fori(0, CPB) as j:
                    c = n * CPB + j
                    for name, step, buf, scale in (("ek", "ksub", e_k, 1.0), ("ep", "psub", e_p, 0.25), ("eb", "bsub", e_b, 0.25),
                                                   ("eq", "qsub", e_q, 1.0), ("e2", "sub2", e_2, 0.25)):
                        act.wait_ge(re_dve.sem, re_dve.at(c, step))
                        act.activation(buf, buf, ACT.Exp, scale=scale).then_inc(re_act.mark(name), 1)

            with act.Fori(0, BATCH // 2) as i:
                B = lambda s, j: bank[4 * s + j]

                def std(stage, s):
                    act.wait_ge(c_dve.sem, c_dve.at(i, f"ag{stage}{s}{TT - 1}"))
                    act.activation(c_std[s], c_mv[s][:, :, 1], ACT.Sqrt, bias=parity[:, 6:7]).then_inc(c_act.mark(f"std{stage}{s}"), 1)

                for s in SLOTS:
                    for k in range(KT):
                        act.wait_ge(c_dve.sem, c_dve.at(i, f"oc{s}{k}"))
                        act.activation(c_osq[s][:, k], c_o[s][:, k], ACT.Square).then_inc(c_act.mark(f"osq{s}{k}"), 1)
                for s in SLOTS:
                    for k in range(KT):
                        act.wait_ge(c_pe.sem, c_pe.at(i, f"var{s}{k}"))
                        act.activation(c_ostd[s][:, k], B(s, 2 + k)[:], ACT.Sqrt, bias=parity[:, 6:7]).then_inc(c_act.mark(f"ostd{s}{k}"), 1)

                def modulate(stage, s, banks):
                    for k in range(KT):
                        act.wait_ge(c_pe.sem, c_pe.at(i, f"turn{stage}{s}{k}"))
                        ins = act.activation(c_h[s][:, k, 1:TOK + 1], B(s, banks[k])[:], ACT.Identity,
                                             bias=c_modb[s][:, {1: 0, 3: 2}[stage], k:k + 1],
                                             scale=c_modb[s][:, {1: 0, 3: 2}[stage], KT + k:KT + k + 1])
                        ins.then_inc(c_act.mark(f"h{1 if stage == 1 else 4}{s}{k}"), 1)

                for s in SLOTS:
                    std(1, s)
                for s in SLOTS:
                    modulate(1, s, (2, 3))
                for s in SLOTS:
                    act.wait_ge(c_pe.sem, c_pe.at(i, f"u1{s}"))
                    act.wait_ge(c_pe.sem, c_pe.at(i, "wo11"))
                    act.activation(c_p[s][0:RANK], B(s, 0)[0:RANK], ACT.Copy).then_inc(c_act.mark(f"p{s}"), 1)
                for f in range(FT):
                    for s in SLOTS:
                        act.wait_ge(c_pe.sem, c_pe.at(i, f"v1{s}{f}"))
                        if f >= 3:
                            act.wait_ge(c_pe.sem, c_pe.at(i, f"u2{s}{f - 3}"))
                        act.activation(c_f[s][:, f % 3], B(s, 1 + f % 3)[:], ACT.Gelu_apprx_tanh).then_inc(c_act.mark(f"gelu{s}{f}"), 1)
                for s in SLOTS:
                    act.wait_ge(c_pe.sem, c_pe.at(i, f"u2{s}{FT - 1}"))
                    act.activation(c_qr[s][0:RANK], B(s, 0)[0:RANK], ACT.Copy).then_inc(c_act.mark(f"qr{s}"), 1)
                for s in SLOTS:
                    std(2, s)

                def segments(dst, src):
                    blocks = src.rearrange("p (f q) -> p f q", q=QF)
                    return ((dst[:, 2:FRAMES, 0:QF], blocks[:, 0:FRAMES - 2]),
                            (dst[:, 1:FRAMES, QF:2 * QF], blocks[:, 0:FRAMES - 1]),
                            (dst[:, :, 2 * QF:3 * QF], blocks),
                            (dst[:, :, 3 * QF:KEYS], src[:, 0:NGLOB].unsqueeze(1).broadcast_to([P, FRAMES, NGLOB])))

                for s in SLOTS:
                    for k in range(KT):
                        act.wait_ge(c_pe.sem, c_pe.at(i, f"turn2{s}{k}"))
                        for g, (dst, src) in enumerate(segments(c_h3[s][:, k], B(s, (3, 0)[k])[:])):
                            ins = act.activation(dst, src, ACT.Identity, bias=c_modb[s][:, 1, k:k + 1],
                                                 scale=c_modb[s][:, 1, KT + k:KT + k + 1])
                            ins.then_inc(c_act.mark(f"h3{s}{k}{g}"), 1)
                for s in SLOTS:
                    for k in range(KT):
                        act.wait_ge(c_pe.sem, c_pe.at(i, f"q{s}{k}"))
                        act.activation(c_qq[s][:, k], B(s, 1 + k)[:], ACT.Copy).then_inc(c_act.mark(f"q{s}{k}"), 1)
                    act.wait_ge(c_pe.sem, c_pe.at(i, f"k{s}1"))
                    for g, (dst, src) in enumerate(segments(c_k[s][:, 1], B(s, 0)[:])):
                        act.activation(dst, src, ACT.Copy).then_inc(c_act.mark(f"ks{s}{g}"), 1)

                def even(s, quarter):
                    act.wait_ge(c_pe.sem, c_pe.at(i, f"pv{s}{quarter * QTR + QTR - 1}"))
                    if quarter:
                        act.wait_ge(c_dve.sem, c_dve.at(i, f"y{s}{quarter - 1}"))
                    src = B(s, 3)[:].rearrange("p (f e q) -> p f e q", e=2, q=QF)[:, :, 0]
                    act.activation(c_yeven[s], src, ACT.Copy, scale=parity[:, 4:5]).then_inc(c_act.mark(f"ye{s}{quarter}"), 1)

                for half in HALVES:
                    for s in SLOTS:
                        for j in (0, 2):
                            act.wait_ge(c_pe.sem, c_pe.at(i, f"vf{s}{half}{j}"))
                            dst = c_v[s][0:KEYS, 2 * j:2 * j + 2]
                            act.activation(dst, B(s, (j + 1) % 4)[0:KEYS].rearrange("p (e d) -> p e d", e=2), ACT.Copy).then_inc(c_act.mark(f"vf{s}{half}{j}"), 1)
                    for f in range(half * HF, half * HF + HF):
                        for s in SLOTS:
                            act.wait_ge(c_dve.sem, c_dve.at(i, f"sub{s}{f}"))
                            act.activation(c_soft[s][:, f % 2], c_soft[s][:, f % 2], ACT.Exp, scale=float(HD) ** -0.5).then_inc(c_act.mark(f"exp{s}{f}"), 1)
                        if f % QTR == 0 and f % HF:
                            for s in SLOTS:
                                even(s, f // QTR - 1)
                        for s in SLOTS:
                            act.wait_ge(c_pe.sem, c_pe.at(i, f"t{s}{f}"))
                            if f > 0:
                                act.wait_ge(c_pe.sem, c_pe.at(i, f"pv{s}{f - 1}"))
                            act.activation(c_pt[s][0:KEYS], B(s, 2)[0:KEYS], ACT.Copy).then_inc(c_act.mark(f"pt{s}{f}"), 1)
                    for s in SLOTS:
                        even(s, 2 * half + 1)
                for s in SLOTS:
                    std(3, s)
                for s in SLOTS:
                    modulate(3, s, (2, 3))
                for s in SLOTS:
                    for a in range(2):
                        act.wait_ge(c_pe.sem, c_pe.at(i, f"r{s}{a}"))
                        act.activation(c_r[s][:, 2 * a:2 * a + 2], B(s, a)[:].rearrange("p (t d) -> p t d", t=2), ACT.Sigmoid).then_inc(c_act.mark(f"r{s}{a}"), 1)
                    for m in range(KT):
                        act.wait_ge(c_pe.sem, c_pe.at(i, f"kk{s}{m}"))
                        act.activation(c_kk[s][:, m], B(s, 2 + m)[:], ACT.Relu).then_inc(c_act.mark(f"kk{s}{m}"), 1)

        @block.gpsimd
        def _(pool):
            for st in (scan_ready, bl_pool, re_pool, c_pool):
                pool.sem_inc(st.sem, len(st.names))
            phase_a_done(pool)
            pool.memset(scan_keep, 1.0).then_inc(scan_ready.mark("ones"), 1)
            pool.wait_ge(scan_ready.sem, scan_ready.at(0, "ones"))
            pool.memset(scan_keep.rearrange("p (a l) -> p a l", l=CHUNK)[:, :, 0:1], 0.0).then_inc(scan_ready.mark("zeros"), 1)
            with pool.Fori(0, GROUPS) as g:
                pool.wait_ge(st_dve.sem, st_dve.at(g, "out"))
                hold(pool)
                with pool.Fori(0, BLOCKS) as b:
                    n = g * BLOCKS + b
                    pool.wait_ge(bl_dve.sem, bl_dve.at(n, "rec"))
                    pool.wait_ge(bl_act.sem, bl_act.at(n, "sq_q"))
                    pool.tensor_tensor(q_blk, q_blk, rnorm[:, 0].unsqueeze(1).broadcast_to([P, HD, BLOCK]), ALU.mult).then_inc(bl_pool.mark("q"), 1)
                    pool.wait_ge(o_stored, 16 * n)
                    hold(pool)
                    with pool.Fori(0, CPB) as j:
                        c = n * CPB + j
                        now = lambda blk: blk[:, :, bass.ds(j * CHUNK, CHUNK)]
                        by_ld = lambda w: w.rearrange("p (a d) -> p a d", a=INNER).unsqueeze(2).broadcast_to([P, INNER, CHUNK, HD])
                        by_dl = lambda w: w.rearrange("p (a l) -> p a l", a=INNER).unsqueeze(2).broadcast_to([P, INNER, HD, CHUNK])
                        tok_ld = lambda b: now(b).rearrange("p d l -> p l d").unsqueeze(1).broadcast_to([P, INNER, CHUNK, HD])
                        tok_dl = lambda b: now(b).unsqueeze(1).broadcast_to([P, INNER, HD, CHUNK])
                        cube = lambda t: t.rearrange("p (a l d) -> p a l d", a=INNER, l=16)

                        pool.wait_ge(bl_pool.sem, bl_pool.at(n, "q"))
                        pool.wait_ge(re_dve.sem, re_dve.before(c, "win"))
                        hold(pool)
                        pool.tensor_tensor(cube(t_q), by_ld(win), tok_ld(q_blk), ALU.mult).then_inc(re_pool.mark("sq_mul"), 1)
                        for name, prev, dst, src, half in (("sq8", "sq_mul", t_q8, t_q, 8), ("sq4", "sq8", t_q4, t_q8, 4),
                                                           ("sq2", "sq4", t_q2, t_q4, 2), ("sq1", "sq2", s_q, t_q2, 1)):
                            pool.wait_ge(re_pool.sem, re_pool.at(c, prev))
                            if name == "sq1":
                                pool.wait_ge(re_dve.sem, re_dve.before(c, "qsub"))
                            v = src.rearrange("p (x h) -> p x h", h=2 * half)
                            pool.tensor_tensor(dst.rearrange("p (x h) -> p x h", h=half), v[:, :, 0:half], v[:, :, half:2 * half], ALU.add).then_inc(re_pool.mark(name), 1)
                        pool.wait_ge(re_dve.sem, re_dve.at(c, "p1"))
                        pool.wait_ge(re_dve.sem, re_dve.before(c, "d_out2"))
                        hold(pool)
                        pool.tensor_tensor(cube(t_g), by_dl(p_out1), tok_dl(v_blk), ALU.mult).then_inc(re_pool.mark("g1"), 1)
                        pool.wait_ge(re_dve.sem, re_dve.at(c, "wout2"))
                        hold(pool)
                        pool.tensor_tensor(cube(t_b2), by_ld(wout2), tok_ld(v_blk), ALU.mult).then_inc(re_pool.mark("b2"), 1)
                        pool.wait_ge(re_dve.sem, re_dve.at(c, "p2"))
                        hold(pool)
                        pool.tensor_tensor(cube(t_g), by_dl(p_2[:, INNER:2 * INNER].rearrange("p a l -> p (a l)")), tok_dl(v_blk), ALU.mult).then_inc(re_pool.mark("g2"), 1)
                        pool.wait_ge(re_dve.sem, re_dve.at(c, "qh"))
                        hold(pool)
                        pool.tensor_tensor(cube(t_o), by_dl(q_hat), cube(run), ALU.mult).then_inc(re_pool.mark("o_mul"), 1)
                        pool.wait_ge(re_pool.sem, re_pool.at(c, "o_mul"))
                        half = PROD // 2
                        pool.tensor_tensor(t_o2, t_o[:, 0:half], t_o[:, half:PROD], ALU.add).then_inc(re_pool.mark("o2"), 1)
                        pool.wait_ge(re_pool.sem, re_pool.at(c, "o2"))
                        hold(pool)
                        quarter = PROD // 4
                        to = lambda t: t.rearrange("p (d l) -> p d l", d=HD)
                        pool.tensor_tensor(now(o_blk), to(t_o2[:, 0:quarter]), to(t_o2[:, quarter:half]), ALU.add).then_inc(re_pool.mark("o1"), 1)

            with pool.Fori(0, BATCH // 2) as i:
                for s in SLOTS:
                    pool.wait_ge(c_pe.sem, c_pe.at(i, "wo11"))
                    hold(pool)
                    pool.memset(c_one[s], 1.0).then_inc(c_pool.mark(f"one{s}"), 1)
                for f in range(FRAMES):
                    for s in SLOTS:
                        pool.wait_ge(c_dve.sem, c_dve.at(i, f"arec{s}{f}"))
                        soft = c_soft[s][:, f % 2]
                        pool.tensor_tensor(soft, soft, c_rec[s].unsqueeze(2).broadcast_to([P, 4, KEYS]), ALU.mult).then_inc(c_pool.mark(f"prob{s}{f}"), 1)
                for s in SLOTS:
                    pool.wait_ge(c_act.sem, c_act.at(i, f"h4{s}{KT - 1}"))
                    h = c_h[s]
                    pool.tensor_tensor(c_d[s], h[:, :, 1:TOK + 1], h[:, :, 0:TOK], ALU.subtract).then_inc(c_pool.mark(f"d{s}"), 1)
                for s in SLOTS:
                    for m in range(KT):
                        pool.wait_ge(c_act.sem, c_act.at(i, f"kk{s}{m}"))
                        pool.tensor_tensor(c_kk[s][:, m], c_kk[s][:, m], c_kk[s][:, m], ALU.mult).then_inc(c_pool.mark(f"kk{s}{m}"), 1)
                for s in SLOTS:
                    for a in range(2):
                        pool.wait_ge(c_dve.sem, c_dve.at(i, f"rv{s}{a}"))
                        half = slice(2 * a, 2 * a + 2)
                        pool.tensor_tensor(c_x[s][:, half], c_x[s][:, half], c_rv[s][:, half], ALU.add).then_inc(c_pool.mark(f"x4{s}{a}"), 1)

        @block.vector
        def _(dve):
            for st in (su_dve, ln_dve, pr_dve, st_dve, bl_dve, re_dve, c_dve):
                dve.sem_inc(st.sem, len(st.names))
            dve.wait_ge(consts_loaded, 48)
            dve.tensor_copy(identb[:], ident[:]).then_inc(su_dve.mark("identb"), 1)
            dve.wait_ge(su_act.sem, su_act.at(0, "modc"))
            for j, layer_which in enumerate((1, 4, 7, 10)):
                cols = modc[:, layer_which * KT:(layer_which + 1) * KT]
                dve.tensor_scalar(cols, cols, 1.0, None, ALU.add).then_inc(su_dve.mark(f"plus{j + 1}"), 1)
            dve.wait_ge(weights_loaded, 16 * (18 + 2 * GROUP_B))
            own_tap = taps_sb[:].rearrange("p k (c j) -> p k c j", j=TAPS)[:, :, :, TAPS - 1]
            dve.tensor_scalar(own_tap, own_tap, 1.0, None, ALU.add).then_inc(su_dve.mark("tap"), 1)
            dve.wait_ge(su_act.sem, su_act.at(0, "raw1"))
            dve.tensor_scalar(g_sign[0:BATCH], g_raw[0:BATCH], 0.0, 2.0, ALU.is_ge, ALU.mult).then_inc(su_dve.mark("side"), 1)
            dve.wait_ge(su_dve.sem, su_dve.at(0, "side"))
            dve.tensor_scalar(g_sign[0:BATCH], g_sign[0:BATCH], -1.0, None, ALU.add).then_inc(su_dve.mark("sign"), 1)
            dve.wait_ge(su_dve.sem, su_dve.at(0, "sign"))
            dve.tensor_tensor(g_size[0:BATCH], g_sign[0:BATCH], g_raw[0:BATCH], ALU.mult).then_inc(su_dve.mark("size"), 1)
            dve.wait_ge(su_dve.sem, su_dve.at(0, "size"))
            dve.scalar_tensor_tensor(out=gates_row[:], in0=g_size[0:BATCH], scalar=0.25, in1=g_sign[0:BATCH],
                                                 op0=ALU.max, op1=ALU.mult).then_inc(su_dve.mark("gates"), 1)

            def normalise_a(m):
                dve.wait_ge(x_loaded, 16 * (m + 1))
                dve.wait_ge(ln_act.sem, ln_act.before(m, "std"))
                for t in range(TT):
                    dve.bn_stats(a_stat[:, t], a_x[:, t]).then_inc(ln_dve.mark(f"st{t}"), 1)
                dve.wait_ge(ln_dve.sem, ln_dve.at(m, f"st{TT - 1}"))
                hold(dve)
                for t in range(TT):
                    dve.bn_aggr(a_mv[:, t], a_stat[:, t]).then_inc(ln_dve.mark(f"ag{t}"), 1)
                dve.wait_ge(ln_act.sem, ln_act.at(m, "std"))
                dve.reciprocal(a_rstd, a_std).then_inc(ln_dve.mark("rec"), 1)
                dve.wait_ge(ln_dve.sem, ln_dve.at(m, "rec"))
                dve.wait_ge(ln_pe.sem, ln_pe.before(m, "t1"))
                for t in range(TT):
                    dve.tensor_scalar(a_xhat[:, t], a_x[:, t], a_mv[:, t, 0:1], a_rstd[:, t:t + 1],
                                                  ALU.subtract, ALU.mult).then_inc(ln_dve.mark(f"xh{t}"), 1)

            def convolve(n):
                for t in range(6):
                    for j in (1, 2, 3):
                        if j == 1:
                            dve.wait_ge(pr_act.sem, pr_act.at(n, f"tap{t}"))
                        else:
                            dve.wait_ge(pr_dve.sem, pr_dve.at(n, f"c{t}{j - 1}"))
                        col = (t // KT) * TAPS + TAPS - 1 - j
                        ins = dve.scalar_tensor_tensor(out=a_acc[:, t, j:TOK], in0=bank[2 + t][:, 0:TOK - j],
                                                       scalar=taps_sb[:, t % KT, col:col + 1], in1=a_acc[:, t, j:TOK],
                                                       op0=ALU.mult, op1=ALU.add)
                        ins.then_inc(pr_dve.mark(f"c{t}{j}"), 1)

            dve.wait_ge(su_dve.sem, su_dve.at(0, "tap"))
            normalise_a(0)
            with dve.Fori(0, BATCH - 1) as n:
                normalise_a(n + 1)
                convolve(n)
            convolve(BATCH - 1)

            phase_a_done(dve)
            dve.wait_ge(scan_ready.sem, scan_ready.at(0, "zeros"))
            with dve.Fori(0, GROUPS) as g:
                dve.wait_ge(re_pool.sem, re_pool.before(g * (BLOCKS * CPB), "o_mul"))
                dve.wait_ge(re_dve.sem, re_dve.before(g * (BLOCKS * CPB), "wout"))
                dve.tensor_copy(win, state0[:, 0]).then_inc(st_dve.mark("in"), 1)
                dve.tensor_copy(wout, state0[:, 1]).then_inc(st_dve.mark("out"), 1)
                dve.wait_ge(st_dve.sem, st_dve.at(g, "out"))
                hold(dve)
                with dve.Fori(0, BLOCKS) as b:
                    n = g * BLOCKS + b
                    dl = lambda t: t.rearrange("p d l -> p l d")
                    dve.wait_ge(bl_act.sem, bl_act.at(n, "sq_q"))
                    dve.wait_ge(bl_act.sem, bl_act.before(n, "sqrt"))
                    dve.tensor_reduce(nsq[:, 0], dl(sq_blk[:, 0]), AX.X, ALU.add).then_inc(bl_dve.mark("n_q"), 1)
                    dve.wait_ge(bl_act.sem, bl_act.at(n, "sq_k"))
                    dve.tensor_reduce(nsq[:, 1], dl(sq_blk[:, 1]), AX.X, ALU.add).then_inc(bl_dve.mark("n_k"), 1)
                    dve.wait_ge(bl_act.sem, bl_act.at(n, "sqrt"))
                    dve.wait_ge(bl_pool.sem, bl_pool.before(n, "q"))
                    dve.reciprocal(rnorm, norm).then_inc(bl_dve.mark("rec"), 1)
                    dve.wait_ge(bl_dve.sem, bl_dve.at(n, "rec"))
                    dve.tensor_tensor(k_blk, k_blk, rnorm[:, 1].unsqueeze(1).broadcast_to([P, HD, BLOCK]), ALU.mult).then_inc(bl_dve.mark("k"), 1)
                    dve.wait_ge(bl_act.sem, bl_act.at(n, "ln"))
                    dve.scalar_tensor_tensor(out=lr_fin, in0=lr_blk, scalar=0.0, in1=lr_ln, op0=ALU.max, op1=ALU.add).then_inc(bl_dve.mark("lr"), 1)
                    dve.wait_ge(bl_dve.sem, bl_dve.at(n, "lr"))
                    hold(dve)
                    with dve.Fori(0, CPB) as j:
                        c = n * CPB + j
                        now = lambda blk: blk[:, :, bass.ds(j * CHUNK, CHUNK)]
                        by_ld = lambda w: w.unsqueeze(2).broadcast_to([P, INNER, CHUNK, HD])
                        by_dl = lambda w: w.unsqueeze(2).broadcast_to([P, INNER, HD, CHUNK])
                        tok_ld = lambda blk: now(blk).rearrange("p d l -> p l d").unsqueeze(1).broadcast_to([P, INNER, CHUNK, HD])
                        tok_dl = lambda blk: now(blk).unsqueeze(1).broadcast_to([P, INNER, HD, CHUNK])
                        cube = lambda t: t.rearrange("p (a l d) -> p a l d", a=INNER, l=16)
                        grid = lambda t: t.rearrange("p (a l) -> p a l", a=INNER)
                        rows = lambda t: t.rearrange("p (x d) -> p x d", d=16)
                        over_a = lambda t: t.rearrange("p (a l) -> p l a", a=INNER)
                        per_l = lambda t: t.unsqueeze(1).broadcast_to([P, INNER, CHUNK])
                        per_a = lambda t: t.unsqueeze(2).broadcast_to([P, INNER, CHUNK])
                        rate = lambda which, k: lr_fin[:, which, bass.ds(j * CHUNK, 1)].broadcast_to([P, k])

                        dve.wait_ge(re_dve.sem, re_dve.before(c, "win"))
                        dve.tensor_tensor(cube(t_dve), by_ld(grid(win)), tok_ld(k_blk), ALU.mult).then_inc(re_dve.mark("a0_mul"), 1)
                        dve.wait_ge(re_dve.sem, re_dve.at(c, "a0_mul"))
                        dve.tensor_reduce(s_a, rows(t_dve), AX.X, ALU.add).then_inc(re_dve.mark("a0"), 1)
                        dve.wait_ge(re_dve.sem, re_dve.at(c, "a0"))
                        dve.tensor_reduce(m_k, over_a(s_a), AX.X, ALU.max).then_inc(re_dve.mark("kmax"), 1)
                        dve.wait_ge(re_dve.sem, re_dve.at(c, "kmax"))
                        dve.tensor_tensor(grid(e_k), grid(s_a), per_l(m_k), ALU.subtract).then_inc(re_dve.mark("ksub"), 1)
                        dve.tensor_reduce(m_p, grid(s_a), AX.X, ALU.max).then_inc(re_dve.mark("pmax"), 1)
                        dve.wait_ge(re_dve.sem, re_dve.at(c, "pmax"))
                        dve.tensor_tensor(grid(e_p), grid(s_a), per_a(m_p), ALU.subtract).then_inc(re_dve.mark("psub"), 1)
                        dve.wait_ge(re_act.sem, re_act.at(c, "ek"))
                        dve.tensor_reduce(z_k, over_a(e_k), AX.X, ALU.add).then_inc(re_dve.mark("ksum"), 1)
                        dve.wait_ge(re_dve.sem, re_dve.at(c, "ksum"))
                        dve.reciprocal(r_k, z_k).then_inc(re_dve.mark("krec"), 1)
                        dve.wait_ge(re_dve.sem, re_dve.at(c, "krec"))
                        dve.tensor_tensor(rl_k, r_k, lr_fin[:, 1, bass.ds(j * CHUNK, CHUNK)], ALU.mult).then_inc(re_dve.mark("klr"), 1)
                        dve.wait_ge(re_dve.sem, re_dve.at(c, "klr"))
                        dve.tensor_tensor(grid(k_hat), grid(e_k), per_l(rl_k), ALU.mult).then_inc(re_dve.mark("kh"), 1)
                        dve.wait_ge(re_dve.sem, re_dve.at(c, "kh"))
                        dve.tensor_tensor(cube(t_kv), by_dl(grid(k_hat)), tok_dl(v_blk), ALU.mult).then_inc(re_dve.mark("kv"), 1)
                        dve.wait_ge(re_act.sem, re_act.at(c, "ep"))
                        dve.tensor_reduce(z_p, grid(e_p), AX.X, ALU.add).then_inc(re_dve.mark("psum"), 1)
                        dve.wait_ge(re_dve.sem, re_dve.at(c, "psum"))
                        dve.reciprocal(r_p, z_p).then_inc(re_dve.mark("prec"), 1)
                        dve.wait_ge(re_dve.sem, re_dve.at(c, "prec"))
                        dve.tensor_tensor(rl_p, r_p, rate(1, INNER), ALU.mult).then_inc(re_dve.mark("plr"), 1)
                        dve.wait_ge(re_dve.sem, re_dve.at(c, "plr"))
                        dve.wait_ge(re_pool.sem, re_pool.before(c, "g1"))
                        dve.tensor_tensor(grid(p_out1), grid(e_p), per_a(rl_p), ALU.mult).then_inc(re_dve.mark("p1"), 1)
                        first = t_kv.rearrange("p (x l) -> p x l", l=CHUNK)[:, :, 0]
                        dve.tensor_tensor(first, first, wout, ALU.add).then_inc(re_dve.mark("carry"), 1)
                        dve.wait_ge(re_dve.sem, re_dve.at(c, "carry"))
                        dve.wait_ge(re_pool.sem, re_pool.before(c, "o_mul"))
                        dve.tensor_tensor_scan(run, scan_keep, t_kv, 0.0, ALU.mult, ALU.add).then_inc(re_dve.mark("run"), 1)
                        dve.wait_ge(re_dve.sem, re_dve.at(c, "run"))
                        wout1 = run.rearrange("p (x l) -> p x l", l=CHUNK)[:, :, CHUNK - 1]
                        dve.tensor_tensor(cube(t_dve), by_ld(wout1.rearrange("p (a d) -> p a d", a=INNER)), tok_ld(v_blk), ALU.mult).then_inc(re_dve.mark("b1_mul"), 1)
                        dve.wait_ge(re_dve.sem, re_dve.at(c, "b1_mul"))
                        dve.tensor_reduce(s_b, rows(t_dve), AX.X, ALU.add).then_inc(re_dve.mark("b1"), 1)
                        dve.wait_ge(re_dve.sem, re_dve.at(c, "b1"))
                        dve.tensor_reduce(m_b, grid(s_b), AX.X, ALU.max).then_inc(re_dve.mark("bmax"), 1)
                        dve.wait_ge(re_dve.sem, re_dve.at(c, "bmax"))
                        dve.tensor_tensor(grid(e_b), grid(s_b), per_a(m_b), ALU.subtract).then_inc(re_dve.mark("bsub"), 1)
                        dve.wait_ge(re_pool.sem, re_pool.at(c, "sq1"))
                        dve.tensor_reduce(m_q, over_a(s_q), AX.X, ALU.max).then_inc(re_dve.mark("qmax"), 1)
                        dve.wait_ge(re_dve.sem, re_dve.at(c, "qmax"))
                        dve.tensor_tensor(grid(e_q), grid(s_q), per_l(m_q), ALU.subtract).then_inc(re_dve.mark("qsub"), 1)
                        dve.wait_ge(re_pool.sem, re_pool.at(c, "g1"))
                        dve.tensor_reduce(d_out, rows(t_g), AX.X, ALU.add).then_inc(re_dve.mark("d_out1"), 1)
                        dve.wait_ge(re_dve.sem, re_dve.at(c, "d_out1"))
                        dve.wait_ge(re_pool.sem, re_pool.before(c, "b2"))
                        dve.tensor_tensor(wout2, wout1, d_out, ALU.add).then_inc(re_dve.mark("wout2"), 1)
                        dve.wait_ge(re_act.sem, re_act.at(c, "eb"))
                        dve.tensor_reduce(z_b, grid(e_b), AX.X, ALU.add).then_inc(re_dve.mark("bsum"), 1)
                        dve.wait_ge(re_dve.sem, re_dve.at(c, "bsum"))
                        dve.reciprocal(r_b, z_b).then_inc(re_dve.mark("brec"), 1)
                        dve.wait_ge(re_dve.sem, re_dve.at(c, "brec"))
                        dve.tensor_tensor(rl_b, r_b, rate(0, INNER), ALU.mult).then_inc(re_dve.mark("blr"), 1)
                        dve.wait_ge(re_dve.sem, re_dve.at(c, "blr"))
                        dve.tensor_tensor(grid(p_in1), grid(e_b), per_a(rl_b), ALU.mult).then_inc(re_dve.mark("pin"), 1)
                        dve.wait_ge(re_dve.sem, re_dve.at(c, "pin"))
                        dve.tensor_tensor(cube(t_dve), by_dl(grid(p_in1)), tok_dl(k_blk), ALU.mult).then_inc(re_dve.mark("d1_mul"), 1)
                        dve.wait_ge(re_dve.sem, re_dve.at(c, "d1_mul"))
                        dve.tensor_reduce(d_in, rows(t_dve), AX.X, ALU.add).then_inc(re_dve.mark("d1"), 1)
                        dve.wait_ge(re_dve.sem, re_dve.at(c, "d1"))
                        dve.tensor_tensor(win1, win, d_in, ALU.add).then_inc(re_dve.mark("win1"), 1)
                        dve.wait_ge(re_dve.sem, re_dve.at(c, "win1"))
                        dve.tensor_tensor(cube(t_dve), by_ld(grid(win1)), tok_ld(k_blk), ALU.mult).then_inc(re_dve.mark("a1_mul"), 1)
                        dve.wait_ge(re_dve.sem, re_dve.at(c, "a1_mul"))
                        dve.tensor_reduce(s_2[:, INNER:2 * INNER].rearrange("p a l -> p (a l)"), rows(t_dve), AX.X, ALU.add).then_inc(re_dve.mark("a1"), 1)
                        dve.wait_ge(re_pool.sem, re_pool.at(c, "b2"))
                        dve.tensor_reduce(s_2[:, 0:INNER].rearrange("p a l -> p (a l)"), rows(t_b2), AX.X, ALU.add).then_inc(re_dve.mark("b2"), 1)
                        dve.wait_ge(re_dve.sem, re_dve.at(c, "b2"))
                        dve.tensor_reduce(m_2, s_2, AX.X, ALU.max).then_inc(re_dve.mark("max2"), 1)
                        dve.wait_ge(re_dve.sem, re_dve.at(c, "max2"))
                        dve.tensor_tensor(e_2, s_2, m_2.unsqueeze(2).broadcast_to([P, 2 * INNER, CHUNK]), ALU.subtract).then_inc(re_dve.mark("sub2"), 1)
                        dve.wait_ge(re_act.sem, re_act.at(c, "eq"))
                        dve.tensor_reduce(z_q, over_a(e_q), AX.X, ALU.add).then_inc(re_dve.mark("qsum"), 1)
                        dve.wait_ge(re_dve.sem, re_dve.at(c, "qsum"))
                        dve.reciprocal(r_q, z_q).then_inc(re_dve.mark("qrec"), 1)
                        dve.wait_ge(re_dve.sem, re_dve.at(c, "qrec"))
                        dve.tensor_tensor(grid(q_hat), grid(e_q), per_l(r_q), ALU.mult).then_inc(re_dve.mark("qh"), 1)
                        dve.wait_ge(re_act.sem, re_act.at(c, "e2"))
                        dve.tensor_reduce(z_2, e_2, AX.X, ALU.add).then_inc(re_dve.mark("sum2"), 1)
                        dve.wait_ge(re_dve.sem, re_dve.at(c, "sum2"))
                        dve.reciprocal(r_2, z_2).then_inc(re_dve.mark("rec2"), 1)
                        dve.wait_ge(re_dve.sem, re_dve.at(c, "rec2"))
                        rates = lr_fin[:, :, bass.ds(j * CHUNK, 1)].broadcast_to([P, 2, INNER])
                        dve.tensor_tensor(rl_2.rearrange("p (i a) -> p i a", i=2), r_2.rearrange("p (i a) -> p i a", i=2), rates, ALU.mult).then_inc(re_dve.mark("lr2"), 1)
                        dve.wait_ge(re_dve.sem, re_dve.at(c, "lr2"))
                        dve.wait_ge(re_pool.sem, re_pool.before(c, "g2"))
                        dve.tensor_tensor(p_2, e_2, rl_2.unsqueeze(2).broadcast_to([P, 2 * INNER, CHUNK]), ALU.mult).then_inc(re_dve.mark("p2"), 1)
                        dve.wait_ge(re_dve.sem, re_dve.at(c, "p2"))
                        dve.tensor_tensor(cube(t_dve), by_dl(p_2[:, 0:INNER]), tok_dl(k_blk), ALU.mult).then_inc(re_dve.mark("d2_mul"), 1)
                        dve.wait_ge(re_dve.sem, re_dve.at(c, "d2_mul"))
                        dve.tensor_reduce(d_in, rows(t_dve), AX.X, ALU.add).then_inc(re_dve.mark("d2"), 1)
                        dve.wait_ge(re_dve.sem, re_dve.at(c, "d2"))
                        dve.wait_ge(re_pool.sem, re_pool.at(c, "sq_mul"))
                        dve.tensor_tensor(win, win1, d_in, ALU.add).then_inc(re_dve.mark("win"), 1)
                        dve.wait_ge(re_pool.sem, re_pool.at(c, "g2"))
                        dve.tensor_reduce(d_out, rows(t_g), AX.X, ALU.add).then_inc(re_dve.mark("d_out2"), 1)
                        dve.wait_ge(re_dve.sem, re_dve.at(c, "d_out2"))
                        dve.tensor_tensor(wout, wout2, d_out, ALU.add).then_inc(re_dve.mark("wout"), 1)

            dve.wait_ge(re_pool.sem, re_pool.before(NBLK * CPB, "o1"))
            dve.wait_ge(re_act.sem, re_act.before(NBLK * CPB, "e2"))
            dve.wait_ge(re_dve.sem, re_dve.before(NBLK * CPB, "wout"))
            dve.wait_ge(o_stored, 16 * NBLK)
            for s in SLOTS:
                for pad in (c_h[s][:, :, 0:1], c_h3[s][:, :, 0:2, 0:QF], c_h3[s][:, :, 0:1, QF:2 * QF],
                            c_k[s][:, :, 0:2, 0:QF], c_k[s][:, :, 0:1, QF:2 * QF]):
                    dve.memset(pad, 0.0).then_inc(c_ready, 1)
            dve.wait_ge(c_ready, 5 * len(SLOTS))
            with dve.Fori(0, BATCH // 2) as i:
                B = lambda s, j: bank[4 * s + j]

                def residual(stage, s, pe_step, banks):
                    for a in range(2):
                        dve.wait_ge(c_pe.sem, c_pe.at(i, f"{pe_step}{s}{a}"))
                        half = slice(2 * a, 2 * a + 2)
                        dve.tensor_tensor(c_x[s][:, half], c_x[s][:, half],
                                               B(s, banks[a])[:].rearrange("p (t d) -> p t d", t=2), ALU.add).then_inc(c_dve.mark(f"x{stage}{s}{a}"), 1)
                    for t in range(TT):
                        dve.wait_ge(c_dve.sem, c_dve.at(i, f"x{stage}{s}{t // 2}"))
                        dve.bn_stats(c_stat[s][:, t], c_x[s][:, t]).then_inc(c_dve.mark(f"st{stage}{s}{t}"), 1)
                    dve.wait_ge(c_dve.sem, c_dve.at(i, f"st{stage}{s}{TT - 1}"))
                    hold(dve)
                    for t in range(TT):
                        dve.bn_aggr(c_mv[s][:, t], c_stat[s][:, t]).then_inc(c_dve.mark(f"ag{stage}{s}{t}"), 1)

                def normalise(stage, s):
                    dve.wait_ge(c_act.sem, c_act.at(i, f"std{stage}{s}"))
                    dve.reciprocal(c_rstd[s], c_std[s]).then_inc(c_dve.mark(f"rec{stage}{s}"), 1)
                    dve.wait_ge(c_dve.sem, c_dve.at(i, f"rec{stage}{s}"))
                    for t in range(TT):
                        dve.tensor_scalar(c_xhat[s][:, t], c_x[s][:, t], c_mv[s][:, t, 0:1], c_rstd[s][:, t:t + 1],
                                               ALU.subtract, ALU.mult).then_inc(c_dve.mark(f"xh{stage}{s}{t}"), 1)

                for s in SLOTS:
                    b = i * 2 + s
                    dve.wait_ge(c_pe.sem, c_pe.before(i, f"gb{s}1"))
                    dve.tensor_copy(c_pick[s][0:BATCH], ident[0:BATCH, bass.ds(b, 1)].broadcast_to([BATCH, P])).then_inc(c_dve.mark(f"pick{s}"), 1)
                    mods = modc[:, N_MOD // 2 * KT:, bass.ds(b, 1)].rearrange("p (a c) o -> p a (c o)", c=N_MOD // 2 * KT)
                    dve.wait_ge(c_act.sem, c_act.before(i, f"h4{s}{KT - 1}"))
                    dve.tensor_copy(c_modb[s], mods[:, :, 0:2 * KT]).then_inc(c_dve.mark(f"modb{s}"), 1)
                for s in SLOTS:
                    dve.wait_ge(c_pe.sem, c_pe.at(i, f"gb{s}1"))
                    dve.wait_ge(c_pe.sem, c_pe.before(i, f"vv{s}1"))
                    gate = lambda layer, j, p: B(s, layer)[0:p, j * DIM:(j + 1) * DIM]
                    both = lambda layer, j: gate(layer, j, P).unsqueeze(1).broadcast_to([P, KT, DIM])
                    dve.tensor_tensor(c_wo[s], w_out_sb[:], both(0, 0), ALU.mult).then_inc(c_dve.mark(f"wo{s}"), 1)
                    dve.tensor_tensor(c_v2[s][0:RANK + 1], v2_sb[:], gate(0, 1, RANK + 1), ALU.mult).then_inc(c_dve.mark(f"v2{s}"), 1)
                    dve.tensor_tensor(c_wp[s], w_proj_sb[:], both(1, 0), ALU.mult).then_inc(c_dve.mark(f"wp{s}"), 1)
                    dve.tensor_tensor(c_wv[s], w_rkv_sb[:, 2], both(1, 1), ALU.mult).then_inc(c_dve.mark(f"wv{s}"), 1)
                for s in SLOTS:
                    for k in range(KT):
                        dve.wait_ge(c_pe.sem, c_pe.at(i, f"mean{s}{k}"))
                        dve.tensor_tensor(c_o[s][:, k], c_o[s][:, k], B(s, 2 + k)[:], ALU.subtract).then_inc(c_dve.mark(f"oc{s}{k}"), 1)
                for s in SLOTS:
                    dve.wait_ge(c_act.sem, c_act.at(i, f"ostd{s}{KT - 1}"))
                    dve.reciprocal(c_ostd[s], c_ostd[s]).then_inc(c_dve.mark(f"orec{s}"), 1)
                    dve.wait_ge(c_dve.sem, c_dve.at(i, f"orec{s}"))
                    dve.tensor_tensor(c_o[s], c_o[s], c_ostd[s], ALU.mult).then_inc(c_dve.mark(f"on{s}"), 1)
                    dve.wait_ge(c_dve.sem, c_dve.at(i, f"on{s}"))
                    dve.tensor_scalar(c_o[s], c_o[s], lngb_sb[:, 0:1], lngb_sb[:, 1:2], ALU.mult, ALU.add).then_inc(c_dve.mark(f"og{s}"), 1)
                    dve.wait_ge(c_dve.sem, c_dve.at(i, f"og{s}"))
                    dve.tensor_tensor(c_o[s], c_o[s], c_gate[s], ALU.mult).then_inc(c_dve.mark(f"oz{s}"), 1)
                for s in SLOTS:
                    residual(1, s, "wo", (0, 1))
                for s in SLOTS:
                    normalise(1, s)
                for s in SLOTS:
                    residual(2, s, "v2", (1, 2))
                for s in SLOTS:
                    normalise(2, s)

                def segments(dst, src):
                    blocks = src.rearrange("p (f q) -> p f q", q=QF)
                    return ((dst[:, 2:FRAMES, 0:QF], blocks[:, 0:FRAMES - 2]),
                            (dst[:, 1:FRAMES, QF:2 * QF], blocks[:, 0:FRAMES - 1]),
                            (dst[:, :, 2 * QF:3 * QF], blocks),
                            (dst[:, :, 3 * QF:KEYS], src[:, 0:NGLOB].unsqueeze(1).broadcast_to([P, FRAMES, NGLOB])))

                for s in SLOTS:
                    dve.wait_ge(c_pe.sem, c_pe.at(i, f"k{s}0"))
                    for g, (dst, src) in enumerate(segments(c_k[s][:, 0], B(s, 3)[:])):
                        dve.tensor_copy(dst, src).then_inc(c_dve.mark(f"ks{s}{g}"), 1)
                for half in HALVES:
                    for s in SLOTS:
                        dve.wait_ge(c_act.sem, c_act.at(i, f"q{s}1"))
                        if half:
                            dve.wait_ge(c_pe.sem, c_pe.at(i, f"s{s}{HF - 1}"))
                        for k in range(KT):
                            for j in range(4):
                                src = c_qq[s][:, k, half * TOK // 2:(half + 1) * TOK // 2].rearrange("p (f q) -> p f q", q=QF)
                                dve.tensor_scalar(c_qb[s][:, k, :, j * QF:(j + 1) * QF], src, parity[:, j:j + 1], None, ALU.mult).then_inc(c_dve.mark(f"qb{s}{half}{k}{j}"), 1)
                    for s in SLOTS:
                        for j in (1, 3):
                            dve.wait_ge(c_pe.sem, c_pe.at(i, f"vf{s}{half}{j}"))
                            dve.tensor_copy(c_v[s][0:KEYS, 2 * j:2 * j + 2], B(s, (j + 1) % 4)[0:KEYS].rearrange("p (e d) -> p e d", e=2)).then_inc(c_dve.mark(f"vf{s}{half}{j}"), 1)

                    def scores(s, f):
                        dve.wait_ge(c_pe.sem, c_pe.at(i, f"s{s}{f}"))
                        sc = psum[:, 4 * s:4 * s + 2, 0:KT * KEYS].rearrange("p t (k y) -> p t k y", k=KT)
                        quads = lambda t: t.rearrange("p (t k) -> p t k", t=2)
                        dve.tensor_reduce(quads(c_max[s]), sc, AX.X, ALU.max).then_inc(c_dve.mark(f"max{s}{f}"), 1)
                        dve.wait_ge(c_dve.sem, c_dve.at(i, f"max{s}{f}"))
                        if f >= 2:
                            dve.wait_ge(c_pe.sem, c_pe.at(i, f"t{s}{f - 2}"))
                        dve.tensor_tensor(c_soft[s][:, f % 2].rearrange("p (t k) y -> p t k y", t=2), sc,
                                               quads(c_max[s]).unsqueeze(3).broadcast_to([P, 2, KT, KEYS]), ALU.subtract).then_inc(c_dve.mark(f"sub{s}{f}"), 1)

                    def both_heads(s, quarter):
                        dve.wait_ge(c_act.sem, c_act.at(i, f"ye{s}{quarter}"))
                        src = B(s, 3)[:].rearrange("p (f e q) -> p f e q", e=2, q=QF)[:, :, 1]
                        dve.scalar_tensor_tensor(out=c_y[s][:, quarter].rearrange("p k (f q) -> p (k f) q", q=QF), in0=src, scalar=parity[:, 5:6],
                                                      in1=c_yeven[s], op0=ALU.mult, op1=ALU.add).then_inc(c_dve.mark(f"y{s}{quarter}"), 1)

                    for s in SLOTS:
                        scores(s, half * HF)
                    for f in range(half * HF, half * HF + HF):
                        for s in SLOTS:
                            if f + 1 < half * HF + HF:
                                scores(s, f + 1)
                            dve.wait_ge(c_act.sem, c_act.at(i, f"exp{s}{f}"))
                            if f > 0:
                                dve.wait_ge(c_pool.sem, c_pool.at(i, f"prob{s}{f - 1}"))
                            dve.tensor_reduce(c_sum[s], c_soft[s][:, f % 2], AX.X, ALU.add).then_inc(c_dve.mark(f"sum{s}{f}"), 1)
                            dve.wait_ge(c_dve.sem, c_dve.at(i, f"sum{s}{f}"))
                            dve.reciprocal(c_rec[s], c_sum[s]).then_inc(c_dve.mark(f"arec{s}{f}"), 1)
                        if f % QTR == 0 and f % HF:
                            for s in SLOTS:
                                both_heads(s, f // QTR - 1)
                    for s in SLOTS:
                        both_heads(s, 2 * half + 1)
                for s in SLOTS:
                    residual(3, s, "wp", (0, 1))
                for s in SLOTS:
                    normalise(3, s)
                for s in SLOTS:
                    dve.wait_ge(c_pool.sem, c_pool.at(i, f"d{s}"))
                    for k in range(KT):
                        for m, (name, dst) in enumerate((("xr", c_xr[s]), ("xk", c_xk[s]))):
                            dve.scalar_tensor_tensor(out=dst[:, k], in0=c_d[s][:, k], scalar=mu_sb[:, m, k:k + 1],
                                                          in1=c_h[s][:, k, 0:TOK], op0=ALU.mult, op1=ALU.add).then_inc(c_dve.mark(f"{name}{s}{k}"), 1)
                for s in SLOTS:
                    for a in range(2):
                        dve.wait_ge(c_pe.sem, c_pe.at(i, f"vv{s}{a}"))
                        half = slice(2 * a, 2 * a + 2)
                        dve.tensor_tensor(c_rv[s][:, half], c_r[s][:, half], B(s, a)[:].rearrange("p (t d) -> p t d", t=2), ALU.mult).then_inc(c_dve.mark(f"rv{s}{a}"), 1)


def kernel(**inputs):
    import concourse.bacc as bacc
    from concourse.bass_utils import run_bass_kernel_spmd

    def a(name):
        return np.asarray(inputs[name])

    def turned(name):
        return np.ascontiguousarray(a(name).T)

    def row(name):
        return np.ascontiguousarray(a(name).reshape(1, -1))

    part = np.arange(P)
    ident = np.eye(P, dtype=np.float32)
    blocks = (part[:, None] // HD == part[None, :] // HD).astype(np.float32) / HD
    parity = np.zeros((P, 7), np.float32)
    for j in range(4):
        parity[:, j] = part // HD % 4 == j
    parity[:, 4] = part // HD % 2 == 0
    parity[:, 5] = part // HD % 2 == 1
    parity[:, 6] = EPS
    q, key = part[:, None] % QF, np.arange(KEYS)[None, :]
    local = (key <= q + WINDOW) & (key > q) & (key < WINDOW + QF)
    glob = key >= WINDOW + QF
    seen = [local & (key >= WINDOW), (local & (key >= QF)) | ((key >= QF) & (key < QF + NGLOB)),
            local | (key < NGLOB), local | glob]
    mask = np.stack([np.tile(np.where(m, 0.0, MASKED), (1, KT)) for m in seen], axis=1).astype(mybir.dt.np(BF16))

    arrays = {
        "x": a("L0_attn_hidden_states"),
        "w_in": np.concatenate([turned(f"L0_attn_{n}") for n in ("Wq", "Wk", "Wv", "Wg", "Wlr")], axis=1),
        "taps": np.concatenate([a(f"L0_attn_{n}") for n in ("cq", "ck", "cv")], axis=1),
        "w_out": turned("L0_attn_Wo"),
        "ln_g": np.tile(a("L0_attn_ln_g"), P // HD).reshape(P, 1),
        "ln_b": np.tile(a("L0_attn_ln_b"), P // HD).reshape(P, 1),
        "w_in_init": a("L0_attn_W_in_init")[0],
        "w_out_init": a("L0_attn_W_out_init")[0],
        "u1": a("L0_ffn_U1"), "v1": a("L0_ffn_V1"), "b1": row("L0_ffn_b1"),
        "u2": a("L0_ffn_U2"), "v2": a("L0_ffn_V2"), "b2": row("L0_ffn_b2"),
        "cond": np.stack([turned("L0_c"), turned("L1_c")]),
        "wmod": np.stack([a("L0_wmod"), a("L1_wmod")]),
        "w_attn": turned("L1_attn_w_attn"), "w_proj": turned("L1_attn_w_proj"),
        "w_r": turned("L1_ffn_W_r"), "w_k": turned("L1_ffn_W_k"), "w_v": turned("L1_ffn_W_v"),
        "mu": np.stack([a("L1_ffn_mu_r").reshape(KT, P).T, a("L1_ffn_mu_k").reshape(KT, P).T], axis=1),
        "ident_c": ident, "blocks_c": blocks, "parity_c": parity, "mask_c": mask,
    }
    arrays = {n: np.ascontiguousarray(v) for n, v in arrays.items()}
    nc = bacc.Bacc("TRN2", target_bir_lowering=False, num_devices=1)
    args = [nc.dram_tensor(n, v.shape, mybir.dt.from_np(v.dtype), kind="ExternalInput").ap() for n, v in arrays.items()]
    args.append(nc.dram_tensor("out", (BATCH, TOK, DIM), F32, kind="ExternalOutput").ap())
    adaln_two_layers(nc, *args)
    r = run_bass_kernel_spmd(nc, [arrays], core_ids=[0])
    return r.results[0]["out"]
```

```python
from contextlib import ExitStack

import numpy as np
import concourse.bass as bass
from concourse import mybir

P = 128
BATCH, TOK, DIM = 16, 512, 256
HEADS, HD = 16, 16
KT = DIM // P
TT = TOK // P
INNER, CHUNK, TAPS = 4, 16, 4
D_FF, RANK = 1024, 64
FT = D_FF // P
WINDOW, NGLOB = 64, 4
GROUP_B = P // HEADS
GROUPS = BATCH // GROUP_B
BLOCK = 64
BLOCKS = TOK // BLOCK
CPB = BLOCK // CHUNK
CPR = 2 * CPB
ROUNDS = TOK // (CPR * CHUNK)
QF = 32
FRAMES = TOK // QF
HF, QTR = FRAMES // 2, FRAMES // 4
KEYS = WINDOW + QF + NGLOB
QUADS = HEADS // 4
ROWS = INNER * CHUNK
PROD = ROWS * HD
BASE_LR = 0.001
EPS = 1e-5
MASKED = -3.0e38
N_MOD = 6
LAYERS = 2
AHEAD = 2
ARENA = 36816

ALU = mybir.AluOpType
ACT = mybir.ActivationFunctionType
AX = mybir.AxisListType
F32 = mybir.dt.float32
BF16 = mybir.dt.bfloat16


class Steps:

    def __init__(self, sem, names):
        self.sem, self.names, self.marked = sem, list(names), 0
        self.index = {name: k for k, name in enumerate(self.names)}
        assert len(self.index) == len(self.names)

    def mark(self, name):
        assert self.names[self.marked % len(self.names)] == name, (self.names[self.marked % len(self.names)], name)
        self.marked += 1
        return self.sem

    def at(self, n, name):
        return (n + 1) * len(self.names) + self.index[name] + 1

    def before(self, n, name):
        return n * len(self.names) + self.index[name] + 1


QKV = ["q0", "q1", "k0", "k1", "v0", "v1"]


def adaln_two_layers(nc, x, w_in, taps, w_out, ln_g, ln_b, w_in_init, w_out_init, u1, v1, b1, u2, v2, b2,
                     cond, wmod, w_attn, w_proj, w_r, w_k, w_v, mu, ident_c, blocks_c, parity_c, mask_c, out):
    ctx = ExitStack()
    with ctx:
        def sb(name, shape, dt=F32):
            return ctx.enter_context(nc.sbuf_tensor(name, shape, dt))

        def sem(name):
            return ctx.enter_context(nc.semaphore(name))

        psum = ctx.enter_context(nc.psum_tensor("psum", [P, 8, 512], F32))
        bank = [psum[:, i] for i in range(8)]

        def dram(name, shape):
            return nc.dram_tensor(name, shape, F32, kind="Internal").ap()

        qkv_d = [dram(f"{c}_d", [BLOCKS, BATCH, DIM, BLOCK]) for c in "qkv"]
        gate_d = dram("gate_d", [BATCH + AHEAD, DIM, TOK])
        lr_d = dram("lr_d", [BATCH, 2 * HEADS, TOK])
        o_d = dram("o_d", [BATCH + AHEAD, DIM, TOK])

        w_in_sb = sb("w_in_sb", [P, KT, 4 * DIM + 2 * HEADS])
        taps_sb = sb("taps_sb", [P, KT, 3 * TAPS])
        w_out_sb = sb("w_out_sb", [P, KT, DIM])
        lngb_sb = sb("lngb_sb", [P, 2])
        u1_sb = sb("u1_sb", [P, KT, RANK])
        v1_sb = sb("v1_sb", [RANK + 1, D_FF])
        u2_sb = sb("u2_sb", [P, FT, RANK])
        v2_sb = sb("v2_sb", [RANK + 1, DIM])
        w_attn_sb = sb("w_attn_sb", [P, KT, 3 * DIM])
        w_proj_sb = sb("w_proj_sb", [P, KT, DIM])
        w_rkv_sb = sb("w_rkv_sb", [P, 3, KT, DIM])
        mu_sb = sb("mu_sb", [P, 2, KT])
        ident = sb("ident", [P, P])
        identb = sb("identb", [P, P], BF16)
        mean16 = sb("mean16", [P, P])
        parity = sb("parity", [P, 7])
        mask_sb = sb("mask_sb", [P, 4, KT * KEYS], BF16)
        state0 = sb("state0", [P, 2, ROWS])
        modc = sb("modc", [P, LAYERS * N_MOD * KT, BATCH])
        gates_row = sb("gates_row", [BATCH, 2 * LAYERS * DIM])

        arena = sb("arena", [P, ARENA])
        top = [0]

        def carve(*shape):
            size = int(np.prod(shape))
            ap = arena[:, top[0]:top[0] + size]
            top[0] += size
            assert top[0] <= ARENA, top[0]
            if len(shape) == 2:
                ap = ap.rearrange("p (a b) -> p a b", a=shape[0])
            if len(shape) == 3:
                ap = ap.rearrange("p (a b c) -> p a b c", a=shape[0], b=shape[1])
            return ap


        wmod_sb = carve(LAYERS, KT, N_MOD * DIM)
        cond_sb = carve(LAYERS, KT, BATCH)
        cond_silu = carve(LAYERS, KT, BATCH)
        g_raw = carve(2 * LAYERS * DIM)
        g_sign = carve(2 * LAYERS * DIM)
        g_size = carve(2 * LAYERS * DIM)

        top[0] = 0
        a_x = carve(TT, DIM)
        a_xhat = carve(TT, DIM)
        a_stat = carve(TT, 6)
        a_mv = carve(TT, 2)
        a_std = carve(TT)
        a_rstd = carve(TT)
        a_modb = carve(2 * KT)
        a_h = carve(KT, TOK)
        a_acc = carve(6, TOK)
        a_gate = carve(KT, TOK)
        a_lr = carve(TOK)
        a_sq = carve(2 * KT, TOK)
        a_rn = carve(2 * KT, TOK)

        top[0] = 0
        PAIRS = range(GROUPS)

        def of_group(*shape):
            return [carve(*shape) for _ in PAIRS]

        scan_keep = carve(PROD)
        lr_fin = carve(GROUPS * 2, CHUNK + TOK)
        q_blk, k_blk, v_blk, o_blk = ([of_group(HD, BLOCK) for _ in range(2)] for _ in range(4))
        t_mul = of_group(2 * PROD)
        t_run, t_g1, t_g2, t_q = (of_group(PROD) for _ in range(4))
        t_q8 = of_group(PROD // 2)
        win, win1, wout2, wout, s_a, s_2, g_1, g_2 = (of_group(ROWS) for _ in range(8))
        e_k, e_p, p_out1, k_hat, e_q, q_hat, e_2, p_2 = (of_group(ROWS) for _ in range(8))
        e_b, p_in = of_group(2 * ROWS), of_group(2 * ROWS)
        m_k, z_k, r_k, rl_k, m_q, z_q, r_q = (of_group(CHUNK) for _ in range(7))
        m_p, z_p, r_p, m_2, z_2, r_2 = (of_group(INNER) for _ in range(6))
        m_b, z_b, r_b = (of_group(2 * INNER) for _ in range(3))
        lr_raw, lr_tmp = (t.rearrange("p (i t) -> p i t", i=2 * GROUPS) for t in t_mul)

        top[0] = 0
        SLOTS = range(2)
        c_x = [carve(TT, DIM) for _ in SLOTS]
        c_xy = [carve(TT * DIM) for _ in SLOTS]
        c_xhat = [t.rearrange("p (a b) -> p a b", a=TT) for t in c_xy]
        c_y = [t.rearrange("p (t k q) -> p t k q", t=TT, k=KT) for t in c_xy]
        c_stat = [carve(TT, 6) for _ in SLOTS]
        c_mv = [carve(TT, 2) for _ in SLOTS]
        c_std = [carve(TT) for _ in SLOTS]
        c_rstd = [carve(TT) for _ in SLOTS]
        c_modb = [carve(3, 2 * KT) for _ in SLOTS]
        c_pick = [carve(P) for _ in SLOTS]
        c_h = [carve(KT, TOK + 1) for _ in SLOTS]
        c_vt = c_xhat
        c_wo = [carve(KT, DIM) for _ in SLOTS]
        c_wp = [carve(KT, DIM) for _ in SLOTS]
        c_wv = [carve(KT, DIM) for _ in SLOTS]
        c_v2 = [carve(DIM) for _ in SLOTS]
        c_soft = [carve(2, 4, KEYS) for _ in SLOTS]
        c_max, c_sum, c_rec = ([carve(4) for _ in SLOTS] for _ in range(3))
        c_pt = [carve(4 * P) for _ in SLOTS]
        c_yeven = [carve(KT * QTR, QF) for _ in SLOTS]
        base = top[0]
        c_pq = [carve(2, TOK) for _ in SLOTS]
        c_p, c_qr = [t[:, 0] for t in c_pq], [t[:, 1] for t in c_pq]
        c_one = [t[RANK:RANK + 1] for t in c_pq]
        c_f = [carve(3, TOK) for _ in SLOTS]
        top[0] = base
        c_qb = [carve(KT, FRAMES, 4 * QF) for _ in SLOTS]
        keys_at = top[0]
        c_k = [carve(KT, FRAMES, KEYS) for _ in SLOTS]
        c_v = [carve(FRAMES, DIM) for _ in SLOTS]
        top[0] = base
        c_d = [carve(KT, TOK) for _ in SLOTS]
        c_xr = [carve(KT, TOK) for _ in SLOTS]
        c_xk = [carve(KT, TOK) for _ in SLOTS]
        c_r = [carve(TT, DIM) for _ in SLOTS]
        c_kk = [carve(KT, TOK) for _ in SLOTS]
        c_rv = [carve(TT, DIM) for _ in SLOTS]

        top[0] = keys_at
        c_o, c_gate, c_ostd = ([carve(KT, TOK) for _ in SLOTS] for _ in range(3))
        c_oz = [w_in_sb[:, s, 0:KT * TOK].rearrange("p (k t) -> p k t", k=KT) for s in SLOTS]

        held = sem("held")

        def hold(eng):
            eng.sem_inc(held, 1)

        cond_loaded, wmod_loaded = sem("cond_loaded"), sem("wmod_loaded")
        consts_loaded = sem("consts_loaded")
        weights_loaded = sem("weights_loaded")
        su_act = Steps(sem("su_act"), ["silu", "modc", "raw0", "raw1"])
        su_pe = Steps(sem("su_pe"), ["mod", "gate0", "gate1"])
        su_dve = Steps(sem("su_dve"), ["identb", "plus1", "plus2", "plus3", "plus4", "tap", "side", "sign", "size", "gates"])

        x_loaded = sem("x_loaded")
        a_stored = {t: sem(f"stored_{t}") for t in QKV + ["g0", "g1", "lr"]}
        ln_dve = Steps(sem("ln_dve"), [f"st{t}" for t in range(TT)] + [f"ag{t}" for t in range(TT)] + ["rec"]
                       + [f"xh{t}" for t in range(TT)])
        ln_act = Steps(sem("ln_act"), ["modb", "std", "h0", "h1"])
        ln_pe = Steps(sem("ln_pe"), ["t0", "t1"])
        pr_pe = Steps(sem("pr_pe"), QKV + ["g0", "g1", "lr"] + [f"ss{t}" for t in range(4)])
        pr_pool = Steps(sem("pr_pool"), [f"sq{t}" for t in range(4)] + [f"unit{t}" for t in range(4)])
        pr_act = Steps(sem("pr_act"), ["tap0", "tap1", "tap2", "silu0", "tap3", "silu1", "tap4", "silu2", "tap5",
                                       "silu3", "g0", "silu4", "g1", "silu5", "lr"]
                       + [f"ln{t}" for t in range(4)] + [f"rn{t}" for t in range(4)])
        pr_dve = Steps(sem("pr_dve"), [f"c{t}{j}" for t in range(6) for j in (1, 2, 3)])

        blk_loaded = [[sem(f"blk_loaded{b}{g}") for g in PAIRS] for b in range(2)]
        o_stored = [[sem(f"o_stored{b}{g}") for g in PAIRS] for b in range(2)]
        lr_loaded = sem("lr_loaded")
        scan_ready = Steps(sem("scan_ready"), ["ones", "zeros"])
        st_dve = Steps(sem("st_dve"), ["pad", "lr"] + [f"{n}{g}" for g in PAIRS for n in ("no_v", "no_s2", "in", "out")])
        st_act = Steps(sem("st_act"), ["abs", "exp", "ln"])
        re_dve = [Steps(sem(f"re_dve{g}"), [
            "a0_mul", "max2", "a0", "sub2", "pmax", "kmax", "psub", "ksub", "sum2", "psum", "ksum",
            "rec2", "prec", "krec", "p2", "klr", "p1", "kh",
            "g2s", "wout", "g1s", "carry", "run", "wout2", "b1_mul", "b2_mul",
            "bmax", "bsub", "bsum", "brec", "pin", "d_mul", "qmax", "qsub",
            "qsum", "win1", "qrec", "a1_mul", "qh", "win", "a1"]) for g in PAIRS]
        re_pool = [Steps(sem(f"re_pool{g}"), ["g2", "g1", "kv", "sq_mul", "o_mul", "o2", "o1"]) for g in PAIRS]
        re_act = [Steps(sem(f"re_act{g}"), ["e2", "ep", "ek", "eb", "eq"]) for g in PAIRS]
        re_pe = [Steps(sem(f"re_pe{g}"), ["b", "sq", "d"]) for g in PAIRS]
        PHASES = 3 * CPR + 1

        def staggered(program):
            programs = [program(g) for g in PAIRS]
            for t in range(PHASES + GROUPS - 1):
                for g in PAIRS:
                    if 0 <= t - g < PHASES:
                        next(programs[g])

        c_ready = sem("c_ready")
        c_loaded = [sem(f"c_loaded{s}") for s in SLOTS]
        o_loaded = [sem(f"o_loaded{s}") for s in SLOTS]
        ahead_filled = sem("ahead_filled")
        out_stored = [sem(f"out_stored{s}") for s in SLOTS]
        FRAMED = 3 * TT + 1
        v_framed = [sem(f"v_framed{s}") for s in SLOTS]
        ATT = [(f, s) for f in range(FRAMES) for s in SLOTS]

        T_LAG, PV_LAG, YE_LAG, Y_LAG = 3, 4, 5, 6
        WARM = {"s0": 9, "t0": 6, "t1": 4, "pv0": 4, "t2": 2, "pv1": 2}
        TURNED, Y_BANKS = 2, (3, 6, 7)

        def y_bank(s, quarter):
            return bank[Y_BANKS[(len(SLOTS) * quarter + s) % len(Y_BANKS)]]

        def ends_quarter(f):
            return f % QTR == QTR - 1

        ln_names = lambda i, s: [f"st{i}{s}{t}" for t in range(TT)] + [f"ag{i}{s}{t}" for t in range(TT)]
        xh_names = lambda i, s: [f"rec{i}{s}"] + [f"xh{i}{s}{t}" for t in range(TT)]

        def norm_dve(i):
            return ([f"x{i}00", f"x{i}01"] + ln_names(i, 0) + [f"x{i}10", f"x{i}11"] + xh_names(i, 0)
                    + ln_names(i, 1) + xh_names(i, 1))

        def norm_act(i):
            return [f"std{i}0", f"h{i}00", f"std{i}1", f"h{i}01"] + [f"h{i}1{k}" for k in range(KT)]

        def each(*fs):
            return [n for s in SLOTS for f in fs for n in f(s)]

        def att_pe():
            names = []
            for t in range(len(ATT) + PV_LAG):
                names += [f"{what}{s}{f}" for what, lag in (("s", 0), ("t", T_LAG), ("pv", PV_LAG)) if 0 <= t - lag < len(ATT)
                          for f, s in [ATT[t - lag]]]
            return names

        def att_act():
            names = []
            for t in range(len(ATT) + YE_LAG + 1):
                if t < len(ATT):
                    names += [f"exp{ATT[t][1]}{ATT[t][0]}u{u}" for u in range(QUADS)]
                if 0 <= t - T_LAG < len(ATT):
                    names.append(f"pt{ATT[t - T_LAG][1]}{ATT[t - T_LAG][0]}")
                if 0 <= t - YE_LAG < len(ATT) and ends_quarter(ATT[t - YE_LAG][0]):
                    names.append(f"ye{ATT[t - YE_LAG][1]}{ATT[t - YE_LAG][0] // QTR}")
            return names

        def att_dve():
            names = []
            for t in range(len(ATT) + Y_LAG + 1):
                for what, lag in (("max", 0), ("sum", 1), ("arec", 1)):
                    if 0 <= t - lag < len(ATT):
                        names.append(f"{what}{ATT[t - lag][1]}{ATT[t - lag][0]}")
                if 0 <= t - Y_LAG < len(ATT) and ends_quarter(ATT[t - Y_LAG][0]):
                    names.append(f"y{ATT[t - Y_LAG][1]}{ATT[t - Y_LAG][0] // QTR}")
            return names

        out_dve = [f"{what}{s}{k}" for what in ("oc", "ov") for s in SLOTS for k in range(KT)], [f"{what}{s}" for s in SLOTS for what in ("on", "oz")]
        out_act = [f"oln{s}" for s in SLOTS], [f"orstd{s}" for s in SLOTS]
        first_dve = Steps(sem("first_dve"), out_dve[0] + out_dve[1] + each(lambda s: [f"pick{s}"]))
        first_act = Steps(sem("first_act"), out_act[0] + out_act[1])
        first_pe = Steps(sem("first_pe"), [f"{what}{s}{k}" for what in ("mean", "var") for s in SLOTS for k in range(KT)])
        first_pool = Steps(sem("first_pool"), [f"osq{s}" for s in SLOTS])
        c_dve = Steps(sem("c_dve"),
            each(lambda s: [f"modb{s}"]) + each(lambda s: [f"wo{s}"]) + each(lambda s: [f"v2{s}", f"wp{s}", f"wv{s}"])
            + norm_dve(1) + out_dve[0] + norm_dve(2) + out_dve[1]
            + each(lambda s: [f"vt{s}1"]) + each(lambda s: [f"qb{s}1{j}" for j in range(4)])
            + each(lambda s: [f"ks{s}{g}" for g in range(4)]) + att_dve()
            + norm_dve(3) + ["d0"] + each(lambda s: [f"{m}{s}{k}" for m in ("xr", "xk") for k in range(KT)])
            + each(lambda s: [f"pick{s}"]) + each(lambda s: [f"rv{s}0", f"rv{s}1"]))
        c_act = Steps(sem("c_act"),
            norm_act(1)
            + each(lambda s: [f"p{s}"]) + [f"gelu{s}{f}" for f in range(FT) for s in SLOTS]
            + out_act[0] + each(lambda s: [f"qr{s}"]) + out_act[1] + norm_act(2)
            + each(lambda s: [f"vt{s}0"]) + each(lambda s: [f"qb{s}0{j}" for j in range(4)])
            + each(lambda s: [f"ks{s}{g}" for g in range(4)]) + att_act()
            + norm_act(3)
            + each(lambda s: [f"r{s}0", f"r{s}1", f"kk{s}0", f"kk{s}1"]))

        UP_BANKS = 2
        OUT_AT = {(0, 1): ("mean", 0), (2, 1): ("mean", 1), (4, 1): ("var", 0), (6, 1): ("var", 1)}

        def ffn_pe():
            names = [f"v1{s}{f}" for s in SLOTS for f in range(UP_BANKS)]
            for f in range(FT):
                for s in SLOTS:
                    names.append(f"u2{s}{f}")
                    if f + UP_BANKS < FT:
                        names.append(f"v1{s}{f + UP_BANKS}")
                    names += [f"{what}{r}{k}" for k in range(KT) for what, r in [OUT_AT.get((f, s), ("", 0))] if what]
            return names

        c_pe = Steps(sem("c_pe"),
            each(lambda s: [f"gb{s}0", f"gb{s}1"]) + each(lambda s: [f"wo{s}0", f"wo{s}1"])
            + each(lambda s: [f"turn1{s}0", f"turn1{s}1", f"u1{s}"]) + ffn_pe()
            + each(lambda s: [f"v2{s}0", f"v2{s}1"])
            + each(lambda s: [f"turn2{s}0", f"turn2{s}1", f"vt{s}0", f"vt{s}1"]) + each(lambda s: [f"q{s}0", f"q{s}1"])
            + each(lambda s: [f"k{s}0", f"k{s}1"]) + att_pe()
            + each(lambda s: [f"wp{s}0", f"wp{s}1"]) + each(lambda s: [f"turn3{s}0", f"turn3{s}1"])
            + each(lambda s: [f"r{s}0", f"r{s}1", f"kk{s}0", f"kk{s}1"]) + each(lambda s: [f"vv{s}0", f"vv{s}1"]))
        c_pool = Steps(sem("c_pool"),
            each(lambda s: [f"one{s}"]) + [f"osq{s}" for s in SLOTS] + each(lambda s: [f"pad{s}{j}" for j in range(4)])
            + [f"prob{s}{f}" for f, s in ATT]
            + ["d1"] + each(lambda s: [f"kk{s}0", f"kk{s}1"]) + each(lambda s: [f"x4{s}0", f"x4{s}1"]))

        block = ctx.enter_context(nc.Block())

        def phase_a_done(eng):
            eng.wait_ge(pr_act.sem, pr_act.before(BATCH, "rn3"))
            eng.wait_ge(pr_dve.sem, pr_dve.before(BATCH, "c53"))
            eng.wait_ge(pr_pe.sem, pr_pe.before(BATCH, "ss3"))
            eng.wait_ge(pr_pool.sem, pr_pool.before(BATCH, "unit3"))
            for s in a_stored.values():
                eng.wait_ge(s, 16 * BATCH)

        CHUNKS = ROUNDS * CPR

        def recurrence_done(eng):
            for g in PAIRS:
                eng.wait_ge(re_dve[g].sem, re_dve[g].before(CHUNKS, "a1"))
                eng.wait_ge(re_pool[g].sem, re_pool[g].before(CHUNKS, "o1"))
                eng.wait_ge(re_act[g].sem, re_act[g].before(CHUNKS, "eq"))
                eng.wait_ge(re_pe[g].sem, re_pe[g].before(CHUNKS, "d"))
                for b in range(2):
                    eng.wait_ge(o_stored[b][g], 16 * ROUNDS)

        @block.sync
        def _(sp):
            sp.dma_start(cond_sb, cond.rearrange("l (k p) b -> p l k b", p=P)).then_inc(cond_loaded, 16)
            for layer in range(LAYERS):
                sp.dma_start(wmod_sb[:, layer], wmod[layer].rearrange("(k p) n -> p k n", p=P)).then_inc(wmod_loaded, 16)
            for dst, src in ((ident[:], ident_c), (mean16[:], blocks_c), (parity[:], parity_c)):
                sp.dma_start(dst, src).then_inc(consts_loaded, 16)
            for dst, src in (
                (w_in_sb[:], w_in.rearrange("(k p) n -> p k n", p=P)),
                (taps_sb[:], taps.rearrange("(k p) n -> p k n", p=P)),
                (w_out_sb[:], w_out.rearrange("(k p) n -> p k n", p=P)),
                (lngb_sb[:, 0:1], ln_g),
                (lngb_sb[:, 1:2], ln_b),
                (u1_sb[:], u1.rearrange("(k p) n -> p k n", p=P)),
                (v1_sb[0:RANK], v1),
                (v1_sb[RANK:RANK + 1], b1),
                (u2_sb[:], u2.rearrange("(k p) n -> p k n", p=P)),
                (v2_sb[0:RANK], v2),
                (v2_sb[RANK:RANK + 1], b2),
                (w_attn_sb[:], w_attn.rearrange("(k p) n -> p k n", p=P)),
                (w_proj_sb[:], w_proj.rearrange("(k p) n -> p k n", p=P)),
                (w_rkv_sb[:, 0], w_r.rearrange("(k p) n -> p k n", p=P)),
                (w_rkv_sb[:, 1], w_k.rearrange("(k p) n -> p k n", p=P)),
                (w_rkv_sb[:, 2], w_v.rearrange("(k p) n -> p k n", p=P)),
                (mu_sb[:], mu),
                (mask_sb[:], mask_c),
            ):
                sp.dma_start(dst, src).then_inc(weights_loaded, 16)
            for past in (o_d, gate_d):
                sp.dma_start(past[BATCH:BATCH + AHEAD].rearrange("b d t -> (b d) t"), x[0:AHEAD].rearrange("b (u v) d -> (b u) (v d)", v=TOK // DIM)).then_inc(ahead_filled, 16)
            for g in range(GROUP_B):
                rows = slice(g * HEADS, (g + 1) * HEADS)
                for i, init in enumerate((w_in_init, w_out_init)):
                    sp.dma_start(state0[rows, i].rearrange("p (a d) -> p a d", a=INNER),
                                 init.rearrange("a h d -> h a d")).then_inc(weights_loaded, 16)

            sp.wait_ge(su_pe.sem, su_pe.before(1, "gate1"))
            sp.wait_ge(su_dve.sem, su_dve.before(1, "gates"))

            def load_x(n):
                sp.dma_start(a_x, x[bass.ds(n, 1)].rearrange("o (t p) d -> p (o t) d", p=P)).then_inc(x_loaded, 16)

            def stores(n):
                for t, name in ((4, "v0"), (5, "v1"), (0, "q0"), (1, "q1"), (2, "k0"), (3, "k1")):
                    if t < 4:
                        sp.wait_ge(pr_pool.sem, pr_pool.at(n, f"unit{t}"))
                    else:
                        sp.wait_ge(pr_act.sem, pr_act.at(n, f"silu{t}"))
                    dst = qkv_d[t // KT][:, bass.ds(n, 1), (t % KT) * P:(t % KT + 1) * P].rearrange("b o c t -> (o c) b t")
                    sp.dma_start(dst, a_acc[:, t].rearrange("p (b t) -> p b t", b=BLOCKS)).then_inc(a_stored[name], 16)
                for k in range(KT):
                    sp.wait_ge(pr_act.sem, pr_act.at(n, f"g{k}"))
                    dst = gate_d[bass.ds(n, 1)].rearrange("o c t -> (o c) t")[k * P:(k + 1) * P]
                    sp.dma_start(dst, a_gate[:, k]).then_inc(a_stored[f"g{k}"], 16)
                sp.wait_ge(pr_act.sem, pr_act.at(n, "lr"))
                sp.dma_start(lr_d[bass.ds(n, 1)].rearrange("o c t -> (o c) t"), a_lr[0:2 * HEADS]).then_inc(a_stored["lr"], 16)

            def next_x(n):
                sp.wait_ge(ln_dve.sem, ln_dve.before(n, "xh3"))
                hold(sp)
                load_x(n)

            load_x(0)
            next_x(1)
            with sp.Fori(0, BATCH - 2) as n:
                next_x(n + 2)
                stores(n)
            stores(BATCH - 2)
            stores(BATCH - 1)

            phase_a_done(sp)
            for g in PAIRS:
                sp.dma_start(lr_raw[:, 2 * g:2 * g + 2], lr_d[g * GROUP_B:(g + 1) * GROUP_B].rearrange("b (h i) t -> (b h) i t", i=2)).then_inc(lr_loaded, 16)
            pair = lambda d: d.rearrange("b (h d) t -> (b h) d t", h=HEADS)

            def load_block(n, b):
                for g in PAIRS:
                    for dst, src in ((q_blk, qkv_d[0]), (k_blk, qkv_d[1]), (v_blk, qkv_d[2])):
                        rows = src[bass.ds(n * 2 + b, 1), g * GROUP_B:(g + 1) * GROUP_B].rearrange("o b (h d) t -> (o b h) d t", h=HEADS)
                        sp.dma_start(dst[b][g], rows).then_inc(blk_loaded[b][g], 16)

            def store_block(n, b):
                for g in PAIRS:
                    sp.wait_ge(re_pool[g].sem, re_pool[g].at(n * CPR + b * CPB + CPB - 1, "o1"))
                    sp.dma_start(pair(o_d)[g * P:(g + 1) * P, :, bass.ds((n * 2 + b) * BLOCK, BLOCK)], o_blk[b][g]).then_inc(o_stored[b][g], 16)

            def block_used(n, b):
                for g in PAIRS:
                    sp.wait_ge(re_pool[g].sem, re_pool[g].at(n * CPR + b * CPB + CPB, "g2"))
                    hold(sp)

            load_block(0, 0)
            with sp.Fori(0, ROUNDS - 1) as n:
                block_used(n - 1, 1)
                load_block(n, 1)
                store_block(n, 0)
                block_used(n, 0)
                load_block(n + 1, 0)
                store_block(n, 1)
            block_used(ROUNDS - 2, 1)
            load_block(ROUNDS - 1, 1)
            store_block(ROUNDS - 1, 0)
            store_block(ROUNDS - 1, 1)

            sp.wait_ge(c_ready, len(SLOTS))

            def load_outputs(s, b):
                for dst, src in ((c_o[s], o_d), (c_gate[s], gate_d)):
                    sp.dma_start(dst, src[bass.ds(b, 1)].rearrange("o (k p) t -> p (o k) t", p=P)).then_inc(o_loaded[s], 16)

            for s in SLOTS:
                load_outputs(s, s)
            sp.wait_ge(ahead_filled, 32)
            for s in SLOTS:
                sp.wait_ge(first_dve.sem, first_dve.at(0, f"oz{s}"))
            with sp.Fori(0, BATCH // 2) as i:
                for s in SLOTS:
                    b = i * 2 + s
                    sp.wait_ge(out_stored[s], 32 * i)
                    sp.dma_start(c_x[s], x[bass.ds(b, 1)].rearrange("o (t p) d -> p (o t) d", p=P)).then_inc(c_loaded[s], 16)
                    sp.wait_ge(c_pool.sem, c_pool.before(i, "x411"))
                    hold(sp)
                    load_outputs(s, b + AHEAD)
                for s in SLOTS:
                    sp.wait_ge(c_act.sem, c_act.at(i, f"vt{s}0"))
                    hold(sp)
                    sp.wait_ge(c_dve.sem, c_dve.at(i, f"vt{s}1"))
                    hold(sp)
                    for back in range(3):
                        for j in range(TT):
                            first = j + back
                            frames = range(first, FRAMES, TT)
                            rows = slice(WINDOW - back * QF, WINDOW - back * QF + QF)
                            sp.dma_start(c_v[s][rows, first:FRAMES:TT], c_vt[s][j * QF:(j + 1) * QF, 0:len(frames)]).then_inc(v_framed[s], 16)
                    sp.dma_start(c_v[s][WINDOW + QF:KEYS], c_vt[s][0:NGLOB, 0:1].broadcast_to([NGLOB, FRAMES, DIM])).then_inc(v_framed[s], 16)
                for s in SLOTS:
                    b = i * 2 + s
                    for a in range(2):
                        sp.wait_ge(c_pool.sem, c_pool.at(i, f"x4{s}{a}"))
                        hold(sp)
                        sp.dma_start(out[bass.ds(b, 1)].rearrange("o (t p) d -> p (o t) d", p=P)[:, 2 * a:2 * a + 2],
                                     c_x[s][:, 2 * a:2 * a + 2]).then_inc(out_stored[s], 16)
            for s in SLOTS:
                sp.wait_ge(out_stored[s], 32 * (BATCH // 2))

        @block.tensor
        def _(pe):
            for st in (su_pe, ln_pe, pr_pe, *re_pe, first_pe, c_pe):
                pe.sem_inc(st.sem, len(st.names))
            pe.wait_ge(wmod_loaded, 16 * LAYERS)
            pe.wait_ge(su_act.sem, su_act.at(0, "silu"))
            for layer in range(LAYERS):
                for m in range(N_MOD * KT):
                    col = (layer * N_MOD * KT + m) * BATCH
                    for k in range(KT):
                        mm = pe.matmul(bank[0][:, col:col + BATCH], wmod_sb[:, layer, k, m * P:(m + 1) * P],
                                       cond_silu[:, layer, k], start=(k == 0), stop=(k == KT - 1))
            mm.then_inc(su_pe.mark("mod"), 1)
            for layer in range(LAYERS):
                for j, which in enumerate((2, 5)):
                    for k in range(KT):
                        mm = pe.matmul(bank[1 + layer][0:BATCH, j * DIM:(j + 1) * DIM], cond_silu[:, layer, k],
                                       wmod_sb[:, layer, k, which * DIM:(which + 1) * DIM],
                                       start=(k == 0), stop=(k == KT - 1))
                mm.then_inc(su_pe.mark(f"gate{layer}"), 1)

            def turn(m):
                pe.wait_ge(ln_dve.sem, ln_dve.at(m, "xh3"))
                pe.wait_ge(ln_act.sem, ln_act.before(m, "h1"))
                for k in range(KT):
                    for t in range(TT):
                        mm = pe.transpose(bank[k][:, t * P:(t + 1) * P], a_xhat[:, t, k * P:(k + 1) * P], ident[:])
                    mm.then_inc(ln_pe.mark(f"t{k}"), 1)

            def project(n):
                pe.wait_ge(ln_act.sem, ln_act.at(n, "h1"))
                for j, name in enumerate(QKV + ["g0", "g1", "lr"]):
                    if name == "g0":
                        pe.wait_ge(pr_dve.sem, pr_dve.at(n, "c03"))
                    elif name == "g1":
                        pe.wait_ge(pr_dve.sem, pr_dve.at(n, "c13"))
                    elif name == "lr":
                        pe.wait_ge(pr_dve.sem, pr_dve.at(n, "c23"))
                    elif name == "q0":
                        pe.wait_ge(pr_act.sem, pr_act.before(n, "g0"))
                    elif name == "q1":
                        pe.wait_ge(pr_act.sem, pr_act.before(n, "g1"))
                    else:
                        pe.wait_ge(pr_act.sem, pr_act.before(n, f"ln{j - 2}"))
                    rows = 2 * HEADS if name == "lr" else P
                    for k in range(KT):
                        mm = pe.matmul(bank[2 + j % 6][0:rows], w_in_sb[:, k, j * P:j * P + rows], a_h[:, k],
                                       start=(k == 0), stop=(k == KT - 1))
                    mm.then_inc(pr_pe.mark(name), 1)

            def lengths(n):
                for t in range(4):
                    pe.wait_ge(pr_pool.sem, pr_pool.at(n, f"sq{t}"))
                    if t == 0:
                        pe.wait_ge(pr_act.sem, pr_act.at(n, "lr"))
                    else:
                        pe.wait_ge(pr_dve.sem, pr_dve.at(n, f"c{t + 2}3"))
                    pe.matmul(bank[4 + t][:], mean16[:], a_sq[:, t], start=True, stop=True).then_inc(pr_pe.mark(f"ss{t}"), 1)

            pe.wait_ge(consts_loaded, 48)
            pe.wait_ge(weights_loaded, 16 * (18 + 2 * GROUP_B))
            pe.wait_ge(su_act.sem, su_act.at(0, "modc"))
            turn(0)
            pe.wait_ge(su_act.sem, su_act.at(0, "raw1"))
            with pe.Fori(0, BATCH - 1) as n:
                project(n)
                turn(n + 1)
                lengths(n)
            project(BATCH - 1)
            lengths(BATCH - 1)

            phase_a_done(pe)

            def add_up(dst, products):
                terms = products.rearrange("p (j x) -> p j x", j=16)
                for j in range(16):
                    mm = pe.matmul(dst, ident[:], terms[:, j], start=(j == 0), stop=(j == 15))
                return mm

            with pe.Fori(0, ROUNDS) as n:
                def sums(g):
                    dve, pool, mine = re_dve[g], re_pool[g], re_pe[g]
                    scores, d_in, queries = (bank[4 * g + b] for b in range(3))
                    for j in range(CPR):
                        c = n * CPR + j
                        yield
                        pe.wait_ge(dve.sem, dve.at(c, "b2_mul"))
                        add_up(scores[:, 0:2 * ROWS], t_mul[g]).then_inc(mine.mark("b"), 1)
                        pe.wait_ge(pool.sem, pool.at(c, "sq_mul"))
                        add_up(queries[:, 0:ROWS], t_q[g]).then_inc(mine.mark("sq"), 1)
                        yield
                        pe.wait_ge(dve.sem, dve.at(c, "d_mul"))
                        add_up(d_in[:, 0:2 * ROWS], t_mul[g]).then_inc(mine.mark("d"), 1)
                        yield
                    yield

                staggered(sums)

            recurrence_done(pe)

            def out_mean(dve_s, mine, n, s, loads):
                pe.wait_ge(o_loaded[s], loads)
                if s > 0:
                    pe.wait_ge(dve_s.sem, dve_s.at(n, f"oc{s - 1}{KT - 1}"))
                for k in range(KT):
                    pe.matmul(bank[3 + 4 * k][:], mean16[:], c_o[s][:, k], start=True, stop=True).then_inc(mine.mark(f"mean{s}{k}"), 1)

            def out_var(pool_s, dve_s, mine, n, s):
                pe.wait_ge(pool_s.sem, pool_s.at(n, f"osq{s}"))
                pe.wait_ge(dve_s.sem, dve_s.at(n, f"ov{s - 1}{KT - 1}" if s > 0 else f"oc{len(SLOTS) - 1}{KT - 1}"))
                for k in range(KT):
                    pe.matmul(bank[3 + 4 * k][:], mean16[:], c_ostd[s][:, k], start=True, stop=True).then_inc(mine.mark(f"var{s}{k}"), 1)

            for s in SLOTS:
                out_mean(first_dve, first_pe, 0, s, 32)
            for s in SLOTS:
                out_var(first_pool, first_dve, first_pe, 0, s)
            pe.wait_ge(first_dve.sem, first_dve.at(0, f"pick{len(SLOTS) - 1}"))
            with pe.Fori(0, BATCH // 2) as i:
                B = lambda s, j: bank[4 * s + j]
                for s in SLOTS:
                    pe.wait_ge(c_dve.sem, c_dve.before(i, f"rv{s}1"))
                    for layer in range(LAYERS):
                        mm = pe.matmul(B(s, layer)[:], c_pick[s][0:BATCH], gates_row[:, layer * 2 * DIM:(layer + 1) * 2 * DIM],
                                       start=True, stop=True)
                        mm.then_inc(c_pe.mark(f"gb{s}{layer}"), 1)

                def rows_out(s, name, lhs, rhs, banks):
                    for a in range(2):
                        for j in range(2):
                            for k in range(KT):
                                mm = pe.matmul(B(s, banks[a])[:, j * DIM:(j + 1) * DIM], lhs(k, 2 * a + j), rhs(k),
                                               start=(k == 0), stop=(k == KT - 1))
                        mm.then_inc(c_pe.mark(f"{name}{s}{a}"), 1)

                def tok(t):
                    return slice(t * P, (t + 1) * P)

                def turn_c(s, stage, banks):
                    pe.wait_ge(c_dve.sem, c_dve.at(i, f"xh{stage}{s}3"))
                    for k in range(KT):
                        for t in range(TT):
                            mm = pe.transpose(B(s, banks[k])[:, tok(t)], c_xhat[s][:, t, k * P:(k + 1) * P], ident[:])
                        mm.then_inc(c_pe.mark(f"turn{stage}{s}{k}"), 1)

                for s in SLOTS:
                    pe.wait_ge(c_dve.sem, c_dve.at(i, f"wo{s}"))
                    pe.wait_ge(c_act.sem, c_act.before(i, f"kk{s}1"))
                    rows_out(s, "wo", lambda k, t: c_oz[s][:, k, tok(t)], lambda k: c_wo[s][:, k], (2, 3))
                for s in SLOTS:
                    turn_c(s, 1, (0, 1))
                    pe.wait_ge(c_act.sem, c_act.at(i, f"h1{s}1"))
                    for k in range(KT):
                        mm = pe.matmul(B(s, 0)[0:RANK], u1_sb[:, k], c_h[s][:, k, 1:TOK + 1], start=(k == 0), stop=(k == KT - 1))
                    mm.then_inc(c_pe.mark(f"u1{s}"), 1)

                def up(s, f):
                    if f == 0:
                        pe.wait_ge(c_act.sem, c_act.at(i, f"p{s}"))
                        pe.wait_ge(c_pool.sem, c_pool.at(i, f"one{s}"))
                    if f >= UP_BANKS:
                        pe.wait_ge(c_act.sem, c_act.at(i, f"gelu{s}{f - UP_BANKS}"))
                    mm = pe.matmul(B(s, 1 + f % UP_BANKS)[:], v1_sb[:, f * P:(f + 1) * P], c_p[s][0:RANK + 1], start=True, stop=True)
                    mm.then_inc(c_pe.mark(f"v1{s}{f}"), 1)

                for s in SLOTS:
                    for f in range(UP_BANKS):
                        up(s, f)
                for f in range(FT):
                    for s in SLOTS:
                        pe.wait_ge(c_act.sem, c_act.at(i, f"gelu{s}{f}"))
                        mm = pe.matmul(B(s, 0)[0:RANK], u2_sb[:, f], c_f[s][:, f % 3], start=(f == 0), stop=(f == FT - 1))
                        mm.then_inc(c_pe.mark(f"u2{s}{f}"), 1)
                        if f + UP_BANKS < FT:
                            up(s, f + UP_BANKS)
                        what, r = OUT_AT.get((f, s), ("", 0))
                        if what == "mean":
                            out_mean(c_dve, c_pe, i, r, 32 * (i + 2))
                        if what == "var":
                            out_var(c_pool, c_dve, c_pe, i, r)
                for s in SLOTS:
                    pe.wait_ge(c_act.sem, c_act.at(i, f"qr{s}"))
                    for a in range(2):
                        for j in range(2):
                            mm = pe.matmul(B(s, 1 + a)[:, j * DIM:(j + 1) * DIM], c_qr[s][0:RANK + 1, tok(2 * a + j)],
                                           c_v2[s][0:RANK + 1], start=True, stop=True)
                        mm.then_inc(c_pe.mark(f"v2{s}{a}"), 1)
                for s in SLOTS:
                    turn_c(s, 2, (3, 0))
                    pe.wait_ge(c_act.sem, c_act.at(i, f"h2{s}{KT - 1}"))
                    pe.wait_ge(c_dve.sem, c_dve.at(i, f"x2{s}1"))
                    rows_out(s, "vt", lambda k, t: c_h[s][:, k, 1 + t * P:1 + (t + 1) * P], lambda k: w_attn_sb[:, k, 2 * DIM:3 * DIM], (1, 2))
                for which, banks in (("q", (3, 0)), ("k", (1, 2))):
                    for s in SLOTS:
                        if which == "k":
                            pe.wait_ge(c_act.sem, c_act.at(i, f"vt{s}0"))
                            pe.wait_ge(c_dve.sem, c_dve.at(i, f"vt{s}1"))
                        for m in range(KT):
                            j = ("q", "k").index(which) * KT + m
                            for k in range(KT):
                                mm = pe.matmul(B(s, banks[m])[:], w_attn_sb[:, k, j * P:(j + 1) * P], c_h[s][:, k, 1:TOK + 1],
                                               start=(k == 0), stop=(k == KT - 1))
                            mm.then_inc(c_pe.mark(f"{which}{s}{m}"), 1)

                def stay_warm(step):
                    for _ in range(WARM.get(step, 0)):
                        pe.matmul(bank[Y_BANKS[2]][:, 0:2 * KT * KEYS], identb[:], mask_sb[:, 0:2].rearrange("p a b -> p (a b)"), start=True, stop=True)

                pe.wait_ge(c_act.sem, c_act.at(i, "qb103"))
                stay_warm("s0")
                for t in range(len(ATT) + PV_LAG):
                    if t < len(ATT):
                        f, s = ATT[t]
                        if f == 0:
                            pe.wait_ge(c_act.sem, c_act.at(i, "ks13"))
                            pe.wait_ge(c_dve.sem, c_dve.at(i, "ks13"))
                            pe.wait_ge(c_pool.sem, c_pool.at(i, "pad13"))
                        else:
                            pe.wait_ge(c_act.sem, c_act.at(i, f"exp{s}{f - 1}u{QUADS - 1}"))
                        for top in range(2):
                            pe.matmul(B(s, top)[:, 0:KT * KEYS], identb[:], mask_sb[:, min(f, 3)], start=True, stop=False,
                                      skip_group_check=True)
                        for k in range(KT):
                            for top in range(2):
                                rows = slice(64 * top, 64 * top + 64)
                                mm = pe.matmul(B(s, top)[:, k * KEYS:(k + 1) * KEYS], c_qb[s][rows, k, f],
                                               c_k[s][rows, k, f], start=False, stop=True, skip_group_check=True)
                        mm.then_inc(c_pe.mark(f"s{s}{f}"), 1)
                    stay_warm(f"t{t - T_LAG}")
                    if 0 <= t - T_LAG < len(ATT):
                        f, s = ATT[t - T_LAG]
                        pe.wait_ge(c_pool.sem, c_pool.at(i, f"prob{s}{f}"))
                        if t > T_LAG:
                            g, r = ATT[t - T_LAG - 1]
                            pe.wait_ge(c_act.sem, c_act.at(i, f"pt{r}{g}"))
                        for u in range(QUADS):
                            mm = pe.transpose(bank[TURNED][0:KEYS, tok(u)], c_soft[s][:, f % 2, u], ident[:])
                        mm.then_inc(c_pe.mark(f"t{s}{f}"), 1)
                    stay_warm(f"pv{t - PV_LAG}")
                    if 0 <= t - PV_LAG < len(ATT):
                        f, s = ATT[t - PV_LAG]
                        if f == 0:
                            pe.wait_ge(v_framed[s], 16 * FRAMED * (i + 1))
                        pe.wait_ge(c_act.sem, c_act.at(i, f"pt{s}{f}"))
                        turn = len(SLOTS) * (f // QTR) + s
                        if f % QTR == 0 and turn >= len(Y_BANKS):
                            before = turn - len(Y_BANKS)
                            pe.wait_ge(c_dve.sem, c_dve.at(i, f"y{before % 2}{before // 2}"))
                        for u in range(QUADS):
                            top, k = u // 2, u % 2
                            for pr in range(2):
                                head = (k * P + 64 * top) // HD + 2 * pr
                                row = 64 * top + 32 * pr
                                col = (k * QTR + f % QTR) * 2 * QF
                                mm = pe.matmul(y_bank(s, f // QTR)[row:row + 32, col:col + 2 * QF],
                                               c_v[s][0:KEYS, f, head * HD:(head + 2) * HD],
                                               c_pt[s][0:KEYS, u * P + 64 * pr:u * P + 64 * pr + 64],
                                               start=True, stop=True)
                        mm.then_inc(c_pe.mark(f"pv{s}{f}"), 1)
                for s in SLOTS:
                    pe.wait_ge(c_dve.sem, c_dve.at(i, f"y{s}3"))
                    rows_out(s, "wp", lambda k, t: c_y[s][:, t, k], lambda k: c_wp[s][:, k], (0, 1))
                for s in SLOTS:
                    turn_c(s, 3, (2, 3))
                for s in SLOTS:
                    pe.wait_ge(c_dve.sem, c_dve.at(i, f"xr{s}{KT - 1}"))
                    rows_out(s, "r", lambda k, t: c_xr[s][:, k, tok(t)], lambda k: w_rkv_sb[:, 0, k], (0, 1))
                    pe.wait_ge(c_dve.sem, c_dve.at(i, f"xk{s}{KT - 1}"))
                    for m in range(KT):
                        for k in range(KT):
                            mm = pe.matmul(B(s, 2 + m)[:], w_rkv_sb[:, 1, k, m * P:(m + 1) * P], c_xk[s][:, k],
                                           start=(k == 0), stop=(k == KT - 1))
                        mm.then_inc(c_pe.mark(f"kk{s}{m}"), 1)
                for s in SLOTS:
                    pe.wait_ge(c_pool.sem, c_pool.at(i, f"kk{s}1"))
                    pe.wait_ge(c_act.sem, c_act.at(i, f"r{s}1"))
                    rows_out(s, "vv", lambda k, t: c_kk[s][:, k, tok(t)], lambda k: c_wv[s][:, k], (0, 1))

        @block.scalar
        def _(act):
            for st in (su_act, ln_act, pr_act, st_act, *re_act, first_act, c_act):
                act.sem_inc(st.sem, len(st.names))
            act.wait_ge(cond_loaded, 16)
            act.activation(cond_silu, cond_sb, ACT.Silu).then_inc(su_act.mark("silu"), 1)
            act.wait_ge(su_pe.sem, su_pe.at(0, "mod"))
            act.activation(modc[:].rearrange("p a b -> p (a b)"), bank[0][:, 0:LAYERS * N_MOD * KT * BATCH], ACT.Copy).then_inc(su_act.mark("modc"), 1)
            for layer in range(LAYERS):
                act.wait_ge(su_pe.sem, su_pe.at(0, f"gate{layer}"))
                act.activation(g_raw[0:BATCH, layer * 2 * DIM:(layer + 1) * 2 * DIM], bank[1 + layer][0:BATCH], ACT.Copy).then_inc(su_act.mark(f"raw{layer}"), 1)

            def norm_a(m):
                act.wait_ge(su_dve.sem, su_dve.at(0, "gates"))
                act.wait_ge(ln_act.sem, ln_act.before(m, "h1"))
                ins = act.activation(a_modb, modc[:, 0:2 * KT, bass.ds(m, 1)].rearrange("p a o -> p (a o)"), ACT.Copy)
                ins.then_inc(ln_act.mark("modb"), 1)
                act.wait_ge(ln_dve.sem, ln_dve.at(m, "ag3"))
                act.activation(a_std, a_mv[:, :, 1], ACT.Sqrt, bias=parity[:, 6:7]).then_inc(ln_act.mark("std"), 1)

            def modulate_a(m):
                act.wait_ge(ln_act.sem, ln_act.at(m, "modb"))
                act.wait_ge(pr_pe.sem, pr_pe.before(m, "lr"))
                for k in range(KT):
                    act.wait_ge(ln_pe.sem, ln_pe.at(m, f"t{k}"))
                    ins = act.activation(a_h[:, k], bank[k][:], ACT.Identity, bias=a_modb[:, k:k + 1], scale=a_modb[:, KT + k:KT + k + 1])
                    ins.then_inc(ln_act.mark(f"h{k}"), 1)

            def evacuate(n):
                def tap(t):
                    act.wait_ge(pr_pe.sem, pr_pe.at(n, QKV[t]))
                    act.wait_ge(a_stored[QKV[t]], 16 * n)
                    col = (t // KT) * TAPS + TAPS - 1
                    ins = act.activation(a_acc[:, t], bank[2 + t][:], ACT.Copy, scale=taps_sb[:, t % KT, col:col + 1])
                    ins.then_inc(pr_act.mark(f"tap{t}"), 1)

                def silu(t):
                    act.wait_ge(pr_dve.sem, pr_dve.at(n, f"c{t}3"))
                    act.activation(a_acc[:, t], a_acc[:, t], ACT.Silu).then_inc(pr_act.mark(f"silu{t}"), 1)

                def gate(k):
                    act.wait_ge(pr_pe.sem, pr_pe.at(n, f"g{k}"))
                    act.wait_ge(a_stored[f"g{k}"], 16 * n)
                    act.activation(a_gate[:, k], bank[2 + k][:], ACT.Copy).then_inc(pr_act.mark(f"g{k}"), 1)

                tap(0), tap(1), tap(2), silu(0), tap(3), silu(1), tap(4), silu(2), tap(5), silu(3)
                gate(0), silu(4), gate(1), silu(5)
                act.wait_ge(pr_pe.sem, pr_pe.at(n, "lr"))
                act.wait_ge(a_stored["lr"], 16 * n)
                ins = act.activation(a_lr[0:2 * HEADS], bank[4][0:2 * HEADS], ACT.Copy, bias=BASE_LR)
                ins.then_inc(pr_act.mark("lr"), 1)

            def lengths(n):
                for t in range(4):
                    act.wait_ge(pr_pe.sem, pr_pe.at(n, f"ss{t}"))
                    act.wait_ge(pr_pool.sem, pr_pool.before(n, f"unit{t}"))
                    act.activation(a_rn[:, t], bank[4 + t][:], ACT.Ln, scale=float(HD)).then_inc(pr_act.mark(f"ln{t}"), 1)
                for t in range(4):
                    act.wait_ge(pr_act.sem, pr_act.at(n, f"ln{t}"))
                    act.activation(a_rn[:, t], a_rn[:, t], ACT.Exp, scale=-0.5).then_inc(pr_act.mark(f"rn{t}"), 1)

            norm_a(0)
            modulate_a(0)
            with act.Fori(0, BATCH - 1) as n:
                norm_a(n + 1)
                evacuate(n)
                modulate_a(n + 1)
                lengths(n)
            evacuate(BATCH - 1)
            lengths(BATCH - 1)

            phase_a_done(act)
            act.wait_ge(lr_loaded, 16 * GROUPS)
            act.activation(lr_tmp, lr_raw, ACT.Abs).then_inc(st_act.mark("abs"), 1)
            act.wait_ge(st_act.sem, st_act.at(0, "abs"))
            act.activation(lr_tmp, lr_tmp, ACT.Exp, scale=-1.0).then_inc(st_act.mark("exp"), 1)
            act.wait_ge(st_act.sem, st_act.at(0, "exp"))
            act.activation(lr_tmp, lr_tmp, ACT.Ln, bias=1.0).then_inc(st_act.mark("ln"), 1)

            with act.Fori(0, ROUNDS) as n:
                def exponentials(g):
                    dve, mine = re_dve[g], re_act[g]
                    attn = float(HD) ** -0.5
                    for j in range(CPR):
                        c = n * CPR + j
                        act.wait_ge(dve.sem, dve.at(c, "sub2"))
                        act.activation(e_2[g], e_2[g], ACT.Exp, scale=attn).then_inc(mine.mark("e2"), 1)
                        act.wait_ge(dve.sem, dve.at(c, "psub"))
                        act.activation(e_p[g], e_p[g], ACT.Exp, scale=attn).then_inc(mine.mark("ep"), 1)
                        act.wait_ge(dve.sem, dve.at(c, "ksub"))
                        act.activation(e_k[g], e_k[g], ACT.Exp).then_inc(mine.mark("ek"), 1)
                        yield
                        yield
                        act.wait_ge(dve.sem, dve.at(c, "bsub"))
                        act.activation(e_b[g], e_b[g], ACT.Exp, scale=attn).then_inc(mine.mark("eb"), 1)
                        act.wait_ge(dve.sem, dve.at(c, "qsub"))
                        act.activation(e_q[g], e_q[g], ACT.Exp).then_inc(mine.mark("eq"), 1)
                        yield
                    yield

                staggered(exponentials)

            def out_ln(dve_s, mine, n, s):
                act.wait_ge(dve_s.sem, dve_s.at(n, f"ov{s}{KT - 1}"))
                act.activation(c_ostd[s], c_ostd[s], ACT.Ln, bias=parity[:, 6:7]).then_inc(mine.mark(f"oln{s}"), 1)

            def out_exp(mine, n, s):
                act.wait_ge(mine.sem, mine.at(n, f"oln{s}"))
                act.activation(c_ostd[s], c_ostd[s], ACT.Exp, scale=-0.5).then_inc(mine.mark(f"orstd{s}"), 1)

            for s in SLOTS:
                out_ln(first_dve, first_act, 0, s)
            for s in SLOTS:
                out_exp(first_act, 0, s)
            with act.Fori(0, BATCH // 2) as i:
                B = lambda s, j: bank[4 * s + j]

                def std(stage, s):
                    act.wait_ge(c_dve.sem, c_dve.at(i, f"ag{stage}{s}{TT - 1}"))
                    act.activation(c_std[s], c_mv[s][:, :, 1], ACT.Sqrt, bias=parity[:, 6:7]).then_inc(c_act.mark(f"std{stage}{s}"), 1)

                def modulate(stage, s, k, banks):
                    act.wait_ge(c_pe.sem, c_pe.at(i, f"turn{stage}{s}{k}"))
                    ins = act.activation(c_h[s][:, k, 1:TOK + 1], B(s, banks[k])[:], ACT.Identity,
                                         bias=c_modb[s][:, stage - 1, k:k + 1],
                                         scale=c_modb[s][:, stage - 1, KT + k:KT + k + 1])
                    ins.then_inc(c_act.mark(f"h{stage}{s}{k}"), 1)

                def norm(stage, banks):
                    std(stage, 0)
                    modulate(stage, 0, 0, banks)
                    std(stage, 1)
                    modulate(stage, 0, 1, banks)
                    for k in range(KT):
                        modulate(stage, 1, k, banks)

                norm(1, (0, 1))
                for s in SLOTS:
                    act.wait_ge(c_pe.sem, c_pe.at(i, f"u1{s}"))
                    act.wait_ge(c_pe.sem, c_pe.at(i, "wo11"))
                    act.activation(c_p[s][0:RANK], B(s, 0)[0:RANK], ACT.Copy).then_inc(c_act.mark(f"p{s}"), 1)
                for f in range(FT):
                    for s in SLOTS:
                        act.wait_ge(c_pe.sem, c_pe.at(i, f"v1{s}{f}"))
                        if f >= 3:
                            act.wait_ge(c_pe.sem, c_pe.at(i, f"u2{s}{f - 3}"))
                        act.activation(c_f[s][:, f % 3], B(s, 1 + f % UP_BANKS)[:], ACT.Gelu_apprx_tanh).then_inc(c_act.mark(f"gelu{s}{f}"), 1)
                for s in SLOTS:
                    out_ln(c_dve, c_act, i, s)
                for s in SLOTS:
                    act.wait_ge(c_pe.sem, c_pe.at(i, f"u2{s}{FT - 1}"))
                    act.activation(c_qr[s][0:RANK], B(s, 0)[0:RANK], ACT.Copy).then_inc(c_act.mark(f"qr{s}"), 1)
                for s in SLOTS:
                    out_exp(c_act, i, s)
                norm(2, (3, 0))

                def segments(dst, src):
                    blocks = src.rearrange("p (f q) -> p f q", q=QF)
                    return ((dst[:, 2:FRAMES, 0:QF], blocks[:, 0:FRAMES - 2]),
                            (dst[:, 1:FRAMES, QF:2 * QF], blocks[:, 0:FRAMES - 1]),
                            (dst[:, :, 2 * QF:3 * QF], blocks),
                            (dst[:, :, 3 * QF:KEYS], src[:, 0:NGLOB].unsqueeze(1).broadcast_to([P, FRAMES, NGLOB])))

                for s in SLOTS:
                    act.wait_ge(c_pe.sem, c_pe.at(i, f"vt{s}0"))
                    act.activation(c_vt[s][:, 0:2], B(s, 1)[:].rearrange("p (t d) -> p t d", t=2), ACT.Copy).then_inc(c_act.mark(f"vt{s}0"), 1)
                for s in SLOTS:
                    act.wait_ge(c_pe.sem, c_pe.at(i, f"q{s}0"))
                    for j in range(4):
                        act.activation(c_qb[s][:, 0, :, j * QF:(j + 1) * QF], B(s, 3)[:].rearrange("p (f q) -> p f q", q=QF),
                                       ACT.Copy, scale=parity[:, j:j + 1]).then_inc(c_act.mark(f"qb{s}0{j}"), 1)
                for s in SLOTS:
                    act.wait_ge(c_pe.sem, c_pe.at(i, f"k{s}1"))
                    if s == 0:
                        act.wait_ge(c_dve.sem, c_dve.at(i, f"oz{len(SLOTS) - 1}"))
                    for g, (dst, src) in enumerate(segments(c_k[s][:, 1], B(s, 2)[:])):
                        act.activation(dst, src, ACT.Copy).then_inc(c_act.mark(f"ks{s}{g}"), 1)

                for t in range(len(ATT) + YE_LAG + 1):
                    if t < len(ATT):
                        f, s = ATT[t]
                        act.wait_ge(c_dve.sem, c_dve.at(i, f"max{s}{f}"))
                        if f >= 2:
                            act.wait_ge(c_pe.sem, c_pe.at(i, f"t{s}{f - 2}"))
                        for u in range(QUADS):
                            sc = B(s, u // KT)[:, (u % KT) * KEYS:(u % KT + 1) * KEYS]
                            act.activation(c_soft[s][:, f % 2, u], sc, ACT.Exp, bias=c_max[s][:, u:u + 1]).then_inc(c_act.mark(f"exp{s}{f}u{u}"), 1)
                    if 0 <= t - T_LAG < len(ATT):
                        f, s = ATT[t - T_LAG]
                        act.wait_ge(c_pe.sem, c_pe.at(i, f"t{s}{f}"))
                        if f > 0:
                            act.wait_ge(c_pe.sem, c_pe.at(i, f"pv{s}{f - 1}"))
                        act.activation(c_pt[s][0:KEYS], bank[TURNED][0:KEYS], ACT.Copy).then_inc(c_act.mark(f"pt{s}{f}"), 1)
                    if 0 <= t - YE_LAG < len(ATT) and ends_quarter(ATT[t - YE_LAG][0]):
                        f, s = ATT[t - YE_LAG]
                        act.wait_ge(c_pe.sem, c_pe.at(i, f"pv{s}{f}"))
                        if f > QTR:
                            act.wait_ge(c_dve.sem, c_dve.at(i, f"y{s}{f // QTR - 1}"))
                        src = y_bank(s, f // QTR)[:].rearrange("p (f e q) -> p f e q", e=2, q=QF)[:, :, 0]
                        act.activation(c_yeven[s], src, ACT.Copy, scale=parity[:, 4:5]).then_inc(c_act.mark(f"ye{s}{f // QTR}"), 1)
                norm(3, (2, 3))
                for s in SLOTS:
                    for a in range(2):
                        act.wait_ge(c_pe.sem, c_pe.at(i, f"r{s}{a}"))
                        act.activation(c_r[s][:, 2 * a:2 * a + 2], B(s, a)[:].rearrange("p (t d) -> p t d", t=2), ACT.Sigmoid).then_inc(c_act.mark(f"r{s}{a}"), 1)
                    for m in range(KT):
                        act.wait_ge(c_pe.sem, c_pe.at(i, f"kk{s}{m}"))
                        act.activation(c_kk[s][:, m], B(s, 2 + m)[:], ACT.Relu).then_inc(c_act.mark(f"kk{s}{m}"), 1)

        @block.gpsimd
        def _(pool):
            for st in (pr_pool, scan_ready, *re_pool, first_pool, c_pool):
                pool.sem_inc(st.sem, len(st.names))
            with pool.Fori(0, BATCH) as n:
                for t in range(4):
                    pool.wait_ge(pr_act.sem, pr_act.at(n, f"silu{t}"))
                    pool.wait_ge(pr_pe.sem, pr_pe.before(n, f"ss{t}"))
                    pool.tensor_tensor(a_sq[:, t], a_acc[:, t], a_acc[:, t], ALU.mult).then_inc(pr_pool.mark(f"sq{t}"), 1)
                for t in range(4):
                    pool.wait_ge(pr_act.sem, pr_act.at(n, f"rn{t}"))
                    pool.tensor_tensor(a_acc[:, t], a_acc[:, t], a_rn[:, t], ALU.mult).then_inc(pr_pool.mark(f"unit{t}"), 1)

            phase_a_done(pool)
            pool.memset(scan_keep, 1.0).then_inc(scan_ready.mark("ones"), 1)
            pool.wait_ge(scan_ready.sem, scan_ready.at(0, "ones"))
            pool.memset(scan_keep.rearrange("p (a l) -> p a l", l=CHUNK)[:, :, 0:1], 0.0).then_inc(scan_ready.mark("zeros"), 1)
            with pool.Fori(0, ROUNDS) as n:
                def products(g):
                    dve, mine = re_dve[g], re_pool[g]
                    cube = lambda t: t.rearrange("p (a l d) -> p a l d", a=INNER, l=16)
                    terms = lambda t: t.rearrange("p (d a l) -> p a l d", d=HD, a=INNER)
                    grid = lambda t: t.rearrange("p (a l) -> p a l", a=INNER)
                    by_ld = lambda w: grid(w).unsqueeze(2).broadcast_to([P, INNER, CHUNK, HD])
                    by_dl = lambda w: grid(w).unsqueeze(2).broadcast_to([P, INNER, HD, CHUNK])
                    for j in range(CPR):
                        c = n * CPR + j
                        buf, before = j // CPB, (j - 1) % CPR // CPB
                        now = slice(j % CPB * CHUNK, (j % CPB + 1) * CHUNK)
                        last = slice((j - 1) % CPB * CHUNK, ((j - 1) % CPB + 1) * CHUNK)
                        pool.wait_ge(dve.sem, dve.at(c, "p2"))
                        v_dl = v_blk[before][g][:, :, last].unsqueeze(1).broadcast_to([P, INNER, HD, CHUNK])
                        pool.tensor_tensor(cube(t_g2[g]), by_dl(p_2[g]), v_dl, ALU.mult).then_inc(mine.mark("g2"), 1)
                        if j % CPB == 0:
                            pool.wait_ge(blk_loaded[buf][g], 48 * (n + 1))
                        pool.wait_ge(dve.sem, dve.at(c, "p1"))
                        v_dl = v_blk[buf][g][:, :, now].unsqueeze(1).broadcast_to([P, INNER, HD, CHUNK])
                        pool.tensor_tensor(cube(t_g1[g]), by_dl(p_out1[g]), v_dl, ALU.mult).then_inc(mine.mark("g1"), 1)
                        pool.wait_ge(dve.sem, dve.at(c, "kh"))
                        pool.tensor_tensor(cube(t_run[g]), by_dl(k_hat[g]), v_dl, ALU.mult).then_inc(mine.mark("kv"), 1)
                        yield
                        if j == 0:
                            pool.wait_ge(st_dve.sem, st_dve.at(0, f"out{g}"))
                        pool.wait_ge(dve.sem, dve.before(c, "win"))
                        q_ld = q_blk[buf][g][:, :, now].rearrange("p d l -> p l d").unsqueeze(1).broadcast_to([P, INNER, CHUNK, HD])
                        pool.tensor_tensor(terms(t_q[g]), by_ld(win[g]), q_ld, ALU.mult).then_inc(mine.mark("sq_mul"), 1)
                        yield
                        yield
                        pool.wait_ge(dve.sem, dve.at(c, "qh"))
                        pool.tensor_tensor(cube(t_q[g]), by_dl(q_hat[g]), cube(t_run[g]), ALU.mult).then_inc(mine.mark("o_mul"), 1)
                        pool.wait_ge(mine.sem, mine.at(c, "o_mul"))
                        half, quarter = PROD // 2, PROD // 4
                        pool.tensor_tensor(t_q8[g], t_q[g][:, 0:half], t_q[g][:, half:PROD], ALU.add).then_inc(mine.mark("o2"), 1)
                        pool.wait_ge(mine.sem, mine.at(c, "o2"))
                        if j % CPB == 0:
                            pool.wait_ge(o_stored[buf][g], 16 * n)
                        to = lambda t: t.rearrange("p (d l) -> p d l", d=HD)
                        pool.tensor_tensor(o_blk[buf][g][:, :, now], to(t_q8[g][:, 0:quarter]), to(t_q8[g][:, quarter:half]), ALU.add).then_inc(mine.mark("o1"), 1)
                    yield

                staggered(products)

            def out_square(dve_s, mine, n, s):
                pool.wait_ge(dve_s.sem, dve_s.at(n, f"oc{s}{KT - 1}"))
                pool.tensor_tensor(c_ostd[s], c_o[s], c_o[s], ALU.mult).then_inc(mine.mark(f"osq{s}"), 1)

            for s in SLOTS:
                out_square(first_dve, first_pool, 0, s)
            with pool.Fori(0, BATCH // 2) as i:
                pool.wait_ge(c_pool.sem, c_pool.before(i, "x411"))
                hold(pool)
                for s in SLOTS:
                    pool.wait_ge(c_pe.sem, c_pe.at(i, "wo11"))
                    hold(pool)
                    pool.memset(c_one[s], 1.0).then_inc(c_pool.mark(f"one{s}"), 1)
                for s in SLOTS:
                    out_square(c_dve, c_pool, i, s)
                pool.wait_ge(c_pe.sem, c_pe.at(i, "v211"))
                hold(pool)
                pool.wait_ge(c_dve.sem, c_dve.at(i, f"oz{len(SLOTS) - 1}"))
                hold(pool)
                for s in SLOTS:
                    for j, pad in enumerate((c_k[s][:, :, 0:2, 0:QF], c_k[s][:, :, 0:1, QF:2 * QF], c_v[s][0:2 * QF, 0:1], c_v[s][0:QF, 1:2])):
                        pool.memset(pad, 0.0).then_inc(c_pool.mark(f"pad{s}{j}"), 1)
                for f, s in ATT:
                    pool.wait_ge(c_dve.sem, c_dve.at(i, f"arec{s}{f}"))
                    soft = c_soft[s][:, f % 2]
                    pool.tensor_tensor(soft, soft, c_rec[s].unsqueeze(2).broadcast_to([P, 4, KEYS]), ALU.mult).then_inc(c_pool.mark(f"prob{s}{f}"), 1)
                pool.wait_ge(c_act.sem, c_act.at(i, f"h31{KT - 1}"))
                pool.tensor_tensor(c_d[1], c_h[1][:, :, 1:TOK + 1], c_h[1][:, :, 0:TOK], ALU.subtract).then_inc(c_pool.mark("d1"), 1)
                for s in SLOTS:
                    for m in range(KT):
                        pool.wait_ge(c_act.sem, c_act.at(i, f"kk{s}{m}"))
                        pool.tensor_tensor(c_kk[s][:, m], c_kk[s][:, m], c_kk[s][:, m], ALU.mult).then_inc(c_pool.mark(f"kk{s}{m}"), 1)
                for s in SLOTS:
                    for a in range(2):
                        pool.wait_ge(c_dve.sem, c_dve.at(i, f"rv{s}{a}"))
                        half = slice(2 * a, 2 * a + 2)
                        pool.tensor_tensor(c_x[s][:, half], c_x[s][:, half], c_rv[s][:, half], ALU.add).then_inc(c_pool.mark(f"x4{s}{a}"), 1)

        @block.vector
        def _(dve):
            for st in (su_dve, ln_dve, pr_dve, st_dve, *re_dve, first_dve, c_dve):
                dve.sem_inc(st.sem, len(st.names))
            dve.wait_ge(consts_loaded, 48)
            dve.tensor_copy(identb[:], ident[:]).then_inc(su_dve.mark("identb"), 1)
            dve.wait_ge(su_act.sem, su_act.at(0, "modc"))
            for j, layer_which in enumerate((1, 4, 7, 10)):
                cols = modc[:, layer_which * KT:(layer_which + 1) * KT]
                dve.tensor_scalar(cols, cols, 1.0, None, ALU.add).then_inc(su_dve.mark(f"plus{j + 1}"), 1)
            dve.wait_ge(weights_loaded, 16 * (18 + 2 * GROUP_B))
            own_tap = taps_sb[:].rearrange("p k (c j) -> p k c j", j=TAPS)[:, :, :, TAPS - 1]
            dve.tensor_scalar(own_tap, own_tap, 1.0, None, ALU.add).then_inc(su_dve.mark("tap"), 1)
            dve.wait_ge(su_act.sem, su_act.at(0, "raw1"))
            dve.tensor_scalar(g_sign[0:BATCH], g_raw[0:BATCH], 0.0, 2.0, ALU.is_ge, ALU.mult).then_inc(su_dve.mark("side"), 1)
            dve.wait_ge(su_dve.sem, su_dve.at(0, "side"))
            dve.tensor_scalar(g_sign[0:BATCH], g_sign[0:BATCH], -1.0, None, ALU.add).then_inc(su_dve.mark("sign"), 1)
            dve.wait_ge(su_dve.sem, su_dve.at(0, "sign"))
            dve.tensor_tensor(g_size[0:BATCH], g_sign[0:BATCH], g_raw[0:BATCH], ALU.mult).then_inc(su_dve.mark("size"), 1)
            dve.wait_ge(su_dve.sem, su_dve.at(0, "size"))
            dve.scalar_tensor_tensor(out=gates_row[:], in0=g_size[0:BATCH], scalar=0.25, in1=g_sign[0:BATCH],
                                                 op0=ALU.max, op1=ALU.mult).then_inc(su_dve.mark("gates"), 1)

            def normalise_a(m):
                dve.wait_ge(x_loaded, 16 * (m + 1))
                dve.wait_ge(ln_act.sem, ln_act.before(m, "std"))
                for t in range(TT):
                    dve.bn_stats(a_stat[:, t], a_x[:, t]).then_inc(ln_dve.mark(f"st{t}"), 1)
                dve.wait_ge(ln_dve.sem, ln_dve.at(m, f"st{TT - 1}"))
                hold(dve)
                for t in range(TT):
                    dve.bn_aggr(a_mv[:, t], a_stat[:, t]).then_inc(ln_dve.mark(f"ag{t}"), 1)
                dve.wait_ge(ln_act.sem, ln_act.at(m, "std"))
                dve.reciprocal(a_rstd, a_std).then_inc(ln_dve.mark("rec"), 1)
                dve.wait_ge(ln_dve.sem, ln_dve.at(m, "rec"))
                dve.wait_ge(ln_pe.sem, ln_pe.before(m, "t1"))
                for t in range(TT):
                    dve.tensor_scalar(a_xhat[:, t], a_x[:, t], a_mv[:, t, 0:1], a_rstd[:, t:t + 1],
                                                  ALU.subtract, ALU.mult).then_inc(ln_dve.mark(f"xh{t}"), 1)

            def convolve(n):
                for t in range(6):
                    for j in (1, 2, 3):
                        if j == 1:
                            dve.wait_ge(pr_act.sem, pr_act.at(n, f"tap{t}"))
                        else:
                            dve.wait_ge(pr_dve.sem, pr_dve.at(n, f"c{t}{j - 1}"))
                        col = (t // KT) * TAPS + TAPS - 1 - j
                        ins = dve.scalar_tensor_tensor(out=a_acc[:, t, j:TOK], in0=bank[2 + t][:, 0:TOK - j],
                                                       scalar=taps_sb[:, t % KT, col:col + 1], in1=a_acc[:, t, j:TOK],
                                                       op0=ALU.mult, op1=ALU.add)
                        ins.then_inc(pr_dve.mark(f"c{t}{j}"), 1)

            dve.wait_ge(su_dve.sem, su_dve.at(0, "tap"))
            normalise_a(0)
            with dve.Fori(0, BATCH - 1) as n:
                normalise_a(n + 1)
                convolve(n)
            convolve(BATCH - 1)

            phase_a_done(dve)
            dve.wait_ge(scan_ready.sem, scan_ready.at(0, "zeros"))
            dve.memset(lr_fin[:, :, 0:CHUNK], 0.0).then_inc(st_dve.mark("pad"), 1)
            dve.wait_ge(st_act.sem, st_act.at(0, "ln"))
            dve.scalar_tensor_tensor(out=lr_fin[:, :, CHUNK:CHUNK + TOK], in0=lr_raw, scalar=0.0, in1=lr_tmp, op0=ALU.max, op1=ALU.add).then_inc(st_dve.mark("lr"), 1)
            dve.wait_ge(st_dve.sem, st_dve.at(0, "lr"))
            for g in PAIRS:
                dve.memset(v_blk[1][g], 0.0).then_inc(st_dve.mark(f"no_v{g}"), 1)
                dve.memset(s_2[g], 0.0).then_inc(st_dve.mark(f"no_s2{g}"), 1)
                dve.tensor_copy(win[g], state0[:, 0]).then_inc(st_dve.mark(f"in{g}"), 1)
                dve.tensor_copy(wout2[g], state0[:, 1]).then_inc(st_dve.mark(f"out{g}"), 1)
            dve.wait_ge(st_dve.sem, st_dve.at(0, f"out{GROUPS - 1}"))
            hold(dve)

            with dve.Fori(0, ROUNDS) as n:
                def states(g):
                    act, pool, pe, mine = re_act[g], re_pool[g], re_pe[g], re_dve[g]
                    scores, d_in, queries = (bank[4 * g + b] for b in range(3))
                    cube = lambda t: t.rearrange("p (a l d) -> p a l d", l=16, d=16)
                    summands = lambda t: t.rearrange("p (x j) -> p x j", j=16)
                    rounds = t_mul[g].rearrange("p (j r a i) -> p r a i j", j=16, r=2, i=16)
                    both_terms = t_mul[g].rearrange("p (j a i) -> p a i j", j=16, i=16)
                    grid = lambda t: t.rearrange("p (a l) -> p a l", l=16)
                    over_a = lambda t: t.rearrange("p (a l) -> p l a", a=INNER)
                    by_ld = lambda w: grid(w).unsqueeze(2).broadcast_to([P, INNER, CHUNK, HD])
                    by_dl = lambda w, a: grid(w).unsqueeze(2).broadcast_to([P, a, HD, CHUNK])
                    tok_ld = lambda t: t.rearrange("p d l -> p l d").unsqueeze(1).broadcast_to([P, INNER, CHUNK, HD])
                    tok_dl = lambda t, a: t.unsqueeze(1).broadcast_to([P, a, HD, CHUNK])
                    per_l = lambda t: t.unsqueeze(1).broadcast_to([P, INNER, CHUNK])
                    per_a = lambda t, a: t.unsqueeze(2).broadcast_to([P, a, CHUNK])
                    for j in range(CPR):
                        c = n * CPR + j
                        buf = j // CPB
                        now = slice(j % CPB * CHUNK, (j % CPB + 1) * CHUNK)
                        k_now, v_now = k_blk[buf][g][:, :, now], v_blk[buf][g][:, :, now]
                        rate = lambda i, ahead: lr_fin[:, 2 * g + i, bass.ds((c + 1 - ahead) * CHUNK, 1)]

                        if j % CPB == 0:
                            dve.wait_ge(blk_loaded[buf][g], 48 * (n + 1))
                        dve.wait_ge(mine.sem, mine.before(c, "a1"))
                        dve.tensor_tensor(cube(t_mul[g][:, PROD:2 * PROD]), by_ld(win[g]), tok_ld(k_now), ALU.mult).then_inc(mine.mark("a0_mul"), 1)
                        dve.tensor_reduce(m_2[g], grid(s_2[g]), AX.X, ALU.max).then_inc(mine.mark("max2"), 1)
                        dve.wait_ge(mine.sem, mine.at(c, "a0_mul"))
                        dve.tensor_reduce(s_a[g], summands(t_mul[g][:, PROD:2 * PROD]), AX.X, ALU.add).then_inc(mine.mark("a0"), 1)
                        dve.wait_ge(mine.sem, mine.at(c, "max2"))
                        dve.tensor_tensor(grid(e_2[g]), grid(s_2[g]), per_a(m_2[g], INNER), ALU.subtract).then_inc(mine.mark("sub2"), 1)
                        dve.wait_ge(mine.sem, mine.at(c, "a0"))
                        dve.tensor_reduce(m_p[g], grid(s_a[g]), AX.X, ALU.max).then_inc(mine.mark("pmax"), 1)
                        dve.tensor_reduce(m_k[g], over_a(s_a[g]), AX.X, ALU.max).then_inc(mine.mark("kmax"), 1)
                        dve.wait_ge(mine.sem, mine.at(c, "pmax"))
                        dve.tensor_tensor(grid(e_p[g]), grid(s_a[g]), per_a(m_p[g], INNER), ALU.subtract).then_inc(mine.mark("psub"), 1)
                        dve.wait_ge(mine.sem, mine.at(c, "kmax"))
                        dve.tensor_tensor(grid(e_k[g]), grid(s_a[g]), per_l(m_k[g]), ALU.subtract).then_inc(mine.mark("ksub"), 1)
                        dve.wait_ge(act.sem, act.at(c, "e2"))
                        dve.tensor_reduce(z_2[g], grid(e_2[g]), AX.X, ALU.add).then_inc(mine.mark("sum2"), 1)
                        dve.wait_ge(act.sem, act.at(c, "ep"))
                        dve.tensor_reduce(z_p[g], grid(e_p[g]), AX.X, ALU.add).then_inc(mine.mark("psum"), 1)
                        dve.wait_ge(act.sem, act.at(c, "ek"))
                        dve.tensor_reduce(z_k[g], over_a(e_k[g]), AX.X, ALU.add).then_inc(mine.mark("ksum"), 1)
                        dve.wait_ge(mine.sem, mine.at(c, "sum2"))
                        dve.reciprocal(r_2[g], z_2[g]).then_inc(mine.mark("rec2"), 1)
                        dve.wait_ge(mine.sem, mine.at(c, "psum"))
                        dve.reciprocal(r_p[g], z_p[g]).then_inc(mine.mark("prec"), 1)
                        dve.wait_ge(mine.sem, mine.at(c, "ksum"))
                        dve.reciprocal(r_k[g], z_k[g]).then_inc(mine.mark("krec"), 1)
                        dve.wait_ge(mine.sem, mine.at(c, "rec2"))
                        dve.wait_ge(pool.sem, pool.before(c, "g2"))
                        dve.scalar_tensor_tensor(out=grid(p_2[g]), in0=grid(e_2[g]), scalar=rate(1, 1), in1=per_a(r_2[g], INNER), op0=ALU.mult, op1=ALU.mult).then_inc(mine.mark("p2"), 1)
                        dve.wait_ge(mine.sem, mine.at(c, "krec"))
                        dve.tensor_tensor(rl_k[g], r_k[g], lr_fin[:, 2 * g + 1, bass.ds((c + 1) * CHUNK, CHUNK)], ALU.mult).then_inc(mine.mark("klr"), 1)
                        dve.wait_ge(mine.sem, mine.at(c, "prec"))
                        dve.wait_ge(pool.sem, pool.before(c, "g1"))
                        dve.scalar_tensor_tensor(out=grid(p_out1[g]), in0=grid(e_p[g]), scalar=rate(1, 0), in1=per_a(r_p[g], INNER), op0=ALU.mult, op1=ALU.mult).then_inc(mine.mark("p1"), 1)
                        dve.wait_ge(mine.sem, mine.at(c, "klr"))
                        dve.wait_ge(pool.sem, pool.before(c, "kv"))
                        dve.tensor_tensor(grid(k_hat[g]), grid(e_k[g]), per_l(rl_k[g]), ALU.mult).then_inc(mine.mark("kh"), 1)
                        yield
                        dve.wait_ge(pool.sem, pool.at(c, "g2"))
                        dve.tensor_reduce(g_2[g], summands(t_g2[g]), AX.X, ALU.add).then_inc(mine.mark("g2s"), 1)
                        dve.wait_ge(mine.sem, mine.at(c, "g2s"))
                        dve.tensor_tensor(wout[g], wout2[g], g_2[g], ALU.add).then_inc(mine.mark("wout"), 1)
                        dve.wait_ge(pool.sem, pool.at(c, "g1"))
                        dve.tensor_reduce(g_1[g], summands(t_g1[g]), AX.X, ALU.add).then_inc(mine.mark("g1s"), 1)
                        by_l = grid(t_run[g])
                        dve.wait_ge(mine.sem, mine.at(c, "wout"))
                        dve.wait_ge(pool.sem, pool.at(c, "kv"))
                        dve.tensor_tensor(by_l[:, :, 0], by_l[:, :, 0], wout[g], ALU.add).then_inc(mine.mark("carry"), 1)
                        dve.wait_ge(mine.sem, mine.at(c, "carry"))
                        dve.tensor_tensor_scan(t_run[g], scan_keep, t_run[g], 0.0, ALU.mult, ALU.add).then_inc(mine.mark("run"), 1)
                        wout1 = by_l[:, :, CHUNK - 1]
                        dve.wait_ge(mine.sem, mine.at(c, "run"))
                        dve.tensor_tensor(wout2[g], wout1, g_1[g], ALU.add).then_inc(mine.mark("wout2"), 1)
                        dve.tensor_tensor(rounds[:, 0], wout1.rearrange("p (a d) -> p a d", a=INNER).unsqueeze(2).broadcast_to([P, INNER, CHUNK, HD]),
                                          tok_ld(v_now), ALU.mult).then_inc(mine.mark("b1_mul"), 1)
                        dve.wait_ge(mine.sem, mine.at(c, "wout2"))
                        dve.tensor_tensor(rounds[:, 1], by_ld(wout2[g]), tok_ld(v_now), ALU.mult).then_inc(mine.mark("b2_mul"), 1)
                        yield
                        dve.wait_ge(pe.sem, pe.at(c, "b"))
                        dve.tensor_reduce(m_b[g], grid(scores[:, 0:2 * ROWS]), AX.X, ALU.max).then_inc(mine.mark("bmax"), 1)
                        dve.wait_ge(mine.sem, mine.at(c, "bmax"))
                        dve.tensor_tensor(grid(e_b[g]), grid(scores[:, 0:2 * ROWS]), per_a(m_b[g], 2 * INNER), ALU.subtract).then_inc(mine.mark("bsub"), 1)
                        dve.wait_ge(act.sem, act.at(c, "eb"))
                        dve.tensor_reduce(z_b[g], grid(e_b[g]), AX.X, ALU.add).then_inc(mine.mark("bsum"), 1)
                        dve.wait_ge(mine.sem, mine.at(c, "bsum"))
                        dve.reciprocal(r_b[g], z_b[g]).then_inc(mine.mark("brec"), 1)
                        dve.wait_ge(mine.sem, mine.at(c, "brec"))
                        dve.scalar_tensor_tensor(out=grid(p_in[g]), in0=grid(e_b[g]), scalar=rate(0, 0), in1=per_a(r_b[g], 2 * INNER), op0=ALU.mult, op1=ALU.mult).then_inc(mine.mark("pin"), 1)
                        dve.wait_ge(mine.sem, mine.at(c, "pin"))
                        dve.tensor_tensor(both_terms, by_dl(p_in[g], 2 * INNER), tok_dl(k_now, 2 * INNER), ALU.mult).then_inc(mine.mark("d_mul"), 1)
                        dve.wait_ge(pe.sem, pe.at(c, "sq"))
                        dve.tensor_reduce(m_q[g], over_a(queries[:, 0:ROWS]), AX.X, ALU.max).then_inc(mine.mark("qmax"), 1)
                        dve.wait_ge(mine.sem, mine.at(c, "qmax"))
                        dve.tensor_tensor(grid(e_q[g]), grid(queries[:, 0:ROWS]), per_l(m_q[g]), ALU.subtract).then_inc(mine.mark("qsub"), 1)
                        yield
                        dve.wait_ge(act.sem, act.at(c, "eq"))
                        dve.tensor_reduce(z_q[g], over_a(e_q[g]), AX.X, ALU.add).then_inc(mine.mark("qsum"), 1)
                        dve.wait_ge(pe.sem, pe.at(c, "d"))
                        dve.tensor_tensor(win1[g], win[g], d_in[:, 0:ROWS], ALU.add).then_inc(mine.mark("win1"), 1)
                        dve.wait_ge(mine.sem, mine.at(c, "qsum"))
                        dve.reciprocal(r_q[g], z_q[g]).then_inc(mine.mark("qrec"), 1)
                        dve.wait_ge(mine.sem, mine.at(c, "win1"))
                        dve.tensor_tensor(cube(t_mul[g][:, 0:PROD]), by_ld(win1[g]), tok_ld(k_now), ALU.mult).then_inc(mine.mark("a1_mul"), 1)
                        dve.wait_ge(mine.sem, mine.at(c, "qrec"))
                        dve.wait_ge(pool.sem, pool.before(c, "o_mul"))
                        dve.tensor_tensor(grid(q_hat[g]), grid(e_q[g]), per_l(r_q[g]), ALU.mult).then_inc(mine.mark("qh"), 1)
                        dve.wait_ge(pool.sem, pool.at(c, "sq_mul"))
                        dve.tensor_tensor(win[g], win1[g], d_in[:, ROWS:2 * ROWS], ALU.add).then_inc(mine.mark("win"), 1)
                        dve.wait_ge(mine.sem, mine.at(c, "a1_mul"))
                        dve.tensor_reduce(s_2[g], summands(t_mul[g][:, 0:PROD]), AX.X, ALU.add).then_inc(mine.mark("a1"), 1)
                    yield

                staggered(states)

            recurrence_done(dve)
            for s in SLOTS:
                dve.memset(c_h[s][:, :, 0:1], 0.0).then_inc(c_ready, 1)
            dve.wait_ge(c_ready, len(SLOTS))

            def out_centre(pe_s, mine, n, s):
                for k in range(KT):
                    dve.wait_ge(pe_s.sem, pe_s.at(n, f"mean{s}{k}"))
                    dve.tensor_tensor(c_o[s][:, k], c_o[s][:, k], bank[3 + 4 * k][:], ALU.subtract).then_inc(mine.mark(f"oc{s}{k}"), 1)

            def out_var(pe_s, mine, n, s):
                for k in range(KT):
                    dve.wait_ge(pe_s.sem, pe_s.at(n, f"var{s}{k}"))
                    dve.tensor_copy(c_ostd[s][:, k], bank[3 + 4 * k][:]).then_inc(mine.mark(f"ov{s}{k}"), 1)

            def out_gated(act_s, mine, n, s):
                dve.wait_ge(act_s.sem, act_s.at(n, f"orstd{s}"))
                dve.scalar_tensor_tensor(out=c_oz[s], in0=c_o[s], scalar=lngb_sb[:, 0:1], in1=c_ostd[s], op0=ALU.mult, op1=ALU.mult).then_inc(mine.mark(f"on{s}"), 1)
                dve.wait_ge(mine.sem, mine.at(n, f"on{s}"))
                dve.scalar_tensor_tensor(out=c_oz[s], in0=c_oz[s], scalar=lngb_sb[:, 1:2], in1=c_gate[s], op0=ALU.add, op1=ALU.mult).then_inc(mine.mark(f"oz{s}"), 1)

            def pick(mine, s, b):
                dve.tensor_copy(c_pick[s][0:BATCH], ident[0:BATCH, bass.ds(b, 1)].broadcast_to([BATCH, P])).then_inc(mine.mark(f"pick{s}"), 1)

            for s in SLOTS:
                out_centre(first_pe, first_dve, 0, s)
            for s in SLOTS:
                out_var(first_pe, first_dve, 0, s)
            for s in SLOTS:
                out_gated(first_act, first_dve, 0, s)
            for s in SLOTS:
                pick(first_dve, s, s)
            with dve.Fori(0, BATCH // 2) as i:
                B = lambda s, j: bank[4 * s + j]

                def residual(stage, s, pe_step, banks):
                    for a in range(2):
                        dve.wait_ge(c_pe.sem, c_pe.at(i, f"{pe_step}{s}{a}"))
                        half = slice(2 * a, 2 * a + 2)
                        dve.tensor_tensor(c_x[s][:, half], c_x[s][:, half],
                                          B(s, banks[a])[:].rearrange("p (t d) -> p t d", t=2), ALU.add).then_inc(c_dve.mark(f"x{stage}{s}{a}"), 1)

                def statistics(stage, s):
                    for t in range(TT):
                        dve.wait_ge(c_dve.sem, c_dve.at(i, f"x{stage}{s}{t // 2}"))
                        dve.bn_stats(c_stat[s][:, t], c_x[s][:, t]).then_inc(c_dve.mark(f"st{stage}{s}{t}"), 1)
                    dve.wait_ge(c_dve.sem, c_dve.at(i, f"st{stage}{s}{TT - 1}"))
                    hold(dve)
                    for t in range(TT):
                        dve.bn_aggr(c_mv[s][:, t], c_stat[s][:, t]).then_inc(c_dve.mark(f"ag{stage}{s}{t}"), 1)

                def normalise(stage, s):
                    dve.wait_ge(c_act.sem, c_act.at(i, f"std{stage}{s}"))
                    dve.reciprocal(c_rstd[s], c_std[s]).then_inc(c_dve.mark(f"rec{stage}{s}"), 1)
                    dve.wait_ge(c_dve.sem, c_dve.at(i, f"rec{stage}{s}"))
                    for t in range(TT):
                        dve.tensor_scalar(c_xhat[s][:, t], c_x[s][:, t], c_mv[s][:, t, 0:1], c_rstd[s][:, t:t + 1],
                                          ALU.subtract, ALU.mult).then_inc(c_dve.mark(f"xh{stage}{s}{t}"), 1)

                def norm(stage, pe_step, banks):
                    residual(stage, 0, pe_step, banks)
                    statistics(stage, 0)
                    residual(stage, 1, pe_step, banks)
                    normalise(stage, 0)
                    statistics(stage, 1)
                    normalise(stage, 1)

                for s in SLOTS:
                    b = i * 2 + s
                    mods = modc[:, N_MOD // 2 * KT:, bass.ds(b, 1)].rearrange("p (a c) o -> p a (c o)", c=N_MOD // 2 * KT)
                    dve.wait_ge(c_act.sem, c_act.before(i, f"h3{s}{KT - 1}"))
                    dve.tensor_copy(c_modb[s], mods[:, :, 0:2 * KT]).then_inc(c_dve.mark(f"modb{s}"), 1)
                gate = lambda s, layer, j, p: B(s, layer)[0:p, j * DIM:(j + 1) * DIM]
                both = lambda s, layer, j: gate(s, layer, j, P).unsqueeze(1).broadcast_to([P, KT, DIM])
                for s in SLOTS:
                    dve.wait_ge(c_pe.sem, c_pe.at(i, f"gb{s}0"))
                    dve.tensor_tensor(c_wo[s], w_out_sb[:], both(s, 0, 0), ALU.mult).then_inc(c_dve.mark(f"wo{s}"), 1)
                for s in SLOTS:
                    dve.wait_ge(c_pe.sem, c_pe.at(i, f"gb{s}1"))
                    dve.tensor_tensor(c_v2[s][0:RANK + 1], v2_sb[:], gate(s, 0, 1, RANK + 1), ALU.mult).then_inc(c_dve.mark(f"v2{s}"), 1)
                    dve.tensor_tensor(c_wp[s], w_proj_sb[:], both(s, 1, 0), ALU.mult).then_inc(c_dve.mark(f"wp{s}"), 1)
                    dve.tensor_tensor(c_wv[s], w_rkv_sb[:, 2], both(s, 1, 1), ALU.mult).then_inc(c_dve.mark(f"wv{s}"), 1)
                for s in SLOTS:
                    dve.wait_ge(c_loaded[s], 16 * (i + 1))
                    hold(dve)
                norm(1, "wo", (2, 3))
                for s in SLOTS:
                    out_centre(c_pe, c_dve, i, s)
                for s in SLOTS:
                    out_var(c_pe, c_dve, i, s)
                norm(2, "v2", (1, 2))
                for s in SLOTS:
                    out_gated(c_act, c_dve, i, s)

                def segments(dst, src):
                    blocks = src.rearrange("p (f q) -> p f q", q=QF)
                    return ((dst[:, 2:FRAMES, 0:QF], blocks[:, 0:FRAMES - 2]),
                            (dst[:, 1:FRAMES, QF:2 * QF], blocks[:, 0:FRAMES - 1]),
                            (dst[:, :, 2 * QF:3 * QF], blocks),
                            (dst[:, :, 3 * QF:KEYS], src[:, 0:NGLOB].unsqueeze(1).broadcast_to([P, FRAMES, NGLOB])))

                for s in SLOTS:
                    dve.wait_ge(c_pe.sem, c_pe.at(i, f"vt{s}1"))
                    dve.tensor_copy(c_vt[s][:, 2:4], B(s, 2)[:].rearrange("p (t d) -> p t d", t=2)).then_inc(c_dve.mark(f"vt{s}1"), 1)
                for s in SLOTS:
                    dve.wait_ge(c_pe.sem, c_pe.at(i, f"q{s}1"))
                    for j in range(4):
                        dve.tensor_scalar(c_qb[s][:, 1, :, j * QF:(j + 1) * QF], B(s, 0)[:].rearrange("p (f q) -> p f q", q=QF),
                                          parity[:, j:j + 1], None, ALU.mult).then_inc(c_dve.mark(f"qb{s}1{j}"), 1)
                for s in SLOTS:
                    dve.wait_ge(c_pe.sem, c_pe.at(i, f"k{s}0"))
                    for g, (dst, src) in enumerate(segments(c_k[s][:, 0], B(s, 1)[:])):
                        dve.tensor_copy(dst, src).then_inc(c_dve.mark(f"ks{s}{g}"), 1)

                quads = lambda t: t.rearrange("p (t k) -> p t k", t=2)
                for t in range(len(ATT) + Y_LAG + 1):
                    if t < len(ATT):
                        f, s = ATT[t]
                        dve.wait_ge(c_pe.sem, c_pe.at(i, f"s{s}{f}"))
                        sc = psum[:, 4 * s:4 * s + 2, 0:KT * KEYS].rearrange("p t (k y) -> p t k y", k=KT)
                        if f > 0:
                            dve.wait_ge(c_act.sem, c_act.at(i, f"exp{s}{f - 1}u{QUADS - 1}"))
                        dve.tensor_reduce(quads(c_max[s]), sc, AX.X, ALU.max, negate=True).then_inc(c_dve.mark(f"max{s}{f}"), 1)
                    if 0 <= t - 1 < len(ATT):
                        f, s = ATT[t - 1]
                        dve.wait_ge(c_act.sem, c_act.at(i, f"exp{s}{f}u{QUADS - 1}"))
                        dve.tensor_reduce(c_sum[s], c_soft[s][:, f % 2], AX.X, ALU.add).then_inc(c_dve.mark(f"sum{s}{f}"), 1)
                        dve.wait_ge(c_dve.sem, c_dve.at(i, f"sum{s}{f}"))
                        if f > 0:
                            dve.wait_ge(c_pool.sem, c_pool.at(i, f"prob{s}{f - 1}"))
                        dve.reciprocal(c_rec[s], c_sum[s]).then_inc(c_dve.mark(f"arec{s}{f}"), 1)
                    if 0 <= t - Y_LAG < len(ATT) and ends_quarter(ATT[t - Y_LAG][0]):
                        f, s = ATT[t - Y_LAG]
                        quarter = f // QTR
                        if quarter == 0:
                            dve.wait_ge(v_framed[s], 16 * FRAMED * (i + 1))
                        dve.wait_ge(c_act.sem, c_act.at(i, f"ye{s}{quarter}"))
                        src = y_bank(s, quarter)[:].rearrange("p (f e q) -> p f e q", e=2, q=QF)[:, :, 1]
                        dve.scalar_tensor_tensor(out=c_y[s][:, quarter].rearrange("p k (f q) -> p (k f) q", q=QF), in0=src, scalar=parity[:, 5:6],
                                                 in1=c_yeven[s], op0=ALU.mult, op1=ALU.add).then_inc(c_dve.mark(f"y{s}{quarter}"), 1)
                norm(3, "wp", (0, 1))
                dve.wait_ge(c_act.sem, c_act.at(i, f"h30{KT - 1}"))
                dve.tensor_tensor(c_d[0], c_h[0][:, :, 1:TOK + 1], c_h[0][:, :, 0:TOK], ALU.subtract).then_inc(c_dve.mark("d0"), 1)
                for s in SLOTS:
                    if s == 0:
                        dve.wait_ge(c_dve.sem, c_dve.at(i, "d0"))
                    else:
                        dve.wait_ge(c_pool.sem, c_pool.at(i, "d1"))
                    for m, (name, dst) in enumerate((("xr", c_xr[s]), ("xk", c_xk[s]))):
                        for k in range(KT):
                            dve.scalar_tensor_tensor(out=dst[:, k], in0=c_d[s][:, k], scalar=mu_sb[:, m, k:k + 1],
                                                     in1=c_h[s][:, k, 0:TOK], op0=ALU.mult, op1=ALU.add).then_inc(c_dve.mark(f"{name}{s}{k}"), 1)
                for s in SLOTS:
                    pick(c_dve, s, i * 2 + s + AHEAD)
                for s in SLOTS:
                    for a in range(2):
                        dve.wait_ge(c_pe.sem, c_pe.at(i, f"vv{s}{a}"))
                        half = slice(2 * a, 2 * a + 2)
                        dve.tensor_tensor(c_rv[s][:, half], c_r[s][:, half], B(s, a)[:].rearrange("p (t d) -> p t d", t=2), ALU.mult).then_inc(c_dve.mark(f"rv{s}{a}"), 1)


def kernel(**inputs):
    import concourse.bacc as bacc
    from concourse.bass_utils import run_bass_kernel_spmd

    def a(name):
        return np.asarray(inputs[name])

    def turned(name):
        return np.ascontiguousarray(a(name).T)

    def row(name):
        return np.ascontiguousarray(a(name).reshape(1, -1))

    part = np.arange(P)
    ident = np.eye(P, dtype=np.float32)
    blocks = (part[:, None] // HD == part[None, :] // HD).astype(np.float32) / HD
    parity = np.zeros((P, 7), np.float32)
    for j in range(4):
        parity[:, j] = (part // HD % 4 == j) / np.sqrt(HD)
    parity[:, 4] = part // HD % 2 == 0
    parity[:, 5] = part // HD % 2 == 1
    parity[:, 6] = EPS
    q, key = part[:, None] % QF, np.arange(KEYS)[None, :]
    local = (key <= q + WINDOW) & (key > q) & (key < WINDOW + QF)
    glob = key >= WINDOW + QF
    seen = [local & (key >= WINDOW), (local & (key >= QF)) | ((key >= QF) & (key < QF + NGLOB)),
            local | (key < NGLOB), local | glob]
    mask = np.stack([np.tile(np.where(m, 0.0, MASKED), (1, KT)) for m in seen], axis=1).astype(mybir.dt.np(BF16))

    arrays = {
        "x": a("L0_attn_hidden_states"),
        "w_in": np.concatenate([turned(f"L0_attn_{n}") for n in ("Wq", "Wk", "Wv", "Wg", "Wlr")], axis=1),
        "taps": np.concatenate([a(f"L0_attn_{n}") for n in ("cq", "ck", "cv")], axis=1),
        "w_out": turned("L0_attn_Wo"),
        "ln_g": np.tile(a("L0_attn_ln_g"), P // HD).reshape(P, 1),
        "ln_b": np.tile(a("L0_attn_ln_b"), P // HD).reshape(P, 1),
        "w_in_init": a("L0_attn_W_in_init")[0],
        "w_out_init": a("L0_attn_W_out_init")[0],
        "u1": a("L0_ffn_U1"), "v1": a("L0_ffn_V1"), "b1": row("L0_ffn_b1"),
        "u2": a("L0_ffn_U2"), "v2": a("L0_ffn_V2"), "b2": row("L0_ffn_b2"),
        "cond": np.stack([turned("L0_c"), turned("L1_c")]),
        "wmod": np.stack([a("L0_wmod"), a("L1_wmod")]),
        "w_attn": turned("L1_attn_w_attn"), "w_proj": turned("L1_attn_w_proj"),
        "w_r": turned("L1_ffn_W_r"), "w_k": turned("L1_ffn_W_k"), "w_v": turned("L1_ffn_W_v"),
        "mu": np.stack([a("L1_ffn_mu_r").reshape(KT, P).T, a("L1_ffn_mu_k").reshape(KT, P).T], axis=1),
        "ident_c": ident, "blocks_c": blocks, "parity_c": parity, "mask_c": mask,
    }
    arrays = {n: np.ascontiguousarray(v) for n, v in arrays.items()}
    nc = bacc.Bacc("TRN2", target_bir_lowering=False, num_devices=1)
    args = [nc.dram_tensor(n, v.shape, mybir.dt.from_np(v.dtype), kind="ExternalInput").ap() for n, v in arrays.items()]
    args.append(nc.dram_tensor("out", (BATCH, TOK, DIM), F32, kind="ExternalOutput").ap())
    adaln_two_layers(nc, *args)
    r = run_bass_kernel_spmd(nc, [arrays], core_ids=[0])
    return r.results[0]["out"]
```

```python
from contextlib import ExitStack

import numpy as np
import concourse.bass as bass
from concourse import mybir

P = 128
BATCH, TOK, DIM = 16, 512, 256
HEADS, HD = 16, 16
KT = DIM // P
TT = TOK // P
INNER, CHUNK, TAPS = 4, 16, 4
D_FF, RANK = 1024, 64
FT = D_FF // P
WINDOW, NGLOB = 64, 4
GROUP_B = P // HEADS
GROUPS = BATCH // GROUP_B
BLOCK = 64
BLOCKS = TOK // BLOCK
CPB = BLOCK // CHUNK
CPR = 2 * CPB
ROUNDS = TOK // (CPR * CHUNK)
QF = 32
FRAMES = TOK // QF
HF, QTR = FRAMES // 2, FRAMES // 4
KEYS = WINDOW + QF + NGLOB
QUADS = HEADS // 4
ROWS = INNER * CHUNK
PROD = ROWS * HD
BASE_LR = 0.001
EPS = 1e-5
MASKED = -3.0e38
N_MOD = 6
LAYERS = 2
AHEAD = 2
ARENA = 36816

ALU = mybir.AluOpType
ACT = mybir.ActivationFunctionType
AX = mybir.AxisListType
F32 = mybir.dt.float32
BF16 = mybir.dt.bfloat16


class Steps:

    def __init__(self, sem, names):
        self.sem, self.names, self.marked = sem, list(names), 0
        self.index = {name: k for k, name in enumerate(self.names)}
        assert len(self.index) == len(self.names)

    def mark(self, name):
        assert self.names[self.marked % len(self.names)] == name, (self.names[self.marked % len(self.names)], name)
        self.marked += 1
        return self.sem

    def at(self, n, name):
        return (n + 1) * len(self.names) + self.index[name] + 1

    def before(self, n, name):
        return n * len(self.names) + self.index[name] + 1


QKV = ["q0", "q1", "k0", "k1", "v0", "v1"]


def adaln_two_layers(nc, x, w_in, taps, w_out, ln_g, ln_b, w_in_init, w_out_init, u1, v1, b1, u2, v2, b2,
                     cond, wmod, w_attn, w_proj, w_r, w_k, w_v, mu, ident_c, blocks_c, parity_c, mask_c, out):
    ctx = ExitStack()
    with ctx:
        def sb(name, shape, dt=F32):
            return ctx.enter_context(nc.sbuf_tensor(name, shape, dt))

        def sem(name):
            return ctx.enter_context(nc.semaphore(name))

        psum = ctx.enter_context(nc.psum_tensor("psum", [P, 8, 512], F32))
        bank = [psum[:, i] for i in range(8)]

        def dram(name, shape):
            return nc.dram_tensor(name, shape, F32, kind="Internal").ap()

        qkv_d = [dram(f"{c}_d", [BLOCKS, BATCH, DIM, BLOCK]) for c in "qkv"]
        gate_d = dram("gate_d", [BATCH + AHEAD, DIM, TOK])
        lr_d = dram("lr_d", [BATCH, 2 * HEADS, TOK])
        o_d = dram("o_d", [BATCH + AHEAD, DIM, TOK])

        w_in_sb = sb("w_in_sb", [P, KT, 4 * DIM + 2 * HEADS])
        taps_sb = sb("taps_sb", [P, KT, 3 * TAPS])
        w_out_sb = sb("w_out_sb", [P, KT, DIM])
        lngb_sb = sb("lngb_sb", [P, 2])
        u1_sb = sb("u1_sb", [P, KT, RANK])
        v1_sb = sb("v1_sb", [P, D_FF])
        b1_sb = sb("b1_sb", [P, FT])
        u2_sb = sb("u2_sb", [P, FT, RANK])
        v2_sb = sb("v2_sb", [P, DIM])
        b2_sb = sb("b2_sb", [P, DIM])
        w_attn_sb = sb("w_attn_sb", [P, KT, 3 * DIM])
        w_proj_sb = sb("w_proj_sb", [P, KT, DIM])
        w_rkv_sb = sb("w_rkv_sb", [P, 3, KT, DIM])
        mu_sb = sb("mu_sb", [P, 2, KT])
        ident = sb("ident", [P, P])
        identb = sb("identb", [P, P], BF16)
        mean16 = sb("mean16", [P, P])
        parity = sb("parity", [P, 7])
        mask_sb = sb("mask_sb", [P, 4, KT * KEYS], BF16)
        state0 = sb("state0", [P, 2, ROWS])
        modc = sb("modc", [P, LAYERS * N_MOD * KT, BATCH])
        gates_row = sb("gates_row", [BATCH, 2 * LAYERS * DIM])

        arena = sb("arena", [P, ARENA])
        top = [0]

        def carve(*shape):
            size = int(np.prod(shape))
            ap = arena[:, top[0]:top[0] + size]
            top[0] += size
            assert top[0] <= ARENA, top[0]
            if len(shape) == 2:
                ap = ap.rearrange("p (a b) -> p a b", a=shape[0])
            if len(shape) == 3:
                ap = ap.rearrange("p (a b c) -> p a b c", a=shape[0], b=shape[1])
            return ap


        wmod_sb = carve(LAYERS, KT, N_MOD * DIM)
        cond_sb = carve(LAYERS, KT, BATCH)
        cond_silu = carve(LAYERS, KT, BATCH)
        g_raw = carve(2 * LAYERS * DIM)
        g_sign = carve(2 * LAYERS * DIM)
        g_size = carve(2 * LAYERS * DIM)

        top[0] = 0
        a_x = carve(TT, DIM)
        a_xhat = carve(TT, DIM)
        a_stat = carve(TT, 6)
        a_mv = carve(TT, 2)
        a_std = carve(TT)
        a_rstd = carve(TT)
        a_modb = carve(2 * KT)
        a_h = carve(KT, TOK)
        a_acc = carve(6, TOK)
        a_gate = carve(KT, TOK)
        a_lr = carve(TOK)
        a_silu = carve(6, TOK)
        a_unit = carve(2 * KT, TOK)
        a_sq = carve(2 * KT, TOK)
        a_rn = carve(2 * KT, TOK)

        top[0] = 0
        PAIRS = range(GROUPS)

        def of_group(*shape):
            return [carve(*shape) for _ in PAIRS]

        scan_keep = carve(PROD)
        lr_fin = carve(GROUPS * 2, CHUNK + TOK)
        q_blk, k_blk, v_blk, o_blk = ([of_group(HD, BLOCK) for _ in range(2)] for _ in range(4))
        t_mul = of_group(2 * PROD)
        t_run, t_g1, t_g2, t_q = (of_group(PROD) for _ in range(4))
        t_q8 = of_group(PROD // 2)
        win, win1, wout2, wout, s_a, s_2, g_1, g_2 = (of_group(ROWS) for _ in range(8))
        e_k, e_p, p_out1, k_hat, e_q, q_hat, e_2, p_2 = (of_group(ROWS) for _ in range(8))
        e_b, p_in = of_group(2 * ROWS), of_group(2 * ROWS)
        m_k, z_k, r_k, rl_k, m_q, z_q, r_q = (of_group(CHUNK) for _ in range(7))
        m_p, z_p, r_p, m_2, z_2, r_2 = (of_group(INNER) for _ in range(6))
        m_b, z_b, r_b = (of_group(2 * INNER) for _ in range(3))
        lr_raw, lr_tmp = (t.rearrange("p (i t) -> p i t", i=2 * GROUPS) for t in t_mul)

        top[0] = 0
        SLOTS = range(2)
        c_x = [carve(TT, DIM) for _ in SLOTS]
        c_xy = [carve(TT * DIM) for _ in SLOTS]
        c_xhat = [t.rearrange("p (a b) -> p a b", a=TT) for t in c_xy]
        c_y = [t.rearrange("p (t k q) -> p t k q", t=TT, k=KT) for t in c_xy]
        c_stat = [carve(TT, 6) for _ in SLOTS]
        c_mv = [carve(TT, 2) for _ in SLOTS]
        c_std = [carve(TT) for _ in SLOTS]
        c_rstd = [carve(TT) for _ in SLOTS]
        c_modb = [carve(3, 2 * KT) for _ in SLOTS]
        c_pick = [carve(P) for _ in SLOTS]
        c_h = [carve(KT, TOK + 1) for _ in SLOTS]
        c_vt = c_xhat
        c_wo = [carve(KT, DIM) for _ in SLOTS]
        c_wp = [carve(KT, DIM) for _ in SLOTS]
        c_wv = [carve(KT, DIM) for _ in SLOTS]
        c_v2 = carve(DIM)
        c_b2 = [carve(DIM) for _ in SLOTS]
        c_soft = [carve(2, 4, KEYS) for _ in SLOTS]
        c_max, c_sum, c_rec = ([carve(4) for _ in SLOTS] for _ in range(3))
        c_pt = [carve(4 * P) for _ in SLOTS]
        c_yeven = [carve(KT * QTR, QF) for _ in SLOTS]
        base = top[0]
        c_p, c_qr = carve(TOK), carve(TOK)
        c_f = [carve(3, TOK) for _ in SLOTS]
        top[0] = base
        c_qb = [carve(KT, FRAMES, 4 * QF) for _ in SLOTS]
        keys_at = top[0]
        c_k = [carve(KT, FRAMES, KEYS) for _ in SLOTS]
        values_at = top[0]
        c_v = [carve(FRAMES, DIM) for _ in SLOTS]
        top[0] = base
        c_d = [carve(KT, TOK) for _ in SLOTS]
        c_xr = [carve(KT, TOK) for _ in SLOTS]
        c_xk = [carve(KT, TOK) for _ in SLOTS]
        c_r = [carve(TT, DIM) for _ in SLOTS]
        c_kk = [carve(KT, TOK) for _ in SLOTS]
        c_rv = [carve(TT, DIM) for _ in SLOTS]

        top[0] = keys_at
        c_o, c_gate, c_ostd = ([carve(KT, TOK) for _ in SLOTS] for _ in range(3))
        assert top[0] <= values_at
        top[0] = values_at
        c_xin = [carve(TT, DIM) for _ in SLOTS]
        c_oz = [w_in_sb[:, s, 0:KT * TOK].rearrange("p (k t) -> p k t", k=KT) for s in SLOTS]

        held = sem("held")

        def hold(eng):
            eng.sem_inc(held, 1)

        cond_loaded, wmod_loaded = sem("cond_loaded"), sem("wmod_loaded")
        consts_loaded = sem("consts_loaded")
        weights_loaded = sem("weights_loaded")
        su_act = Steps(sem("su_act"), ["silu", "modc", "raw0", "raw1"])
        su_pe = Steps(sem("su_pe"), ["mod", "gate0", "gate1"])
        su_dve = Steps(sem("su_dve"), ["identb", "plus1", "plus2", "plus3", "plus4", "tap", "side", "sign", "size", "gates"])

        x_loaded = sem("x_loaded")
        a_stored = {t: sem(f"stored_{t}") for t in QKV + ["g0", "g1", "lr"]}
        ln_dve = Steps(sem("ln_dve"), [f"st{t}" for t in range(TT)] + [f"ag{t}" for t in range(TT)] + [f"xh{t}" for t in range(TT)])
        ln_act = Steps(sem("ln_act"), ["modb", "ln", "rstd", "h0", "h1"])
        ln_pe = Steps(sem("ln_pe"), ["t0", "t1"])
        pr_pe = Steps(sem("pr_pe"), QKV + ["g0", "g1", "lr"])
        pr_act = Steps(sem("pr_act"), [f"tap{t}" for t in range(6)] + [f"silu{t}" for t in range(4)] + ["g0", "silu4", "g1", "lr", "silu5"])
        le_dve = Steps(sem("le_dve"), [f"sq{t}" for t in range(4)])
        le_pool = Steps(sem("le_pool"), [f"unit{t}" for t in range(4)])
        SS_BANKS = (5, 6, 4, 7)
        le_pe = Steps(sem("le_pe"), [f"ss{t}" for t in range(4)])
        le_act = Steps(sem("le_act"), [f"ln{t}" for t in range(4)] + [f"rn{t}" for t in range(4)])
        pr_dve = Steps(sem("pr_dve"), [f"c{t}{j}" for t in range(6) for j in (1, 2, 3)])

        blk_loaded = [[sem(f"blk_loaded{b}{g}") for g in PAIRS] for b in range(2)]
        o_stored = [[sem(f"o_stored{b}{g}") for g in PAIRS] for b in range(2)]
        lr_loaded = sem("lr_loaded")
        scan_ready = Steps(sem("scan_ready"), ["ones", "zeros"])
        st_dve = Steps(sem("st_dve"), ["pad", "lr"] + [f"{n}{g}" for g in PAIRS for n in ("no_v", "no_s2", "in", "out")])
        st_act = Steps(sem("st_act"), ["abs", "exp", "ln"])
        re_dve = [Steps(sem(f"re_dve{g}"), [
            "a0_mul", "max2", "a0", "sub2", "pmax", "kmax", "psub", "ksub", "sum2", "psum", "ksum",
            "rec2", "prec", "krec", "p2", "klr", "p1", "kh",
            "g2s", "wout", "g1s", "carry", "run", "wout2", "b1_mul", "b2_mul",
            "bmax", "bsub", "bsum", "brec", "pin", "d_mul", "qmax", "qsub",
            "qsum", "win1", "qrec", "a1_mul", "qh", "win", "a1"]) for g in PAIRS]
        re_pool = [Steps(sem(f"re_pool{g}"), ["g2", "g1", "kv", "sq_mul", "o_mul", "o2", "o1"]) for g in PAIRS]
        re_act = [Steps(sem(f"re_act{g}"), ["e2", "ep", "ek", "eb", "eq"]) for g in PAIRS]
        re_pe = [Steps(sem(f"re_pe{g}"), ["b", "sq", "d"]) for g in PAIRS]
        PHASES = 3 * CPR + 1

        def staggered(program):
            programs = [program(g) for g in PAIRS]
            for t in range(PHASES + GROUPS - 1):
                for g in PAIRS:
                    if 0 <= t - g < PHASES:
                        next(programs[g])

        c_ready = sem("c_ready")
        c_loaded = [sem(f"c_loaded{s}") for s in SLOTS]
        o_loaded = [sem(f"o_loaded{s}") for s in SLOTS]
        ahead_filled = sem("ahead_filled")
        out_stored = [sem(f"out_stored{s}") for s in SLOTS]
        FRAMED = 3 * TT + 1
        v_framed = [sem(f"v_framed{s}") for s in SLOTS]
        ATT = [(f, s) for f in range(FRAMES) for s in SLOTS]

        T_LAG, PV_LAG, YE_LAG, Y_LAG = 3, 4, 5, 6
        WARM = {"s0": 9, "t0": 6, "t1": 4, "pv0": 4, "t2": 2, "pv1": 2, "norm1": 10, "u10": 6, "u11": 6, "norm2": 22, "vt0": 8, "vt1": 6, "norm3": 10, "turn30": 6, "turn31": 8, "pv28": 1, "t29": 1, "pv29": 1, "t30": 2, "pv30": 2, "t31": 2, "pv31": 2}
        TURNED, Y_BANKS = 2, (3, 6, 7)

        def y_bank(s, quarter):
            return bank[Y_BANKS[(len(SLOTS) * quarter + s) % len(Y_BANKS)]]

        def ends_quarter(f):
            return f % QTR == QTR - 1

        ln_names = lambda i, s: [f"st{i}{s}{t}" for t in range(TT)] + [f"ag{i}{s}{t}" for t in range(TT)]
        xh_names = lambda i, s: [f"rec{i}{s}"] + [f"xh{i}{s}{t}" for t in range(TT)]

        def norm_dve(i):
            return ([f"x{i}00", f"x{i}01"] + ln_names(i, 0) + [f"x{i}10", f"x{i}11"] + xh_names(i, 0)
                    + ln_names(i, 1) + xh_names(i, 1))

        def norm_act(i):
            return [f"std{i}0", f"h{i}00", f"std{i}1", f"h{i}01"] + [f"h{i}1{k}" for k in range(KT)]

        def each(*fs):
            return [n for s in SLOTS for f in fs for n in f(s)]

        def att_pe():
            names = []
            for t in range(len(ATT) + PV_LAG):
                names += [f"{what}{s}{f}" for what, lag in (("s", 0), ("t", T_LAG), ("pv", PV_LAG)) if 0 <= t - lag < len(ATT)
                          for f, s in [ATT[t - lag]]]
            return names

        def att_act():
            names = []
            for t in range(len(ATT) + YE_LAG + 1):
                if t < len(ATT):
                    names += [f"exp{ATT[t][1]}{ATT[t][0]}u{u}" for u in range(QUADS)]
                if 0 <= t - T_LAG < len(ATT):
                    names.append(f"pt{ATT[t - T_LAG][1]}{ATT[t - T_LAG][0]}")
                if 0 <= t - YE_LAG < len(ATT) and ends_quarter(ATT[t - YE_LAG][0]):
                    names.append(f"ye{ATT[t - YE_LAG][1]}{ATT[t - YE_LAG][0] // QTR}")
            return names

        def att_dve():
            names = []
            for t in range(len(ATT) + Y_LAG + 1):
                for what, lag in (("max", 0), ("sum", 1), ("arec", 1)):
                    if 0 <= t - lag < len(ATT):
                        names.append(f"{what}{ATT[t - lag][1]}{ATT[t - lag][0]}")
                if 0 <= t - Y_LAG < len(ATT) and ends_quarter(ATT[t - Y_LAG][0]):
                    names.append(f"y{ATT[t - Y_LAG][1]}{ATT[t - Y_LAG][0] // QTR}")
            return names

        out_dve = [f"{what}{s}{k}" for what in ("oc", "ov") for s in SLOTS for k in range(KT)], [f"{what}{s}" for s in SLOTS for what in ("on", "oz")]
        out_act = [f"oln{s}" for s in SLOTS], [f"orstd{s}" for s in SLOTS]
        first_dve = Steps(sem("first_dve"), out_dve[0] + out_dve[1] + each(lambda s: [f"pick{s}"]))
        first_act = Steps(sem("first_act"), out_act[0] + out_act[1])
        first_pe = Steps(sem("first_pe"), [f"{what}{s}{k}" for what in ("mean", "var") for s in SLOTS for k in range(KT)])
        first_pool = Steps(sem("first_pool"), [f"osq{s}" for s in SLOTS])
        c_dve = Steps(sem("c_dve"),
            each(lambda s: [f"modb{s}"]) + each(lambda s: [f"wo{s}"]) + each(lambda s: [f"v2{s}", f"b2{s}", f"wp{s}", f"wv{s}"])
            + norm_dve(1) + out_dve[0] + each(lambda s: [f"qr{s}"]) + norm_dve(2) + out_dve[1]
            + each(lambda s: [f"vt{s}1"]) + each(lambda s: [f"qb{s}1{j}" for j in range(4)])
            + each(lambda s: [f"ks{s}{g}" for g in range(4)]) + att_dve()
            + norm_dve(3) + ["d0"] + each(lambda s: [f"{m}{s}{k}" for m in ("xr", "xk") for k in range(KT)])
            + each(lambda s: [f"pick{s}"]) + each(lambda s: [f"rv{s}0", f"rv{s}1"]))
        c_act = Steps(sem("c_act"),
            norm_act(1)
            + each(lambda s: [f"p{s}"]) + [f"gelu{s}{f}" for f in range(FT) for s in SLOTS]
            + out_act[0] + out_act[1] + norm_act(2)
            + each(lambda s: [f"vt{s}0"]) + each(lambda s: [f"qb{s}0{j}" for j in range(4)])
            + each(lambda s: [f"ks{s}{g}" for g in range(4)]) + att_act()
            + norm_act(3)
            + each(lambda s: [f"r{s}0", f"r{s}1", f"kk{s}0", f"kk{s}1"]))

        UP_BANKS = 2
        OUT_AT = {0: ("mean", 0), 1: ("mean", 1), 3: ("var", 0), 4: ("var", 1)}

        def ffn_pe():
            names = [f"v1{s}{f}" for f in range(UP_BANKS) for s in SLOTS]
            for f in range(FT):
                names += [f"u2{s}{f}" for s in SLOTS]
                if f + UP_BANKS < FT:
                    names += [f"v1{s}{f + UP_BANKS}" for s in SLOTS]
                names += [f"{what}{r}{k}" for k in range(KT) for what, r in [OUT_AT.get(f, ("", 0))] if what]
            return names

        c_pe = Steps(sem("c_pe"),
            each(lambda s: [f"gb{s}0", f"gb{s}1"]) + each(lambda s: [f"wo{s}0", f"wo{s}1"])
            + each(lambda s: [f"turn1{s}0", f"turn1{s}1", f"u1{s}"]) + ffn_pe()
            + [f"v2{s}{a}" for a in range(2) for s in SLOTS]
            + each(lambda s: [f"turn2{s}0", f"turn2{s}1", f"vt{s}0", f"vt{s}1"]) + each(lambda s: [f"q{s}0", f"q{s}1"])
            + each(lambda s: [f"k{s}0", f"k{s}1"]) + att_pe()
            + each(lambda s: [f"wp{s}0", f"wp{s}1"]) + each(lambda s: [f"turn3{s}0", f"turn3{s}1"])
            + each(lambda s: [f"r{s}0", f"r{s}1", f"kk{s}0", f"kk{s}1"]) + each(lambda s: [f"vv{s}0", f"vv{s}1"]))
        c_pool = Steps(sem("c_pool"),
            [f"{what}{s}" for what in ("x2", "osq") for s in SLOTS] + each(lambda s: [f"pad{s}{j}" for j in range(4)])
            + [f"prob{s}{f}" for f, s in ATT]
            + ["d1"] + each(lambda s: [f"kk{s}0", f"kk{s}1"]) + each(lambda s: [f"x4{s}0", f"x4{s}1"]))

        block = ctx.enter_context(nc.Block())

        def phase_a_done(eng):
            eng.wait_ge(pr_act.sem, pr_act.before(BATCH, "silu5"))
            eng.wait_ge(le_act.sem, le_act.before(BATCH, "rn3"))
            eng.wait_ge(pr_dve.sem, pr_dve.before(BATCH, "c53"))
            eng.wait_ge(le_dve.sem, le_dve.before(BATCH, "sq3"))
            eng.wait_ge(le_pe.sem, le_pe.before(BATCH, "ss3"))
            eng.wait_ge(le_pool.sem, le_pool.before(BATCH, "unit3"))
            for s in a_stored.values():
                eng.wait_ge(s, 16 * BATCH)

        CHUNKS = ROUNDS * CPR

        def recurrence_done(eng):
            for g in PAIRS:
                eng.wait_ge(re_dve[g].sem, re_dve[g].before(CHUNKS, "a1"))
                eng.wait_ge(re_pool[g].sem, re_pool[g].before(CHUNKS, "o1"))
                eng.wait_ge(re_act[g].sem, re_act[g].before(CHUNKS, "eq"))
                eng.wait_ge(re_pe[g].sem, re_pe[g].before(CHUNKS, "d"))
                for b in range(2):
                    eng.wait_ge(o_stored[b][g], 16 * ROUNDS)

        @block.sync
        def _(sp):
            sp.dma_start(cond_sb, cond.rearrange("l (k p) b -> p l k b", p=P)).then_inc(cond_loaded, 16)
            for layer in range(LAYERS):
                sp.dma_start(wmod_sb[:, layer], wmod[layer].rearrange("(k p) n -> p k n", p=P)).then_inc(wmod_loaded, 16)
            for dst, src in ((ident[:], ident_c), (mean16[:], blocks_c), (parity[:], parity_c)):
                sp.dma_start(dst, src).then_inc(consts_loaded, 16)
            for dst, src in (
                (w_in_sb[:], w_in.rearrange("(k p) n -> p k n", p=P)),
                (taps_sb[:], taps.rearrange("(k p) n -> p k n", p=P)),
                (w_out_sb[:], w_out.rearrange("(k p) n -> p k n", p=P)),
                (lngb_sb[:, 0:1], ln_g),
                (lngb_sb[:, 1:2], ln_b),
                (u1_sb[:], u1.rearrange("(k p) n -> p k n", p=P)),
                (v1_sb[0:RANK], v1),
                (v1_sb[RANK:P], v1),
                (b1_sb[:], b1),
                (u2_sb[:], u2.rearrange("(k p) n -> p k n", p=P)),
                (v2_sb[0:RANK], v2),
                (v2_sb[RANK:P], v2),
                (b2_sb[:], b2.broadcast_to([P, DIM])),
                (w_attn_sb[:], w_attn.rearrange("(k p) n -> p k n", p=P)),
                (w_proj_sb[:], w_proj.rearrange("(k p) n -> p k n", p=P)),
                (w_rkv_sb[:, 0], w_r.rearrange("(k p) n -> p k n", p=P)),
                (w_rkv_sb[:, 1], w_k.rearrange("(k p) n -> p k n", p=P)),
                (w_rkv_sb[:, 2], w_v.rearrange("(k p) n -> p k n", p=P)),
                (mu_sb[:], mu),
                (mask_sb[:], mask_c),
            ):
                sp.dma_start(dst, src).then_inc(weights_loaded, 16)
            for past in (o_d, gate_d):
                sp.dma_start(past[BATCH:BATCH + AHEAD].rearrange("b d t -> (b d) t"), x[0:AHEAD].rearrange("b (u v) d -> (b u) (v d)", v=TOK // DIM)).then_inc(ahead_filled, 16)
            for g in range(GROUP_B):
                rows = slice(g * HEADS, (g + 1) * HEADS)
                for i, init in enumerate((w_in_init, w_out_init)):
                    sp.dma_start(state0[rows, i].rearrange("p (a d) -> p a d", a=INNER),
                                 init.rearrange("a h d -> h a d")).then_inc(weights_loaded, 16)

            sp.wait_ge(su_pe.sem, su_pe.before(1, "gate1"))
            sp.wait_ge(su_dve.sem, su_dve.before(1, "gates"))

            def load_x(n):
                sp.dma_start(a_x, x[bass.ds(n, 1)].rearrange("o (t p) d -> p (o t) d", p=P)).then_inc(x_loaded, 16)

            def store_qkv(n, t, src):
                dst = qkv_d[t // KT][:, bass.ds(n, 1), (t % KT) * P:(t % KT + 1) * P].rearrange("b o c t -> (o c) b t")
                return sp.dma_start(dst, src[:, t].rearrange("p (b t) -> p b t", b=BLOCKS))

            def store_units(n):
                for t in range(4):
                    sp.wait_ge(le_pool.sem, le_pool.at(n, f"unit{t}"))
                    store_qkv(n, t, a_unit).then_inc(a_stored[QKV[t]], 16)

            def store_rest(n):
                for t in (4, 5):
                    sp.wait_ge(pr_act.sem, pr_act.at(n, f"silu{t}"))
                    store_qkv(n, t, a_silu).then_inc(a_stored[QKV[t]], 16)
                for k in range(KT):
                    sp.wait_ge(pr_act.sem, pr_act.at(n, f"g{k}"))
                    dst = gate_d[bass.ds(n, 1)].rearrange("o c t -> (o c) t")[k * P:(k + 1) * P]
                    sp.dma_start(dst, a_gate[:, k]).then_inc(a_stored[f"g{k}"], 16)
                sp.wait_ge(pr_act.sem, pr_act.at(n, "lr"))
                sp.dma_start(lr_d[bass.ds(n, 1)].rearrange("o c t -> (o c) t"), a_lr[0:2 * HEADS]).then_inc(a_stored["lr"], 16)

            def next_x(n):
                sp.wait_ge(ln_dve.sem, ln_dve.before(n, "xh3"))
                hold(sp)
                load_x(n)

            load_x(0)
            next_x(1)
            next_x(2)
            store_rest(0)
            with sp.Fori(1, BATCH - 2) as n:
                store_units(n - 1)
                next_x(n + 2)
                store_rest(n)
            for n in (BATCH - 2, BATCH - 1):
                store_units(n - 1)
                store_rest(n)
            store_units(BATCH - 1)

            phase_a_done(sp)
            for g in PAIRS:
                sp.dma_start(lr_raw[:, 2 * g:2 * g + 2], lr_d[g * GROUP_B:(g + 1) * GROUP_B].rearrange("b (h i) t -> (b h) i t", i=2)).then_inc(lr_loaded, 16)
            pair = lambda d: d.rearrange("b (h d) t -> (b h) d t", h=HEADS)

            def load_block(n, b):
                for g in PAIRS:
                    for dst, src in ((q_blk, qkv_d[0]), (k_blk, qkv_d[1]), (v_blk, qkv_d[2])):
                        rows = src[bass.ds(n * 2 + b, 1), g * GROUP_B:(g + 1) * GROUP_B].rearrange("o b (h d) t -> (o b h) d t", h=HEADS)
                        sp.dma_start(dst[b][g], rows).then_inc(blk_loaded[b][g], 16)

            def store_block(n, b):
                for g in PAIRS:
                    sp.wait_ge(re_pool[g].sem, re_pool[g].at(n * CPR + b * CPB + CPB - 1, "o1"))
                    sp.dma_start(pair(o_d)[g * P:(g + 1) * P, :, bass.ds((n * 2 + b) * BLOCK, BLOCK)], o_blk[b][g]).then_inc(o_stored[b][g], 16)

            def block_used(n, b):
                for g in PAIRS:
                    sp.wait_ge(re_pool[g].sem, re_pool[g].at(n * CPR + b * CPB + CPB, "g2"))
                    hold(sp)

            load_block(0, 0)
            with sp.Fori(0, ROUNDS - 1) as n:
                block_used(n - 1, 1)
                load_block(n, 1)
                store_block(n, 0)
                block_used(n, 0)
                load_block(n + 1, 0)
                store_block(n, 1)
            block_used(ROUNDS - 2, 1)
            load_block(ROUNDS - 1, 1)
            store_block(ROUNDS - 1, 0)
            store_block(ROUNDS - 1, 1)

            sp.wait_ge(c_ready, len(SLOTS))

            def load_outputs(s, b):
                for dst, src in ((c_o[s], o_d), (c_gate[s], gate_d)):
                    sp.dma_start(dst, src[bass.ds(b, 1)].rearrange("o (k p) t -> p (o k) t", p=P)).then_inc(o_loaded[s], 16)

            for s in SLOTS:
                load_outputs(s, s)
            sp.wait_ge(ahead_filled, 32)
            for s in SLOTS:
                sp.wait_ge(first_dve.sem, first_dve.at(0, f"oz{s}"))

            def load_rows(i, s):
                sp.dma_start(c_xin[s], x[bass.ds(i * 2 + s, 1)].rearrange("o (t p) d -> p (o t) d", p=P)).then_inc(c_loaded[s], 16)

            def store_rows(i):
                for s in SLOTS:
                    for a in range(2):
                        sp.wait_ge(c_pool.sem, c_pool.at(i, f"x4{s}{a}"))
                        hold(sp)
                        sp.dma_start(out[bass.ds(i * 2 + s, 1)].rearrange("o (t p) d -> p (o t) d", p=P)[:, 2 * a:2 * a + 2],
                                     c_x[s][:, 2 * a:2 * a + 2]).then_inc(out_stored[s], 16)

            def frame_values(i):
                for s in SLOTS:
                    sp.wait_ge(c_act.sem, c_act.at(i, f"vt{s}0"))
                    hold(sp)
                    sp.wait_ge(c_dve.sem, c_dve.at(i, f"vt{s}1"))
                    hold(sp)
                    for back in range(3):
                        for j in range(TT):
                            first = j + back
                            frames = range(first, FRAMES, TT)
                            rows = slice(WINDOW - back * QF, WINDOW - back * QF + QF)
                            sp.dma_start(c_v[s][rows, first:FRAMES:TT], c_vt[s][j * QF:(j + 1) * QF, 0:len(frames)]).then_inc(v_framed[s], 16)
                    sp.dma_start(c_v[s][WINDOW + QF:KEYS], c_vt[s][0:NGLOB, 0:1].broadcast_to([NGLOB, FRAMES, DIM])).then_inc(v_framed[s], 16)

            for s in SLOTS:
                load_rows(0, s)
            for s in SLOTS:
                load_outputs(s, s + AHEAD)
            frame_values(0)
            with sp.Fori(1, BATCH // 2) as i:
                for s in SLOTS:
                    sp.wait_ge(c_pe.sem, c_pe.before(i, f"pv{s}{FRAMES - 1}"))
                    hold(sp)
                    load_rows(i, s)
                store_rows(i - 1)
                for s in SLOTS:
                    load_outputs(s, i * 2 + s + AHEAD)
                frame_values(i)
            store_rows(BATCH // 2 - 1)
            for s in SLOTS:
                sp.wait_ge(out_stored[s], 32 * (BATCH // 2))

        @block.tensor
        def _(pe):
            for st in (su_pe, ln_pe, pr_pe, le_pe, *re_pe, first_pe, c_pe):
                pe.sem_inc(st.sem, len(st.names))
            pe.wait_ge(wmod_loaded, 16 * LAYERS)
            pe.wait_ge(su_act.sem, su_act.at(0, "silu"))
            for layer in range(LAYERS):
                for m in range(N_MOD * KT):
                    col = (layer * N_MOD * KT + m) * BATCH
                    for k in range(KT):
                        mm = pe.matmul(bank[0][:, col:col + BATCH], wmod_sb[:, layer, k, m * P:(m + 1) * P],
                                       cond_silu[:, layer, k], start=(k == 0), stop=(k == KT - 1))
            mm.then_inc(su_pe.mark("mod"), 1)
            for layer in range(LAYERS):
                for j, which in enumerate((2, 5)):
                    for k in range(KT):
                        mm = pe.matmul(bank[1 + layer][0:BATCH, j * DIM:(j + 1) * DIM], cond_silu[:, layer, k],
                                       wmod_sb[:, layer, k, which * DIM:(which + 1) * DIM],
                                       start=(k == 0), stop=(k == KT - 1))
                mm.then_inc(su_pe.mark(f"gate{layer}"), 1)

            def turn(m):
                pe.wait_ge(ln_dve.sem, ln_dve.at(m, "xh3"))
                pe.wait_ge(ln_act.sem, ln_act.before(m, "h1"))
                for k in range(KT):
                    for t in range(TT):
                        mm = pe.transpose(bank[k][:, t * P:(t + 1) * P], a_xhat[:, t, k * P:(k + 1) * P], ident[:])
                    mm.then_inc(ln_pe.mark(f"t{k}"), 1)

            def project(n, behind, ahead):
                if behind:
                    lengths(n - 1)
                pe.wait_ge(ln_act.sem, ln_act.at(n, "h1"))
                for j, name in enumerate(QKV + ["g0", "g1", "lr"]):
                    if name == "g0":
                        pe.wait_ge(pr_dve.sem, pr_dve.at(n, "c03"))
                    elif name == "g1":
                        pe.wait_ge(pr_dve.sem, pr_dve.at(n, "c13"))
                    elif name == "lr":
                        pe.wait_ge(pr_dve.sem, pr_dve.at(n, "c23"))
                    elif name in ("q0", "q1"):
                        pe.wait_ge(pr_act.sem, pr_act.before(n, ("g0", "g1")[j]))
                    elif behind:
                        pe.wait_ge(le_act.sem, le_act.at(n - 1, f"ln{SS_BANKS.index(2 + j)}"))
                    rows = 2 * HEADS if name == "lr" else P
                    for k in range(KT):
                        mm = pe.matmul(bank[2 + j % 6][0:rows], w_in_sb[:, k, j * P:j * P + rows], a_h[:, k],
                                       start=(k == 0), stop=(k == KT - 1))
                    mm.then_inc(pr_pe.mark(name), 1)

                if ahead:
                    turn(n + 1)

            def lengths(n):
                for t, b in enumerate(SS_BANKS):
                    pe.wait_ge(le_dve.sem, le_dve.at(n, f"sq{t}"))
                    if b > 4:
                        pe.wait_ge(pr_dve.sem, pr_dve.at(n, f"c{b - 2}3"))
                    if b == 4:
                        pe.wait_ge(pr_act.sem, pr_act.at(n, "lr"))
                    pe.matmul(bank[b][:], mean16[:], a_sq[:, t], start=True, stop=True).then_inc(le_pe.mark(f"ss{t}"), 1)

            pe.wait_ge(consts_loaded, 48)
            pe.wait_ge(weights_loaded, 16 * (20 + 2 * GROUP_B))
            pe.wait_ge(su_act.sem, su_act.at(0, "modc"))
            turn(0)
            pe.wait_ge(su_act.sem, su_act.at(0, "raw1"))
            project(0, False, True)
            with pe.Fori(1, BATCH - 1) as n:
                project(n, True, True)
            project(BATCH - 1, True, False)
            lengths(BATCH - 1)

            phase_a_done(pe)

            def add_up(dst, products):
                terms = products.rearrange("p (j x) -> p j x", j=16)
                for j in range(16):
                    mm = pe.matmul(dst, ident[:], terms[:, j], start=(j == 0), stop=(j == 15))
                return mm

            with pe.Fori(0, ROUNDS) as n:
                def sums(g):
                    dve, pool, mine = re_dve[g], re_pool[g], re_pe[g]
                    scores, d_in, queries = (bank[4 * g + b] for b in range(3))
                    for j in range(CPR):
                        c = n * CPR + j
                        yield
                        pe.wait_ge(dve.sem, dve.at(c, "b2_mul"))
                        add_up(scores[:, 0:2 * ROWS], t_mul[g]).then_inc(mine.mark("b"), 1)
                        pe.wait_ge(pool.sem, pool.at(c, "sq_mul"))
                        add_up(queries[:, 0:ROWS], t_q[g]).then_inc(mine.mark("sq"), 1)
                        yield
                        pe.wait_ge(dve.sem, dve.at(c, "d_mul"))
                        add_up(d_in[:, 0:2 * ROWS], t_mul[g]).then_inc(mine.mark("d"), 1)
                        yield
                    yield

                staggered(sums)

            recurrence_done(pe)

            def out_mean(dve_s, mine, n, s, loads):
                pe.wait_ge(o_loaded[s], loads)
                if s > 0:
                    pe.wait_ge(dve_s.sem, dve_s.at(n, f"oc{s - 1}{KT - 1}"))
                for k in range(KT):
                    pe.matmul(bank[3 + 4 * k][:], mean16[:], c_o[s][:, k], start=True, stop=True).then_inc(mine.mark(f"mean{s}{k}"), 1)

            def out_var(pool_s, dve_s, mine, n, s):
                pe.wait_ge(pool_s.sem, pool_s.at(n, f"osq{s}"))
                pe.wait_ge(dve_s.sem, dve_s.at(n, f"ov{s - 1}{KT - 1}" if s > 0 else f"oc{len(SLOTS) - 1}{KT - 1}"))
                for k in range(KT):
                    pe.matmul(bank[3 + 4 * k][:], mean16[:], c_ostd[s][:, k], start=True, stop=True).then_inc(mine.mark(f"var{s}{k}"), 1)

            for s in SLOTS:
                out_mean(first_dve, first_pe, 0, s, 32)
            for s in SLOTS:
                out_var(first_pool, first_dve, first_pe, 0, s)
            pe.wait_ge(first_dve.sem, first_dve.at(0, f"pick{len(SLOTS) - 1}"))
            with pe.Fori(0, BATCH // 2) as i:
                B = lambda s, j: bank[4 * s + j]
                for s in SLOTS:
                    pe.wait_ge(c_dve.sem, c_dve.before(i, f"rv{s}1"))
                    for layer in range(LAYERS):
                        mm = pe.matmul(B(s, layer)[:], c_pick[s][0:BATCH], gates_row[:, layer * 2 * DIM:(layer + 1) * 2 * DIM],
                                       start=True, stop=True)
                        mm.then_inc(c_pe.mark(f"gb{s}{layer}"), 1)

                def stay_warm(step, spare):
                    for _ in range(WARM.get(step, 0)):
                        pe.matmul(spare[:, 0:2 * KT * KEYS], identb[:], mask_sb[:, 0:2].rearrange("p a b -> p (a b)"), start=True, stop=True)

                def rows_out(s, name, lhs, rhs, banks):
                    for a in range(2):
                        for j in range(2):
                            for k in range(KT):
                                mm = pe.matmul(B(s, banks[a])[:, j * DIM:(j + 1) * DIM], lhs(k, 2 * a + j), rhs(k),
                                               start=(k == 0), stop=(k == KT - 1))
                        mm.then_inc(c_pe.mark(f"{name}{s}{a}"), 1)

                def tok(t):
                    return slice(t * P, (t + 1) * P)

                def turn_c(s, stage, banks):
                    pe.wait_ge(c_dve.sem, c_dve.at(i, f"xh{stage}{s}3"))
                    for k in range(KT):
                        for t in range(TT):
                            mm = pe.transpose(B(s, banks[k])[:, tok(t)], c_xhat[s][:, t, k * P:(k + 1) * P], ident[:])
                        mm.then_inc(c_pe.mark(f"turn{stage}{s}{k}"), 1)

                for s in SLOTS:
                    pe.wait_ge(c_dve.sem, c_dve.at(i, f"wo{s}"))
                    pe.wait_ge(c_act.sem, c_act.before(i, f"kk{s}1"))
                    rows_out(s, "wo", lambda k, t: c_oz[s][:, k, tok(t)], lambda k: c_wo[s][:, k], (2, 3))
                def half(s):
                    return slice(s * RANK, (s + 1) * RANK)

                for s in SLOTS:
                    if s == 0:
                        pe.wait_ge(c_dve.sem, c_dve.at(i, "wv1"))
                        stay_warm("norm1", B(1, 1))
                    turn_c(s, 1, (0, 1))
                    stay_warm(f"u1{s}", B(1, 0) if s == 0 else B(0, 1))
                    pe.wait_ge(c_act.sem, c_act.at(i, f"h1{s}1"))
                    for k in range(KT):
                        mm = pe.matmul(B(s, 0)[half(s)], u1_sb[:, k], c_h[s][:, k, 1:TOK + 1], start=(k == 0), stop=(k == KT - 1))
                    mm.then_inc(c_pe.mark(f"u1{s}"), 1)

                def up(f):
                    for s in SLOTS:
                        if f == 0:
                            pe.wait_ge(c_act.sem, c_act.at(i, f"p{s}"))
                        if f >= UP_BANKS:
                            pe.wait_ge(c_act.sem, c_act.at(i, f"gelu{s}{f - UP_BANKS}"))
                        mm = pe.matmul(B(s, 1 + f % UP_BANKS)[:], v1_sb[half(s), f * P:(f + 1) * P], c_p[half(s)], start=True, stop=True)
                        mm.then_inc(c_pe.mark(f"v1{s}{f}"), 1)

                for f in range(UP_BANKS):
                    up(f)
                for f in range(FT):
                    for s in SLOTS:
                        pe.wait_ge(c_act.sem, c_act.at(i, f"gelu{s}{f}"))
                        mm = pe.matmul(B(s, 0)[half(s)], u2_sb[:, f], c_f[s][:, f % 3], start=(f == 0), stop=(f == FT - 1))
                        mm.then_inc(c_pe.mark(f"u2{s}{f}"), 1)
                    if f + UP_BANKS < FT:
                        up(f + UP_BANKS)
                    what, r = OUT_AT.get(f, ("", 0))
                    if what == "mean":
                        out_mean(c_dve, c_pe, i, r, 32 * (i + 2))
                    if what == "var":
                        out_var(c_pool, c_dve, c_pe, i, r)
                for s in SLOTS:
                    pe.wait_ge(c_dve.sem, c_dve.at(i, f"qr{s}"))
                for a in range(2):
                    for j in range(2):
                        for s in SLOTS:
                            mm = pe.matmul(B(s, 1 + a)[:, j * DIM:(j + 1) * DIM], c_qr[half(s), tok(2 * a + j)],
                                           c_v2[half(s)], start=True, stop=True)
                            if j == 1:
                                mm.then_inc(c_pe.mark(f"v2{s}{a}"), 1)
                for s in SLOTS:
                    if s == 0:
                        stay_warm("norm2", B(1, 0))
                    turn_c(s, 2, (3, 0))
                    stay_warm(f"vt{s}", B(1, 0) if s == 0 else B(0, 3))
                    pe.wait_ge(c_act.sem, c_act.at(i, f"h2{s}{KT - 1}"))
                    pe.wait_ge(c_dve.sem, c_dve.at(i, f"x2{s}1"))
                    rows_out(s, "vt", lambda k, t: c_h[s][:, k, 1 + t * P:1 + (t + 1) * P], lambda k: w_attn_sb[:, k, 2 * DIM:3 * DIM], (1, 2))
                for which, banks in (("q", (3, 0)), ("k", (1, 2))):
                    for s in SLOTS:
                        if which == "k":
                            pe.wait_ge(c_act.sem, c_act.at(i, f"vt{s}0"))
                            pe.wait_ge(c_dve.sem, c_dve.at(i, f"vt{s}1"))
                        for m in range(KT):
                            j = ("q", "k").index(which) * KT + m
                            for k in range(KT):
                                mm = pe.matmul(B(s, banks[m])[:], w_attn_sb[:, k, j * P:(j + 1) * P], c_h[s][:, k, 1:TOK + 1],
                                               start=(k == 0), stop=(k == KT - 1))
                            mm.then_inc(c_pe.mark(f"{which}{s}{m}"), 1)

                pe.wait_ge(c_act.sem, c_act.at(i, "qb103"))
                stay_warm("s0", bank[Y_BANKS[2]])
                for t in range(len(ATT) + PV_LAG):
                    if t < len(ATT):
                        f, s = ATT[t]
                        if f == 0:
                            pe.wait_ge(c_act.sem, c_act.at(i, "ks13"))
                            pe.wait_ge(c_dve.sem, c_dve.at(i, "ks13"))
                            pe.wait_ge(c_pool.sem, c_pool.at(i, "pad13"))
                        else:
                            pe.wait_ge(c_act.sem, c_act.at(i, f"exp{s}{f - 1}u{QUADS - 1}"))
                        for top in range(2):
                            pe.matmul(B(s, top)[:, 0:KT * KEYS], identb[:], mask_sb[:, min(f, 3)], start=True, stop=False,
                                      skip_group_check=True)
                        for k in range(KT):
                            for top in range(2):
                                rows = slice(64 * top, 64 * top + 64)
                                mm = pe.matmul(B(s, top)[:, k * KEYS:(k + 1) * KEYS], c_qb[s][rows, k, f],
                                               c_k[s][rows, k, f], start=False, stop=True, skip_group_check=True)
                        mm.then_inc(c_pe.mark(f"s{s}{f}"), 1)
                    stay_warm(f"t{t - T_LAG}", bank[Y_BANKS[2]])
                    if 0 <= t - T_LAG < len(ATT):
                        f, s = ATT[t - T_LAG]
                        pe.wait_ge(c_pool.sem, c_pool.at(i, f"prob{s}{f}"))
                        if t > T_LAG:
                            g, r = ATT[t - T_LAG - 1]
                            pe.wait_ge(c_act.sem, c_act.at(i, f"pt{r}{g}"))
                        for u in range(QUADS):
                            mm = pe.transpose(bank[TURNED][0:KEYS, tok(u)], c_soft[s][:, f % 2, u], ident[:])
                        mm.then_inc(c_pe.mark(f"t{s}{f}"), 1)
                    stay_warm(f"pv{t - PV_LAG}", bank[Y_BANKS[2]])
                    if 0 <= t - PV_LAG < len(ATT):
                        f, s = ATT[t - PV_LAG]
                        if f == 0:
                            pe.wait_ge(v_framed[s], 16 * FRAMED * (i + 1))
                        pe.wait_ge(c_act.sem, c_act.at(i, f"pt{s}{f}"))
                        turn = len(SLOTS) * (f // QTR) + s
                        if f % QTR == 0 and turn >= len(Y_BANKS):
                            before = turn - len(Y_BANKS)
                            pe.wait_ge(c_dve.sem, c_dve.at(i, f"y{before % 2}{before // 2}"))
                        for u in range(QUADS):
                            top, k = u // 2, u % 2
                            for pr in range(2):
                                head = (k * P + 64 * top) // HD + 2 * pr
                                row = 64 * top + 32 * pr
                                col = (k * QTR + f % QTR) * 2 * QF
                                mm = pe.matmul(y_bank(s, f // QTR)[row:row + 32, col:col + 2 * QF],
                                               c_v[s][0:KEYS, f, head * HD:(head + 2) * HD],
                                               c_pt[s][0:KEYS, u * P + 64 * pr:u * P + 64 * pr + 64],
                                               start=True, stop=True)
                        mm.then_inc(c_pe.mark(f"pv{s}{f}"), 1)
                for s in SLOTS:
                    pe.wait_ge(c_dve.sem, c_dve.at(i, f"y{s}3"))
                    rows_out(s, "wp", lambda k, t: c_y[s][:, t, k], lambda k: c_wp[s][:, k], (0, 1))
                stay_warm("norm3", bank[Y_BANKS[2]])
                for s in SLOTS:
                    turn_c(s, 3, (2, 3))
                    stay_warm(f"turn3{s}", bank[Y_BANKS[2]] if s == 0 else B(1, 1))
                for s in SLOTS:
                    pe.wait_ge(c_dve.sem, c_dve.at(i, f"xr{s}{KT - 1}"))
                    rows_out(s, "r", lambda k, t: c_xr[s][:, k, tok(t)], lambda k: w_rkv_sb[:, 0, k], (0, 1))
                    pe.wait_ge(c_dve.sem, c_dve.at(i, f"xk{s}{KT - 1}"))
                    for m in range(KT):
                        for k in range(KT):
                            mm = pe.matmul(B(s, 2 + m)[:], w_rkv_sb[:, 1, k, m * P:(m + 1) * P], c_xk[s][:, k],
                                           start=(k == 0), stop=(k == KT - 1))
                        mm.then_inc(c_pe.mark(f"kk{s}{m}"), 1)
                for s in SLOTS:
                    pe.wait_ge(c_pool.sem, c_pool.at(i, f"kk{s}1"))
                    pe.wait_ge(c_act.sem, c_act.at(i, f"r{s}1"))
                    rows_out(s, "vv", lambda k, t: c_kk[s][:, k, tok(t)], lambda k: c_wv[s][:, k], (0, 1))

        @block.scalar
        def _(act):
            for st in (su_act, ln_act, pr_act, le_act, st_act, *re_act, first_act, c_act):
                act.sem_inc(st.sem, len(st.names))
            act.wait_ge(cond_loaded, 16)
            act.activation(cond_silu, cond_sb, ACT.Silu).then_inc(su_act.mark("silu"), 1)
            act.wait_ge(su_pe.sem, su_pe.at(0, "mod"))
            act.activation(modc[:].rearrange("p a b -> p (a b)"), bank[0][:, 0:LAYERS * N_MOD * KT * BATCH], ACT.Copy).then_inc(su_act.mark("modc"), 1)
            for layer in range(LAYERS):
                act.wait_ge(su_pe.sem, su_pe.at(0, f"gate{layer}"))
                act.activation(g_raw[0:BATCH, layer * 2 * DIM:(layer + 1) * 2 * DIM], bank[1 + layer][0:BATCH], ACT.Copy).then_inc(su_act.mark(f"raw{layer}"), 1)

            def norm_a(m):
                act.wait_ge(ln_act.sem, ln_act.before(m, "h1"))
                ins = act.activation(a_modb, modc[:, 0:2 * KT, bass.ds(m, 1)].rearrange("p a o -> p (a o)"), ACT.Copy)
                ins.then_inc(ln_act.mark("modb"), 1)
                act.wait_ge(ln_dve.sem, ln_dve.at(m, "ag3"))
                act.activation(a_std, a_mv[:, :, 1], ACT.Ln, bias=parity[:, 6:7]).then_inc(ln_act.mark("ln"), 1)

            def norm_exp(m):
                act.wait_ge(ln_act.sem, ln_act.at(m, "ln"))
                act.wait_ge(ln_dve.sem, ln_dve.before(m, "xh3"))
                act.activation(a_rstd, a_std, ACT.Exp, scale=-0.5).then_inc(ln_act.mark("rstd"), 1)

            def modulate_a(m):
                act.wait_ge(ln_act.sem, ln_act.at(m, "modb"))
                act.wait_ge(pr_pe.sem, pr_pe.before(m, "lr"))
                for k in range(KT):
                    act.wait_ge(ln_pe.sem, ln_pe.at(m, f"t{k}"))
                    ins = act.activation(a_h[:, k], bank[k][:], ACT.Identity, bias=a_modb[:, k:k + 1], scale=a_modb[:, KT + k:KT + k + 1])
                    ins.then_inc(ln_act.mark(f"h{k}"), 1)

            def tap(n, t):
                act.wait_ge(pr_pe.sem, pr_pe.at(n, QKV[t]))
                act.wait_ge(pr_act.sem, pr_act.before(n, f"silu{t}"))
                col = (t // KT) * TAPS + TAPS - 1
                ins = act.activation(a_acc[:, t], bank[2 + t][:], ACT.Copy, scale=taps_sb[:, t % KT, col:col + 1])
                ins.then_inc(pr_act.mark(f"tap{t}"), 1)

            def silu(n, t):
                act.wait_ge(pr_dve.sem, pr_dve.at(n, f"c{t}3"))
                if t < 4:
                    act.wait_ge(le_pool.sem, le_pool.before(n, f"unit{t}"))
                else:
                    act.wait_ge(a_stored[QKV[t]], 16 * n)
                act.activation(a_silu[:, t], a_acc[:, t], ACT.Silu).then_inc(pr_act.mark(f"silu{t}"), 1)

            def gate(n, k):
                act.wait_ge(pr_pe.sem, pr_pe.at(n, f"g{k}"))
                act.wait_ge(a_stored[f"g{k}"], 16 * n)
                act.activation(a_gate[:, k], bank[2 + k][:], ACT.Copy).then_inc(pr_act.mark(f"g{k}"), 1)

            def lengths_log(n):
                for t in range(4):
                    act.wait_ge(le_pe.sem, le_pe.at(n, f"ss{t}"))
                    act.wait_ge(le_pool.sem, le_pool.before(n, f"unit{t}"))
                    act.activation(a_rn[:, t], bank[SS_BANKS[t]][:], ACT.Ln, scale=float(HD)).then_inc(le_act.mark(f"ln{t}"), 1)

            def lengths_exp(n, t):
                act.wait_ge(le_act.sem, le_act.at(n, f"ln{t}"))
                act.activation(a_rn[:, t], a_rn[:, t], ACT.Exp, scale=-0.5).then_inc(le_act.mark(f"rn{t}"), 1)

            def sequence(n, behind, ahead):
                if behind:
                    lengths_log(n - 1)
                if ahead:
                    norm_a(n + 1)
                for t in range(6):
                    tap(n, t)
                    if t == 0 and ahead:
                        norm_exp(n + 1)
                    if t < 4 and behind:
                        lengths_exp(n - 1, t)
                silu(n, 0), silu(n, 1), silu(n, 2), silu(n, 3), gate(n, 0), silu(n, 4), gate(n, 1)
                act.wait_ge(pr_pe.sem, pr_pe.at(n, "lr"))
                act.wait_ge(a_stored["lr"], 16 * n)
                ins = act.activation(a_lr[0:2 * HEADS], bank[4][0:2 * HEADS], ACT.Copy, bias=BASE_LR)
                ins.then_inc(pr_act.mark("lr"), 1)
                if ahead:
                    modulate_a(n + 1)
                silu(n, 5)

            act.wait_ge(su_dve.sem, su_dve.at(0, "gates"))
            norm_a(0)
            norm_exp(0)
            modulate_a(0)
            sequence(0, False, True)
            with act.Fori(1, BATCH - 1) as n:
                sequence(n, True, True)
            sequence(BATCH - 1, True, False)
            lengths_log(BATCH - 1)
            for t in range(4):
                lengths_exp(BATCH - 1, t)

            phase_a_done(act)
            act.wait_ge(lr_loaded, 16 * GROUPS)
            act.activation(lr_tmp, lr_raw, ACT.Abs).then_inc(st_act.mark("abs"), 1)
            act.wait_ge(st_act.sem, st_act.at(0, "abs"))
            act.activation(lr_tmp, lr_tmp, ACT.Exp, scale=-1.0).then_inc(st_act.mark("exp"), 1)
            act.wait_ge(st_act.sem, st_act.at(0, "exp"))
            act.activation(lr_tmp, lr_tmp, ACT.Ln, bias=1.0).then_inc(st_act.mark("ln"), 1)

            with act.Fori(0, ROUNDS) as n:
                def exponentials(g):
                    dve, mine = re_dve[g], re_act[g]
                    attn = float(HD) ** -0.5
                    for j in range(CPR):
                        c = n * CPR + j
                        act.wait_ge(dve.sem, dve.at(c, "sub2"))
                        act.activation(e_2[g], e_2[g], ACT.Exp, scale=attn).then_inc(mine.mark("e2"), 1)
                        act.wait_ge(dve.sem, dve.at(c, "psub"))
                        act.activation(e_p[g], e_p[g], ACT.Exp, scale=attn).then_inc(mine.mark("ep"), 1)
                        act.wait_ge(dve.sem, dve.at(c, "ksub"))
                        act.activation(e_k[g], e_k[g], ACT.Exp).then_inc(mine.mark("ek"), 1)
                        yield
                        yield
                        act.wait_ge(dve.sem, dve.at(c, "bsub"))
                        act.activation(e_b[g], e_b[g], ACT.Exp, scale=attn).then_inc(mine.mark("eb"), 1)
                        act.wait_ge(dve.sem, dve.at(c, "qsub"))
                        act.activation(e_q[g], e_q[g], ACT.Exp).then_inc(mine.mark("eq"), 1)
                        yield
                    yield

                staggered(exponentials)

            def out_ln(dve_s, mine, n, s):
                act.wait_ge(dve_s.sem, dve_s.at(n, f"ov{s}{KT - 1}"))
                act.activation(c_ostd[s], c_ostd[s], ACT.Ln, bias=parity[:, 6:7]).then_inc(mine.mark(f"oln{s}"), 1)

            def out_exp(mine, n, s):
                act.wait_ge(mine.sem, mine.at(n, f"oln{s}"))
                act.activation(c_ostd[s], c_ostd[s], ACT.Exp, scale=-0.5).then_inc(mine.mark(f"orstd{s}"), 1)

            for s in SLOTS:
                out_ln(first_dve, first_act, 0, s)
            for s in SLOTS:
                out_exp(first_act, 0, s)
            with act.Fori(0, BATCH // 2) as i:
                B = lambda s, j: bank[4 * s + j]

                def std(stage, s):
                    act.wait_ge(c_dve.sem, c_dve.at(i, f"ag{stage}{s}{TT - 1}"))
                    act.activation(c_std[s], c_mv[s][:, :, 1], ACT.Sqrt, bias=parity[:, 6:7]).then_inc(c_act.mark(f"std{stage}{s}"), 1)

                def modulate(stage, s, k, banks):
                    act.wait_ge(c_pe.sem, c_pe.at(i, f"turn{stage}{s}{k}"))
                    ins = act.activation(c_h[s][:, k, 1:TOK + 1], B(s, banks[k])[:], ACT.Identity,
                                         bias=c_modb[s][:, stage - 1, k:k + 1],
                                         scale=c_modb[s][:, stage - 1, KT + k:KT + k + 1])
                    ins.then_inc(c_act.mark(f"h{stage}{s}{k}"), 1)

                def norm(stage, banks):
                    std(stage, 0)
                    modulate(stage, 0, 0, banks)
                    std(stage, 1)
                    modulate(stage, 0, 1, banks)
                    for k in range(KT):
                        modulate(stage, 1, k, banks)

                def half(s):
                    return slice(s * RANK, (s + 1) * RANK)

                norm(1, (0, 1))
                for s in SLOTS:
                    act.wait_ge(c_pe.sem, c_pe.at(i, f"u1{s}"))
                    act.wait_ge(c_pe.sem, c_pe.at(i, "wo11"))
                    act.activation(c_p[half(s)], B(s, 0)[half(s)], ACT.Copy).then_inc(c_act.mark(f"p{s}"), 1)
                for f in range(FT):
                    for s in SLOTS:
                        act.wait_ge(c_pe.sem, c_pe.at(i, f"v1{s}{f}"))
                        if f >= 3:
                            act.wait_ge(c_pe.sem, c_pe.at(i, f"u2{s}{f - 3}"))
                        act.activation(c_f[s][:, f % 3], B(s, 1 + f % UP_BANKS)[:], ACT.Gelu_apprx_tanh, bias=b1_sb[:, f:f + 1]).then_inc(c_act.mark(f"gelu{s}{f}"), 1)
                for s in SLOTS:
                    out_ln(c_dve, c_act, i, s)
                for s in SLOTS:
                    out_exp(c_act, i, s)
                norm(2, (3, 0))

                def segments(dst, src):
                    blocks = src.rearrange("p (f q) -> p f q", q=QF)
                    return ((dst[:, 2:FRAMES, 0:QF], blocks[:, 0:FRAMES - 2]),
                            (dst[:, 1:FRAMES, QF:2 * QF], blocks[:, 0:FRAMES - 1]),
                            (dst[:, :, 2 * QF:3 * QF], blocks),
                            (dst[:, :, 3 * QF:KEYS], src[:, 0:NGLOB].unsqueeze(1).broadcast_to([P, FRAMES, NGLOB])))

                for s in SLOTS:
                    act.wait_ge(c_pe.sem, c_pe.at(i, f"vt{s}0"))
                    act.activation(c_vt[s][:, 0:2], B(s, 1)[:].rearrange("p (t d) -> p t d", t=2), ACT.Copy).then_inc(c_act.mark(f"vt{s}0"), 1)
                for s in SLOTS:
                    act.wait_ge(c_pe.sem, c_pe.at(i, f"q{s}0"))
                    for j in range(4):
                        act.activation(c_qb[s][:, 0, :, j * QF:(j + 1) * QF], B(s, 3)[:].rearrange("p (f q) -> p f q", q=QF),
                                       ACT.Copy, scale=parity[:, j:j + 1]).then_inc(c_act.mark(f"qb{s}0{j}"), 1)
                for s in SLOTS:
                    act.wait_ge(c_pe.sem, c_pe.at(i, f"k{s}1"))
                    if s == 0:
                        act.wait_ge(c_dve.sem, c_dve.at(i, f"oz{len(SLOTS) - 1}"))
                    for g, (dst, src) in enumerate(segments(c_k[s][:, 1], B(s, 2)[:])):
                        act.activation(dst, src, ACT.Copy).then_inc(c_act.mark(f"ks{s}{g}"), 1)

                for t in range(len(ATT) + YE_LAG + 1):
                    if t < len(ATT):
                        f, s = ATT[t]
                        act.wait_ge(c_dve.sem, c_dve.at(i, f"max{s}{f}"))
                        if f >= 2:
                            act.wait_ge(c_pe.sem, c_pe.at(i, f"t{s}{f - 2}"))
                        for u in range(QUADS):
                            sc = B(s, u // KT)[:, (u % KT) * KEYS:(u % KT + 1) * KEYS]
                            act.activation(c_soft[s][:, f % 2, u], sc, ACT.Exp, bias=c_max[s][:, u:u + 1]).then_inc(c_act.mark(f"exp{s}{f}u{u}"), 1)
                    if 0 <= t - T_LAG < len(ATT):
                        f, s = ATT[t - T_LAG]
                        act.wait_ge(c_pe.sem, c_pe.at(i, f"t{s}{f}"))
                        if f > 0:
                            act.wait_ge(c_pe.sem, c_pe.at(i, f"pv{s}{f - 1}"))
                        act.activation(c_pt[s][0:KEYS], bank[TURNED][0:KEYS], ACT.Copy).then_inc(c_act.mark(f"pt{s}{f}"), 1)
                    if 0 <= t - YE_LAG < len(ATT) and ends_quarter(ATT[t - YE_LAG][0]):
                        f, s = ATT[t - YE_LAG]
                        act.wait_ge(c_pe.sem, c_pe.at(i, f"pv{s}{f}"))
                        if f > QTR:
                            act.wait_ge(c_dve.sem, c_dve.at(i, f"y{s}{f // QTR - 1}"))
                        src = y_bank(s, f // QTR)[:].rearrange("p (f e q) -> p f e q", e=2, q=QF)[:, :, 0]
                        act.activation(c_yeven[s], src, ACT.Copy, scale=parity[:, 4:5]).then_inc(c_act.mark(f"ye{s}{f // QTR}"), 1)
                norm(3, (2, 3))
                for s in SLOTS:
                    for a in range(2):
                        act.wait_ge(c_pe.sem, c_pe.at(i, f"r{s}{a}"))
                        act.activation(c_r[s][:, 2 * a:2 * a + 2], B(s, a)[:].rearrange("p (t d) -> p t d", t=2), ACT.Sigmoid).then_inc(c_act.mark(f"r{s}{a}"), 1)
                    for m in range(KT):
                        act.wait_ge(c_pe.sem, c_pe.at(i, f"kk{s}{m}"))
                        act.activation(c_kk[s][:, m], B(s, 2 + m)[:], ACT.Relu).then_inc(c_act.mark(f"kk{s}{m}"), 1)

        @block.gpsimd
        def _(pool):
            for st in (le_pool, scan_ready, *re_pool, first_pool, c_pool):
                pool.sem_inc(st.sem, len(st.names))
            def units(n):
                for t in range(4):
                    pool.wait_ge(le_act.sem, le_act.at(n, f"rn{t}"))
                    pool.wait_ge(a_stored[QKV[t]], 16 * n)
                    pool.tensor_tensor(a_unit[:, t], a_silu[:, t], a_rn[:, t], ALU.mult).then_inc(le_pool.mark(f"unit{t}"), 1)

            with pool.Fori(0, BATCH) as n:
                units(n)

            phase_a_done(pool)
            pool.memset(scan_keep, 1.0).then_inc(scan_ready.mark("ones"), 1)
            pool.wait_ge(scan_ready.sem, scan_ready.at(0, "ones"))
            pool.memset(scan_keep.rearrange("p (a l) -> p a l", l=CHUNK)[:, :, 0:1], 0.0).then_inc(scan_ready.mark("zeros"), 1)
            with pool.Fori(0, ROUNDS) as n:
                def products(g):
                    dve, mine = re_dve[g], re_pool[g]
                    cube = lambda t: t.rearrange("p (a l d) -> p a l d", a=INNER, l=16)
                    terms = lambda t: t.rearrange("p (d a l) -> p a l d", d=HD, a=INNER)
                    grid = lambda t: t.rearrange("p (a l) -> p a l", a=INNER)
                    by_ld = lambda w: grid(w).unsqueeze(2).broadcast_to([P, INNER, CHUNK, HD])
                    by_dl = lambda w: grid(w).unsqueeze(2).broadcast_to([P, INNER, HD, CHUNK])
                    for j in range(CPR):
                        c = n * CPR + j
                        buf, before = j // CPB, (j - 1) % CPR // CPB
                        now = slice(j % CPB * CHUNK, (j % CPB + 1) * CHUNK)
                        last = slice((j - 1) % CPB * CHUNK, ((j - 1) % CPB + 1) * CHUNK)
                        pool.wait_ge(dve.sem, dve.at(c, "p2"))
                        v_dl = v_blk[before][g][:, :, last].unsqueeze(1).broadcast_to([P, INNER, HD, CHUNK])
                        pool.tensor_tensor(cube(t_g2[g]), by_dl(p_2[g]), v_dl, ALU.mult).then_inc(mine.mark("g2"), 1)
                        if j % CPB == 0:
                            pool.wait_ge(blk_loaded[buf][g], 48 * (n + 1))
                        pool.wait_ge(dve.sem, dve.at(c, "p1"))
                        v_dl = v_blk[buf][g][:, :, now].unsqueeze(1).broadcast_to([P, INNER, HD, CHUNK])
                        pool.tensor_tensor(cube(t_g1[g]), by_dl(p_out1[g]), v_dl, ALU.mult).then_inc(mine.mark("g1"), 1)
                        pool.wait_ge(dve.sem, dve.at(c, "kh"))
                        pool.tensor_tensor(cube(t_run[g]), by_dl(k_hat[g]), v_dl, ALU.mult).then_inc(mine.mark("kv"), 1)
                        yield
                        if j == 0:
                            pool.wait_ge(st_dve.sem, st_dve.at(0, f"out{g}"))
                        pool.wait_ge(dve.sem, dve.before(c, "win"))
                        q_ld = q_blk[buf][g][:, :, now].rearrange("p d l -> p l d").unsqueeze(1).broadcast_to([P, INNER, CHUNK, HD])
                        pool.tensor_tensor(terms(t_q[g]), by_ld(win[g]), q_ld, ALU.mult).then_inc(mine.mark("sq_mul"), 1)
                        yield
                        yield
                        pool.wait_ge(dve.sem, dve.at(c, "qh"))
                        pool.tensor_tensor(cube(t_q[g]), by_dl(q_hat[g]), cube(t_run[g]), ALU.mult).then_inc(mine.mark("o_mul"), 1)
                        pool.wait_ge(mine.sem, mine.at(c, "o_mul"))
                        half, quarter = PROD // 2, PROD // 4
                        pool.tensor_tensor(t_q8[g], t_q[g][:, 0:half], t_q[g][:, half:PROD], ALU.add).then_inc(mine.mark("o2"), 1)
                        pool.wait_ge(mine.sem, mine.at(c, "o2"))
                        if j % CPB == 0:
                            pool.wait_ge(o_stored[buf][g], 16 * n)
                        to = lambda t: t.rearrange("p (d l) -> p d l", d=HD)
                        pool.tensor_tensor(o_blk[buf][g][:, :, now], to(t_q8[g][:, 0:quarter]), to(t_q8[g][:, quarter:half]), ALU.add).then_inc(mine.mark("o1"), 1)
                    yield

                staggered(products)

            def out_square(dve_s, mine, n, s):
                pool.wait_ge(dve_s.sem, dve_s.at(n, f"oc{s}{KT - 1}"))
                pool.tensor_tensor(c_ostd[s], c_o[s], c_o[s], ALU.mult).then_inc(mine.mark(f"osq{s}"), 1)

            for s in SLOTS:
                out_square(first_dve, first_pool, 0, s)
            with pool.Fori(0, BATCH // 2) as i:
                for s in SLOTS:
                    pool.wait_ge(c_dve.sem, c_dve.at(i, f"xh1{s}{TT - 1}"))
                    pool.tensor_tensor(c_x[s], c_x[s], c_b2[s].unsqueeze(1).broadcast_to([P, TT, DIM]), ALU.add).then_inc(c_pool.mark(f"x2{s}"), 1)
                for s in SLOTS:
                    out_square(c_dve, c_pool, i, s)
                pool.wait_ge(c_pe.sem, c_pe.at(i, "v211"))
                hold(pool)
                pool.wait_ge(c_dve.sem, c_dve.at(i, f"oz{len(SLOTS) - 1}"))
                hold(pool)
                for s in SLOTS:
                    for j, pad in enumerate((c_k[s][:, :, 0:2, 0:QF], c_k[s][:, :, 0:1, QF:2 * QF], c_v[s][0:2 * QF, 0:1], c_v[s][0:QF, 1:2])):
                        pool.memset(pad, 0.0).then_inc(c_pool.mark(f"pad{s}{j}"), 1)
                for f, s in ATT:
                    pool.wait_ge(c_dve.sem, c_dve.at(i, f"arec{s}{f}"))
                    soft = c_soft[s][:, f % 2]
                    pool.tensor_tensor(soft, soft, c_rec[s].unsqueeze(2).broadcast_to([P, 4, KEYS]), ALU.mult).then_inc(c_pool.mark(f"prob{s}{f}"), 1)
                pool.wait_ge(c_act.sem, c_act.at(i, f"h31{KT - 1}"))
                pool.tensor_tensor(c_d[1], c_h[1][:, :, 1:TOK + 1], c_h[1][:, :, 0:TOK], ALU.subtract).then_inc(c_pool.mark("d1"), 1)
                for s in SLOTS:
                    for m in range(KT):
                        pool.wait_ge(c_act.sem, c_act.at(i, f"kk{s}{m}"))
                        pool.tensor_tensor(c_kk[s][:, m], c_kk[s][:, m], c_kk[s][:, m], ALU.mult).then_inc(c_pool.mark(f"kk{s}{m}"), 1)
                for s in SLOTS:
                    for a in range(2):
                        pool.wait_ge(c_dve.sem, c_dve.at(i, f"rv{s}{a}"))
                        half = slice(2 * a, 2 * a + 2)
                        pool.tensor_tensor(c_x[s][:, half], c_x[s][:, half], c_rv[s][:, half], ALU.add).then_inc(c_pool.mark(f"x4{s}{a}"), 1)

        @block.vector
        def _(dve):
            for st in (su_dve, ln_dve, pr_dve, le_dve, st_dve, *re_dve, first_dve, c_dve):
                dve.sem_inc(st.sem, len(st.names))
            dve.wait_ge(consts_loaded, 48)
            dve.tensor_copy(identb[:], ident[:]).then_inc(su_dve.mark("identb"), 1)
            dve.wait_ge(su_act.sem, su_act.at(0, "modc"))
            for j, layer_which in enumerate((1, 4, 7, 10)):
                cols = modc[:, layer_which * KT:(layer_which + 1) * KT]
                dve.tensor_scalar(cols, cols, 1.0, None, ALU.add).then_inc(su_dve.mark(f"plus{j + 1}"), 1)
            dve.wait_ge(weights_loaded, 16 * (20 + 2 * GROUP_B))
            own_tap = taps_sb[:].rearrange("p k (c j) -> p k c j", j=TAPS)[:, :, :, TAPS - 1]
            dve.tensor_scalar(own_tap, own_tap, 1.0, None, ALU.add).then_inc(su_dve.mark("tap"), 1)
            dve.wait_ge(su_act.sem, su_act.at(0, "raw1"))
            dve.tensor_scalar(g_sign[0:BATCH], g_raw[0:BATCH], 0.0, 2.0, ALU.is_ge, ALU.mult).then_inc(su_dve.mark("side"), 1)
            dve.wait_ge(su_dve.sem, su_dve.at(0, "side"))
            dve.tensor_scalar(g_sign[0:BATCH], g_sign[0:BATCH], -1.0, None, ALU.add).then_inc(su_dve.mark("sign"), 1)
            dve.wait_ge(su_dve.sem, su_dve.at(0, "sign"))
            dve.tensor_tensor(g_size[0:BATCH], g_sign[0:BATCH], g_raw[0:BATCH], ALU.mult).then_inc(su_dve.mark("size"), 1)
            dve.wait_ge(su_dve.sem, su_dve.at(0, "size"))
            dve.scalar_tensor_tensor(out=gates_row[:], in0=g_size[0:BATCH], scalar=0.25, in1=g_sign[0:BATCH],
                                                 op0=ALU.max, op1=ALU.mult).then_inc(su_dve.mark("gates"), 1)

            def statistics_a(m):
                dve.wait_ge(x_loaded, 16 * (m + 1))
                dve.wait_ge(ln_act.sem, ln_act.before(m, "ln"))
                for t in range(TT):
                    dve.bn_stats(a_stat[:, t], a_x[:, t]).then_inc(ln_dve.mark(f"st{t}"), 1)
                dve.wait_ge(ln_dve.sem, ln_dve.at(m, f"st{TT - 1}"))
                hold(dve)
                for t in range(TT):
                    dve.bn_aggr(a_mv[:, t], a_stat[:, t]).then_inc(ln_dve.mark(f"ag{t}"), 1)

            def normalise_a(m):
                dve.wait_ge(ln_act.sem, ln_act.at(m, "rstd"))
                dve.wait_ge(ln_pe.sem, ln_pe.before(m, "t1"))
                for t in range(TT):
                    dve.tensor_scalar(a_xhat[:, t], a_x[:, t], a_mv[:, t, 0:1], a_rstd[:, t:t + 1],
                                      ALU.subtract, ALU.mult).then_inc(ln_dve.mark(f"xh{t}"), 1)

            def convolve(n, tiles):
                for t in tiles:
                    for j in (1, 2, 3):
                        if j == 1:
                            dve.wait_ge(pr_act.sem, pr_act.at(n, f"tap{t}"))
                        else:
                            dve.wait_ge(pr_dve.sem, pr_dve.at(n, f"c{t}{j - 1}"))
                        col = (t // KT) * TAPS + TAPS - 1 - j
                        ins = dve.scalar_tensor_tensor(out=a_acc[:, t, j:TOK], in0=bank[2 + t][:, 0:TOK - j],
                                                       scalar=taps_sb[:, t % KT, col:col + 1], in1=a_acc[:, t, j:TOK],
                                                       op0=ALU.mult, op1=ALU.add)
                        ins.then_inc(pr_dve.mark(f"c{t}{j}"), 1)

            def squares(n):
                for t in range(4):
                    dve.wait_ge(pr_act.sem, pr_act.at(n, f"silu{t}"))
                    dve.wait_ge(le_pe.sem, le_pe.before(n, f"ss{t}"))
                    dve.tensor_tensor(a_sq[:, t], a_silu[:, t], a_silu[:, t], ALU.mult).then_inc(le_dve.mark(f"sq{t}"), 1)

            dve.wait_ge(su_dve.sem, su_dve.at(0, "tap"))
            statistics_a(0)
            normalise_a(0)
            with dve.Fori(0, BATCH - 1) as n:
                statistics_a(n + 1)
                convolve(n, range(4))
                normalise_a(n + 1)
                convolve(n, (4,))
                squares(n)
                convolve(n, (5,))
            convolve(BATCH - 1, range(5))
            squares(BATCH - 1)
            convolve(BATCH - 1, (5,))

            phase_a_done(dve)
            dve.wait_ge(scan_ready.sem, scan_ready.at(0, "zeros"))
            dve.memset(lr_fin[:, :, 0:CHUNK], 0.0).then_inc(st_dve.mark("pad"), 1)
            dve.wait_ge(st_act.sem, st_act.at(0, "ln"))
            dve.scalar_tensor_tensor(out=lr_fin[:, :, CHUNK:CHUNK + TOK], in0=lr_raw, scalar=0.0, in1=lr_tmp, op0=ALU.max, op1=ALU.add).then_inc(st_dve.mark("lr"), 1)
            dve.wait_ge(st_dve.sem, st_dve.at(0, "lr"))
            for g in PAIRS:
                dve.memset(v_blk[1][g], 0.0).then_inc(st_dve.mark(f"no_v{g}"), 1)
                dve.memset(s_2[g], 0.0).then_inc(st_dve.mark(f"no_s2{g}"), 1)
                dve.tensor_copy(win[g], state0[:, 0]).then_inc(st_dve.mark(f"in{g}"), 1)
                dve.tensor_copy(wout2[g], state0[:, 1]).then_inc(st_dve.mark(f"out{g}"), 1)
            dve.wait_ge(st_dve.sem, st_dve.at(0, f"out{GROUPS - 1}"))
            hold(dve)

            with dve.Fori(0, ROUNDS) as n:
                def states(g):
                    act, pool, pe, mine = re_act[g], re_pool[g], re_pe[g], re_dve[g]
                    scores, d_in, queries = (bank[4 * g + b] for b in range(3))
                    cube = lambda t: t.rearrange("p (a l d) -> p a l d", l=16, d=16)
                    summands = lambda t: t.rearrange("p (x j) -> p x j", j=16)
                    rounds = t_mul[g].rearrange("p (j r a i) -> p r a i j", j=16, r=2, i=16)
                    both_terms = t_mul[g].rearrange("p (j a i) -> p a i j", j=16, i=16)
                    grid = lambda t: t.rearrange("p (a l) -> p a l", l=16)
                    over_a = lambda t: t.rearrange("p (a l) -> p l a", a=INNER)
                    by_ld = lambda w: grid(w).unsqueeze(2).broadcast_to([P, INNER, CHUNK, HD])
                    by_dl = lambda w, a: grid(w).unsqueeze(2).broadcast_to([P, a, HD, CHUNK])
                    tok_ld = lambda t: t.rearrange("p d l -> p l d").unsqueeze(1).broadcast_to([P, INNER, CHUNK, HD])
                    tok_dl = lambda t, a: t.unsqueeze(1).broadcast_to([P, a, HD, CHUNK])
                    per_l = lambda t: t.unsqueeze(1).broadcast_to([P, INNER, CHUNK])
                    per_a = lambda t, a: t.unsqueeze(2).broadcast_to([P, a, CHUNK])
                    for j in range(CPR):
                        c = n * CPR + j
                        buf = j // CPB
                        now = slice(j % CPB * CHUNK, (j % CPB + 1) * CHUNK)
                        k_now, v_now = k_blk[buf][g][:, :, now], v_blk[buf][g][:, :, now]
                        rate = lambda i, ahead: lr_fin[:, 2 * g + i, bass.ds((c + 1 - ahead) * CHUNK, 1)]

                        if j % CPB == 0:
                            dve.wait_ge(blk_loaded[buf][g], 48 * (n + 1))
                        dve.wait_ge(mine.sem, mine.before(c, "a1"))
                        dve.tensor_tensor(cube(t_mul[g][:, PROD:2 * PROD]), by_ld(win[g]), tok_ld(k_now), ALU.mult).then_inc(mine.mark("a0_mul"), 1)
                        dve.tensor_reduce(m_2[g], grid(s_2[g]), AX.X, ALU.max).then_inc(mine.mark("max2"), 1)
                        dve.wait_ge(mine.sem, mine.at(c, "a0_mul"))
                        dve.tensor_reduce(s_a[g], summands(t_mul[g][:, PROD:2 * PROD]), AX.X, ALU.add).then_inc(mine.mark("a0"), 1)
                        dve.wait_ge(mine.sem, mine.at(c, "max2"))
                        dve.tensor_tensor(grid(e_2[g]), grid(s_2[g]), per_a(m_2[g], INNER), ALU.subtract).then_inc(mine.mark("sub2"), 1)
                        dve.wait_ge(mine.sem, mine.at(c, "a0"))
                        dve.tensor_reduce(m_p[g], grid(s_a[g]), AX.X, ALU.max).then_inc(mine.mark("pmax"), 1)
                        dve.tensor_reduce(m_k[g], over_a(s_a[g]), AX.X, ALU.max).then_inc(mine.mark("kmax"), 1)
                        dve.wait_ge(mine.sem, mine.at(c, "pmax"))
                        dve.tensor_tensor(grid(e_p[g]), grid(s_a[g]), per_a(m_p[g], INNER), ALU.subtract).then_inc(mine.mark("psub"), 1)
                        dve.wait_ge(mine.sem, mine.at(c, "kmax"))
                        dve.tensor_tensor(grid(e_k[g]), grid(s_a[g]), per_l(m_k[g]), ALU.subtract).then_inc(mine.mark("ksub"), 1)
                        dve.wait_ge(act.sem, act.at(c, "e2"))
                        dve.tensor_reduce(z_2[g], grid(e_2[g]), AX.X, ALU.add).then_inc(mine.mark("sum2"), 1)
                        dve.wait_ge(act.sem, act.at(c, "ep"))
                        dve.tensor_reduce(z_p[g], grid(e_p[g]), AX.X, ALU.add).then_inc(mine.mark("psum"), 1)
                        dve.wait_ge(act.sem, act.at(c, "ek"))
                        dve.tensor_reduce(z_k[g], over_a(e_k[g]), AX.X, ALU.add).then_inc(mine.mark("ksum"), 1)
                        dve.wait_ge(mine.sem, mine.at(c, "sum2"))
                        dve.reciprocal(r_2[g], z_2[g]).then_inc(mine.mark("rec2"), 1)
                        dve.wait_ge(mine.sem, mine.at(c, "psum"))
                        dve.reciprocal(r_p[g], z_p[g]).then_inc(mine.mark("prec"), 1)
                        dve.wait_ge(mine.sem, mine.at(c, "ksum"))
                        dve.reciprocal(r_k[g], z_k[g]).then_inc(mine.mark("krec"), 1)
                        dve.wait_ge(mine.sem, mine.at(c, "rec2"))
                        dve.wait_ge(pool.sem, pool.before(c, "g2"))
                        dve.scalar_tensor_tensor(out=grid(p_2[g]), in0=grid(e_2[g]), scalar=rate(1, 1), in1=per_a(r_2[g], INNER), op0=ALU.mult, op1=ALU.mult).then_inc(mine.mark("p2"), 1)
                        dve.wait_ge(mine.sem, mine.at(c, "krec"))
                        dve.tensor_tensor(rl_k[g], r_k[g], lr_fin[:, 2 * g + 1, bass.ds((c + 1) * CHUNK, CHUNK)], ALU.mult).then_inc(mine.mark("klr"), 1)
                        dve.wait_ge(mine.sem, mine.at(c, "prec"))
                        dve.wait_ge(pool.sem, pool.before(c, "g1"))
                        dve.scalar_tensor_tensor(out=grid(p_out1[g]), in0=grid(e_p[g]), scalar=rate(1, 0), in1=per_a(r_p[g], INNER), op0=ALU.mult, op1=ALU.mult).then_inc(mine.mark("p1"), 1)
                        dve.wait_ge(mine.sem, mine.at(c, "klr"))
                        dve.wait_ge(pool.sem, pool.before(c, "kv"))
                        dve.tensor_tensor(grid(k_hat[g]), grid(e_k[g]), per_l(rl_k[g]), ALU.mult).then_inc(mine.mark("kh"), 1)
                        yield
                        dve.wait_ge(pool.sem, pool.at(c, "g2"))
                        dve.tensor_reduce(g_2[g], summands(t_g2[g]), AX.X, ALU.add).then_inc(mine.mark("g2s"), 1)
                        dve.wait_ge(mine.sem, mine.at(c, "g2s"))
                        dve.tensor_tensor(wout[g], wout2[g], g_2[g], ALU.add).then_inc(mine.mark("wout"), 1)
                        dve.wait_ge(pool.sem, pool.at(c, "g1"))
                        dve.tensor_reduce(g_1[g], summands(t_g1[g]), AX.X, ALU.add).then_inc(mine.mark("g1s"), 1)
                        by_l = grid(t_run[g])
                        dve.wait_ge(mine.sem, mine.at(c, "wout"))
                        dve.wait_ge(pool.sem, pool.at(c, "kv"))
                        dve.tensor_tensor(by_l[:, :, 0], by_l[:, :, 0], wout[g], ALU.add).then_inc(mine.mark("carry"), 1)
                        dve.wait_ge(mine.sem, mine.at(c, "carry"))
                        dve.tensor_tensor_scan(t_run[g], scan_keep, t_run[g], 0.0, ALU.mult, ALU.add).then_inc(mine.mark("run"), 1)
                        wout1 = by_l[:, :, CHUNK - 1]
                        dve.wait_ge(mine.sem, mine.at(c, "run"))
                        dve.tensor_tensor(wout2[g], wout1, g_1[g], ALU.add).then_inc(mine.mark("wout2"), 1)
                        dve.tensor_tensor(rounds[:, 0], wout1.rearrange("p (a d) -> p a d", a=INNER).unsqueeze(2).broadcast_to([P, INNER, CHUNK, HD]),
                                          tok_ld(v_now), ALU.mult).then_inc(mine.mark("b1_mul"), 1)
                        dve.wait_ge(mine.sem, mine.at(c, "wout2"))
                        dve.tensor_tensor(rounds[:, 1], by_ld(wout2[g]), tok_ld(v_now), ALU.mult).then_inc(mine.mark("b2_mul"), 1)
                        yield
                        dve.wait_ge(pe.sem, pe.at(c, "b"))
                        dve.tensor_reduce(m_b[g], grid(scores[:, 0:2 * ROWS]), AX.X, ALU.max).then_inc(mine.mark("bmax"), 1)
                        dve.wait_ge(mine.sem, mine.at(c, "bmax"))
                        dve.tensor_tensor(grid(e_b[g]), grid(scores[:, 0:2 * ROWS]), per_a(m_b[g], 2 * INNER), ALU.subtract).then_inc(mine.mark("bsub"), 1)
                        dve.wait_ge(act.sem, act.at(c, "eb"))
                        dve.tensor_reduce(z_b[g], grid(e_b[g]), AX.X, ALU.add).then_inc(mine.mark("bsum"), 1)
                        dve.wait_ge(mine.sem, mine.at(c, "bsum"))
                        dve.reciprocal(r_b[g], z_b[g]).then_inc(mine.mark("brec"), 1)
                        dve.wait_ge(mine.sem, mine.at(c, "brec"))
                        dve.scalar_tensor_tensor(out=grid(p_in[g]), in0=grid(e_b[g]), scalar=rate(0, 0), in1=per_a(r_b[g], 2 * INNER), op0=ALU.mult, op1=ALU.mult).then_inc(mine.mark("pin"), 1)
                        dve.wait_ge(mine.sem, mine.at(c, "pin"))
                        dve.tensor_tensor(both_terms, by_dl(p_in[g], 2 * INNER), tok_dl(k_now, 2 * INNER), ALU.mult).then_inc(mine.mark("d_mul"), 1)
                        dve.wait_ge(pe.sem, pe.at(c, "sq"))
                        dve.tensor_reduce(m_q[g], over_a(queries[:, 0:ROWS]), AX.X, ALU.max).then_inc(mine.mark("qmax"), 1)
                        dve.wait_ge(mine.sem, mine.at(c, "qmax"))
                        dve.tensor_tensor(grid(e_q[g]), grid(queries[:, 0:ROWS]), per_l(m_q[g]), ALU.subtract).then_inc(mine.mark("qsub"), 1)
                        yield
                        dve.wait_ge(act.sem, act.at(c, "eq"))
                        dve.tensor_reduce(z_q[g], over_a(e_q[g]), AX.X, ALU.add).then_inc(mine.mark("qsum"), 1)
                        dve.wait_ge(pe.sem, pe.at(c, "d"))
                        dve.tensor_tensor(win1[g], win[g], d_in[:, 0:ROWS], ALU.add).then_inc(mine.mark("win1"), 1)
                        dve.wait_ge(mine.sem, mine.at(c, "qsum"))
                        dve.reciprocal(r_q[g], z_q[g]).then_inc(mine.mark("qrec"), 1)
                        dve.wait_ge(mine.sem, mine.at(c, "win1"))
                        dve.tensor_tensor(cube(t_mul[g][:, 0:PROD]), by_ld(win1[g]), tok_ld(k_now), ALU.mult).then_inc(mine.mark("a1_mul"), 1)
                        dve.wait_ge(mine.sem, mine.at(c, "qrec"))
                        dve.wait_ge(pool.sem, pool.before(c, "o_mul"))
                        dve.tensor_tensor(grid(q_hat[g]), grid(e_q[g]), per_l(r_q[g]), ALU.mult).then_inc(mine.mark("qh"), 1)
                        dve.wait_ge(pool.sem, pool.at(c, "sq_mul"))
                        dve.tensor_tensor(win[g], win1[g], d_in[:, ROWS:2 * ROWS], ALU.add).then_inc(mine.mark("win"), 1)
                        dve.wait_ge(mine.sem, mine.at(c, "a1_mul"))
                        dve.tensor_reduce(s_2[g], summands(t_mul[g][:, 0:PROD]), AX.X, ALU.add).then_inc(mine.mark("a1"), 1)
                    yield

                staggered(states)

            recurrence_done(dve)
            for s in SLOTS:
                dve.memset(c_h[s][:, :, 0:1], 0.0).then_inc(c_ready, 1)
            dve.wait_ge(c_ready, len(SLOTS))

            def out_centre(pe_s, mine, n, s):
                for k in range(KT):
                    dve.wait_ge(pe_s.sem, pe_s.at(n, f"mean{s}{k}"))
                    dve.tensor_tensor(c_o[s][:, k], c_o[s][:, k], bank[3 + 4 * k][:], ALU.subtract).then_inc(mine.mark(f"oc{s}{k}"), 1)

            def out_var(pe_s, mine, n, s):
                for k in range(KT):
                    dve.wait_ge(pe_s.sem, pe_s.at(n, f"var{s}{k}"))
                    dve.tensor_copy(c_ostd[s][:, k], bank[3 + 4 * k][:]).then_inc(mine.mark(f"ov{s}{k}"), 1)

            def out_gated(act_s, mine, n, s):
                dve.wait_ge(act_s.sem, act_s.at(n, f"orstd{s}"))
                dve.scalar_tensor_tensor(out=c_oz[s], in0=c_o[s], scalar=lngb_sb[:, 0:1], in1=c_ostd[s], op0=ALU.mult, op1=ALU.mult).then_inc(mine.mark(f"on{s}"), 1)
                dve.wait_ge(mine.sem, mine.at(n, f"on{s}"))
                dve.scalar_tensor_tensor(out=c_oz[s], in0=c_oz[s], scalar=lngb_sb[:, 1:2], in1=c_gate[s], op0=ALU.add, op1=ALU.mult).then_inc(mine.mark(f"oz{s}"), 1)

            def pick(mine, s, b):
                dve.tensor_copy(c_pick[s][0:BATCH], ident[0:BATCH, bass.ds(b, 1)].broadcast_to([BATCH, P])).then_inc(mine.mark(f"pick{s}"), 1)

            for s in SLOTS:
                out_centre(first_pe, first_dve, 0, s)
            for s in SLOTS:
                out_var(first_pe, first_dve, 0, s)
            for s in SLOTS:
                out_gated(first_act, first_dve, 0, s)
            for s in SLOTS:
                pick(first_dve, s, s)
            with dve.Fori(0, BATCH // 2) as i:
                B = lambda s, j: bank[4 * s + j]

                def residual(stage, s, pe_step, banks):
                    if stage == 2:
                        dve.wait_ge(c_pool.sem, c_pool.at(i, f"x2{s}"))
                    for a in range(2):
                        dve.wait_ge(c_pe.sem, c_pe.at(i, f"{pe_step}{s}{a}"))
                        half = slice(2 * a, 2 * a + 2)
                        before = c_xin if stage == 1 else c_x
                        dve.tensor_tensor(c_x[s][:, half], before[s][:, half],
                                          B(s, banks[a])[:].rearrange("p (t d) -> p t d", t=2), ALU.add).then_inc(c_dve.mark(f"x{stage}{s}{a}"), 1)

                def statistics(stage, s):
                    for t in range(TT):
                        dve.wait_ge(c_dve.sem, c_dve.at(i, f"x{stage}{s}{t // 2}"))
                        dve.bn_stats(c_stat[s][:, t], c_x[s][:, t]).then_inc(c_dve.mark(f"st{stage}{s}{t}"), 1)
                    dve.wait_ge(c_dve.sem, c_dve.at(i, f"st{stage}{s}{TT - 1}"))
                    hold(dve)
                    for t in range(TT):
                        dve.bn_aggr(c_mv[s][:, t], c_stat[s][:, t]).then_inc(c_dve.mark(f"ag{stage}{s}{t}"), 1)

                def normalise(stage, s):
                    dve.wait_ge(c_act.sem, c_act.at(i, f"std{stage}{s}"))
                    dve.reciprocal(c_rstd[s], c_std[s]).then_inc(c_dve.mark(f"rec{stage}{s}"), 1)
                    dve.wait_ge(c_dve.sem, c_dve.at(i, f"rec{stage}{s}"))
                    for t in range(TT):
                        dve.tensor_scalar(c_xhat[s][:, t], c_x[s][:, t], c_mv[s][:, t, 0:1], c_rstd[s][:, t:t + 1],
                                          ALU.subtract, ALU.mult).then_inc(c_dve.mark(f"xh{stage}{s}{t}"), 1)

                def norm(stage, pe_step, banks):
                    residual(stage, 0, pe_step, banks)
                    statistics(stage, 0)
                    residual(stage, 1, pe_step, banks)
                    normalise(stage, 0)
                    statistics(stage, 1)
                    normalise(stage, 1)

                for s in SLOTS:
                    b = i * 2 + s
                    mods = modc[:, N_MOD // 2 * KT:, bass.ds(b, 1)].rearrange("p (a c) o -> p a (c o)", c=N_MOD // 2 * KT)
                    dve.wait_ge(c_act.sem, c_act.before(i, f"h3{s}{KT - 1}"))
                    dve.tensor_copy(c_modb[s], mods[:, :, 0:2 * KT]).then_inc(c_dve.mark(f"modb{s}"), 1)
                gate = lambda s, layer, j, p: B(s, layer)[0:p, j * DIM:(j + 1) * DIM]
                both = lambda s, layer, j: gate(s, layer, j, P).unsqueeze(1).broadcast_to([P, KT, DIM])
                for s in SLOTS:
                    dve.wait_ge(c_pe.sem, c_pe.at(i, f"gb{s}0"))
                    dve.tensor_tensor(c_wo[s], w_out_sb[:], both(s, 0, 0), ALU.mult).then_inc(c_dve.mark(f"wo{s}"), 1)
                for s in SLOTS:
                    dve.wait_ge(c_pe.sem, c_pe.at(i, f"gb{s}1"))
                    rows = slice(s * RANK, (s + 1) * RANK)
                    dve.tensor_tensor(c_v2[rows], v2_sb[rows], gate(s, 0, 1, P)[rows], ALU.mult).then_inc(c_dve.mark(f"v2{s}"), 1)
                    dve.tensor_tensor(c_b2[s], b2_sb[:], gate(s, 0, 1, P), ALU.mult).then_inc(c_dve.mark(f"b2{s}"), 1)
                    dve.tensor_tensor(c_wp[s], w_proj_sb[:], both(s, 1, 0), ALU.mult).then_inc(c_dve.mark(f"wp{s}"), 1)
                    dve.tensor_tensor(c_wv[s], w_rkv_sb[:, 2], both(s, 1, 1), ALU.mult).then_inc(c_dve.mark(f"wv{s}"), 1)
                for s in SLOTS:
                    dve.wait_ge(c_loaded[s], 16 * (i + 1))
                    hold(dve)
                    dve.wait_ge(out_stored[s], 32 * i)
                    hold(dve)
                norm(1, "wo", (2, 3))
                for s in SLOTS:
                    out_centre(c_pe, c_dve, i, s)
                for s in SLOTS:
                    out_var(c_pe, c_dve, i, s)
                for s in SLOTS:
                    rows = slice(s * RANK, (s + 1) * RANK)
                    dve.wait_ge(c_pe.sem, c_pe.at(i, f"u2{s}{FT - 1}"))
                    dve.tensor_copy(c_qr[rows], B(s, 0)[rows]).then_inc(c_dve.mark(f"qr{s}"), 1)
                norm(2, "v2", (1, 2))
                for s in SLOTS:
                    out_gated(c_act, c_dve, i, s)

                def segments(dst, src):
                    blocks = src.rearrange("p (f q) -> p f q", q=QF)
                    return ((dst[:, 2:FRAMES, 0:QF], blocks[:, 0:FRAMES - 2]),
                            (dst[:, 1:FRAMES, QF:2 * QF], blocks[:, 0:FRAMES - 1]),
                            (dst[:, :, 2 * QF:3 * QF], blocks),
                            (dst[:, :, 3 * QF:KEYS], src[:, 0:NGLOB].unsqueeze(1).broadcast_to([P, FRAMES, NGLOB])))

                for s in SLOTS:
                    dve.wait_ge(c_pe.sem, c_pe.at(i, f"vt{s}1"))
                    dve.tensor_copy(c_vt[s][:, 2:4], B(s, 2)[:].rearrange("p (t d) -> p t d", t=2)).then_inc(c_dve.mark(f"vt{s}1"), 1)
                for s in SLOTS:
                    dve.wait_ge(c_pe.sem, c_pe.at(i, f"q{s}1"))
                    for j in range(4):
                        dve.tensor_scalar(c_qb[s][:, 1, :, j * QF:(j + 1) * QF], B(s, 0)[:].rearrange("p (f q) -> p f q", q=QF),
                                          parity[:, j:j + 1], None, ALU.mult).then_inc(c_dve.mark(f"qb{s}1{j}"), 1)
                for s in SLOTS:
                    dve.wait_ge(c_pe.sem, c_pe.at(i, f"k{s}0"))
                    for g, (dst, src) in enumerate(segments(c_k[s][:, 0], B(s, 1)[:])):
                        dve.tensor_copy(dst, src).then_inc(c_dve.mark(f"ks{s}{g}"), 1)

                quads = lambda t: t.rearrange("p (t k) -> p t k", t=2)
                for t in range(len(ATT) + Y_LAG + 1):
                    if t < len(ATT):
                        f, s = ATT[t]
                        dve.wait_ge(c_pe.sem, c_pe.at(i, f"s{s}{f}"))
                        sc = psum[:, 4 * s:4 * s + 2, 0:KT * KEYS].rearrange("p t (k y) -> p t k y", k=KT)
                        if f > 0:
                            dve.wait_ge(c_act.sem, c_act.at(i, f"exp{s}{f - 1}u{QUADS - 1}"))
                        dve.tensor_reduce(quads(c_max[s]), sc, AX.X, ALU.max, negate=True).then_inc(c_dve.mark(f"max{s}{f}"), 1)
                    if 0 <= t - 1 < len(ATT):
                        f, s = ATT[t - 1]
                        dve.wait_ge(c_act.sem, c_act.at(i, f"exp{s}{f}u{QUADS - 1}"))
                        dve.tensor_reduce(c_sum[s], c_soft[s][:, f % 2], AX.X, ALU.add).then_inc(c_dve.mark(f"sum{s}{f}"), 1)
                        dve.wait_ge(c_dve.sem, c_dve.at(i, f"sum{s}{f}"))
                        if f > 0:
                            dve.wait_ge(c_pool.sem, c_pool.at(i, f"prob{s}{f - 1}"))
                        dve.reciprocal(c_rec[s], c_sum[s]).then_inc(c_dve.mark(f"arec{s}{f}"), 1)
                    if 0 <= t - Y_LAG < len(ATT) and ends_quarter(ATT[t - Y_LAG][0]):
                        f, s = ATT[t - Y_LAG]
                        quarter = f // QTR
                        if quarter == 0:
                            dve.wait_ge(v_framed[s], 16 * FRAMED * (i + 1))
                        dve.wait_ge(c_act.sem, c_act.at(i, f"ye{s}{quarter}"))
                        src = y_bank(s, quarter)[:].rearrange("p (f e q) -> p f e q", e=2, q=QF)[:, :, 1]
                        dve.scalar_tensor_tensor(out=c_y[s][:, quarter].rearrange("p k (f q) -> p (k f) q", q=QF), in0=src, scalar=parity[:, 5:6],
                                                 in1=c_yeven[s], op0=ALU.mult, op1=ALU.add).then_inc(c_dve.mark(f"y{s}{quarter}"), 1)
                norm(3, "wp", (0, 1))
                dve.wait_ge(c_act.sem, c_act.at(i, f"h30{KT - 1}"))
                dve.tensor_tensor(c_d[0], c_h[0][:, :, 1:TOK + 1], c_h[0][:, :, 0:TOK], ALU.subtract).then_inc(c_dve.mark("d0"), 1)
                for s in SLOTS:
                    if s == 0:
                        dve.wait_ge(c_dve.sem, c_dve.at(i, "d0"))
                    else:
                        dve.wait_ge(c_pool.sem, c_pool.at(i, "d1"))
                    for m, (name, dst) in enumerate((("xr", c_xr[s]), ("xk", c_xk[s]))):
                        for k in range(KT):
                            dve.scalar_tensor_tensor(out=dst[:, k], in0=c_d[s][:, k], scalar=mu_sb[:, m, k:k + 1],
                                                     in1=c_h[s][:, k, 0:TOK], op0=ALU.mult, op1=ALU.add).then_inc(c_dve.mark(f"{name}{s}{k}"), 1)
                for s in SLOTS:
                    pick(c_dve, s, i * 2 + s + AHEAD)
                for s in SLOTS:
                    for a in range(2):
                        dve.wait_ge(c_pe.sem, c_pe.at(i, f"vv{s}{a}"))
                        half = slice(2 * a, 2 * a + 2)
                        dve.tensor_tensor(c_rv[s][:, half], c_r[s][:, half], B(s, a)[:].rearrange("p (t d) -> p t d", t=2), ALU.mult).then_inc(c_dve.mark(f"rv{s}{a}"), 1)


def kernel(**inputs):
    import concourse.bacc as bacc
    from concourse.bass_utils import run_bass_kernel_spmd

    def a(name):
        return np.asarray(inputs[name])

    def turned(name):
        return np.ascontiguousarray(a(name).T)

    def row(name):
        return np.ascontiguousarray(a(name).reshape(1, -1))

    part = np.arange(P)
    ident = np.eye(P, dtype=np.float32)
    blocks = (part[:, None] // HD == part[None, :] // HD).astype(np.float32) / HD
    parity = np.zeros((P, 7), np.float32)
    for j in range(4):
        parity[:, j] = (part // HD % 4 == j) / np.sqrt(HD)
    parity[:, 4] = part // HD % 2 == 0
    parity[:, 5] = part // HD % 2 == 1
    parity[:, 6] = EPS
    q, key = part[:, None] % QF, np.arange(KEYS)[None, :]
    local = (key <= q + WINDOW) & (key > q) & (key < WINDOW + QF)
    glob = key >= WINDOW + QF
    seen = [local & (key >= WINDOW), (local & (key >= QF)) | ((key >= QF) & (key < QF + NGLOB)),
            local | (key < NGLOB), local | glob]
    mask = np.stack([np.tile(np.where(m, 0.0, MASKED), (1, KT)) for m in seen], axis=1).astype(mybir.dt.np(BF16))

    arrays = {
        "x": a("L0_attn_hidden_states"),
        "w_in": np.concatenate([turned(f"L0_attn_{n}") for n in ("Wq", "Wk", "Wv", "Wg", "Wlr")], axis=1),
        "taps": np.concatenate([a(f"L0_attn_{n}") for n in ("cq", "ck", "cv")], axis=1),
        "w_out": turned("L0_attn_Wo"),
        "ln_g": np.tile(a("L0_attn_ln_g"), P // HD).reshape(P, 1),
        "ln_b": np.tile(a("L0_attn_ln_b"), P // HD).reshape(P, 1),
        "w_in_init": a("L0_attn_W_in_init")[0],
        "w_out_init": a("L0_attn_W_out_init")[0],
        "u1": a("L0_ffn_U1"), "v1": a("L0_ffn_V1"), "b1": a("L0_ffn_b1").reshape(FT, P).T,
        "u2": a("L0_ffn_U2"), "v2": a("L0_ffn_V2"), "b2": row("L0_ffn_b2"),
        "cond": np.stack([turned("L0_c"), turned("L1_c")]),
        "wmod": np.stack([a("L0_wmod"), a("L1_wmod")]),
        "w_attn": turned("L1_attn_w_attn"), "w_proj": turned("L1_attn_w_proj"),
        "w_r": turned("L1_ffn_W_r"), "w_k": turned("L1_ffn_W_k"), "w_v": turned("L1_ffn_W_v"),
        "mu": np.stack([a("L1_ffn_mu_r").reshape(KT, P).T, a("L1_ffn_mu_k").reshape(KT, P).T], axis=1),
        "ident_c": ident, "blocks_c": blocks, "parity_c": parity, "mask_c": mask,
    }
    arrays = {n: np.ascontiguousarray(v) for n, v in arrays.items()}
    nc = bacc.Bacc("TRN2", target_bir_lowering=False, num_devices=1)
    args = [nc.dram_tensor(n, v.shape, mybir.dt.from_np(v.dtype), kind="ExternalInput").ap() for n, v in arrays.items()]
    args.append(nc.dram_tensor("out", (BATCH, TOK, DIM), F32, kind="ExternalOutput").ap())
    adaln_two_layers(nc, *args)
    r = run_bass_kernel_spmd(nc, [arrays], core_ids=[0])
    return r.results[0]["out"]
```
